# Optimizing a Trainium2 kernel written in Bass

```python
import numpy as np
import jax
import jax.numpy as jnp

def _softmax(x, axis=-1):
    return jax.nn.softmax(x, axis=axis)

def _gelu(x):
    return jax.nn.gelu(x, approximate=True)

def _silu(x):
    return jax.nn.silu(x)

def _sigmoid(x):
    return jax.nn.sigmoid(x)

def _layernorm(x, axis=-1, eps=1e-05):
    m = jnp.mean(x, axis=axis, keepdims=True)
    v = jnp.var(x, axis=axis, keepdims=True)
    return (x - m) / jnp.sqrt(v + eps)

def _scatter_add(tgt, idx, src, axis=0):
    return tgt.at[idx].add(src)

def _segment_sum(src, seg, n):
    return jax.ops.segment_sum(src, seg, n)
kernel_name = 'mk_recurrent_d2_jaxref_r8_66ee3c'

def setup_inputs(seed: int=0):
    np.random.seed(seed)
    _w = jnp.asarray

    def _L0_attn_setup():
        import math
        import jax, jax.numpy as jnp
        import numpy as np
        BATCH, SEQ, D_MODEL, D_STATE = (2, 256, 128, 16)
        PROJ = 2 * D_MODEL + 2 * D_MODEL * D_STATE
        key = jax.random.key(seed)
        kx, kw = jax.random.split(key)
        x = jax.random.normal(kx, (BATCH, SEQ, D_MODEL), dtype=jnp.float32)
        bound = math.sqrt(6.0 / (D_MODEL + PROJ))
        W = jax.random.uniform(kw, (PROJ, D_MODEL), jnp.float32, -bound, bound)
        b = jnp.zeros((PROJ,), jnp.float32)
        dl = jnp.arange(D_STATE, dtype=jnp.float32) / D_STATE
        A = jnp.broadcast_to(-jnp.exp(math.log(1000.0) * dl), (D_MODEL, D_STATE)).astype(jnp.float32)
        D = jnp.ones((D_MODEL,), jnp.float32)
        return {'x': x, 'W': W, 'b': b, 'A': A, 'D': D}
    _L0_attn_in = _L0_attn_setup()

    def _L0_ffn_setup():
        import jax, jax.numpy as jnp
        import numpy as np
        DIM = 128
        DEPTH = 2
        HEADS = 8
        DIM_HEAD = 64
        WINDOW = 64
        INNER = HEADS * DIM_HEAD
        HID = int(DIM * 4 * 2 / 3)
        B, N = (2, 1024)
        QK_SCALE = 8.0

        def shift_token(t):
            t1, t2 = jnp.split(t, 2, axis=-1)
            t2 = jnp.pad(t2, ((0, 0), (1, 0), (0, 0)))[:, :-1]
            return jnp.concatenate([t1, t2], axis=-1)

        def l2norm(t):
            return t / jnp.clip(jnp.linalg.norm(t, axis=-1, keepdims=True), 1e-12)

        def rotate_half(x):
            x1, x2 = jnp.split(x, 2, axis=-1)
            return jnp.concatenate([-x2, x1], axis=-1)

        def rotary_xpos(q, k):
            n = q.shape[-2]
            half_idx = jnp.arange(0, DIM_HEAD, 2, dtype=jnp.float32)
            inv_freq = 1.0 / 10000.0 ** (half_idx / DIM_HEAD)
            t = jnp.arange(n, dtype=jnp.float32)
            freqs = t[:, None] * inv_freq[None, :]
            freqs = jnp.concatenate([freqs, freqs], axis=-1)
            base = (half_idx + 0.4 * DIM_HEAD) / (1.4 * DIM_HEAD)
            power = (t - n // 2) / float(WINDOW // 2)
            scale = base[None, :] ** power[:, None]
            scale = jnp.concatenate([scale, scale], axis=-1)
            cos, sin = (jnp.cos(freqs), jnp.sin(freqs))
            q = q * cos * scale + rotate_half(q) * sin * scale
            k = k * cos / scale + rotate_half(k) * sin / scale
            return (q, k)

        def local_attention(q, k, v):
            b, h, n, d = q.shape
            w = n // WINDOW
            bq = q.reshape(b, h, w, WINDOW, d) * QK_SCALE
            bk = k.reshape(b, h, w, WINDOW, d)
            bv = v.reshape(b, h, w, WINDOW, d)

            def look_around(t):
                p = jnp.pad(t, ((0, 0), (0, 0), (1, 0), (0, 0), (0, 0)))
                return jnp.concatenate([p[:, :, :w], p[:, :, 1:]], axis=3)
            bk, bv = (look_around(bk), look_around(bv))
            bt = jnp.arange(n).reshape(w, WINDOW)
            btp = jnp.pad(bt, ((1, 0), (0, 0)), constant_values=-1)
            btk = jnp.concatenate([btp[:w], btp[1:]], axis=1)
            sim = jnp.einsum('bhwid,bhwjd->bhwij', bq, bk)
            i = bt[:, :, None]
            j = btk[:, None, :]
            mask = (i < j) | (i > j + WINDOW) | (j == -1)
            sim = jnp.where(mask, -jnp.finfo(sim.dtype).max, sim)
            attn = jax.nn.softmax(sim, axis=-1)
            out = jnp.einsum('bhwij,bhwjd->bhwid', attn, bv)
            return out.reshape(b, h, n, d)

        def _layer(x, wqkv, qs, ksc, wo, lg, lb, w1, b1, w2, b2):
            b, n, _ = x.shape
            h = shift_token(x)
            qkv = h @ wqkv
            q, k, v = jnp.split(qkv, 3, axis=-1)
            to_heads = lambda t: t.reshape(b, n, HEADS, DIM_HEAD).transpose(0, 2, 1, 3)
            q, k, v = (to_heads(q), to_heads(k), to_heads(v))
            q = l2norm(q) * qs
            k = l2norm(k) * ksc
            q, k = rotary_xpos(q, k)
            o = local_attention(q, k, v)
            o = o.transpose(0, 2, 1, 3).reshape(b, n, INNER)
            x = x + o @ wo
            h = shift_token(x)
            mu = h.mean(-1, keepdims=True)
            var = h.var(-1, keepdims=True)
            h = (h - mu) / jnp.sqrt(var + 1e-05) * lg + lb
            h = h @ w1 + b1
            a, g = jnp.split(h, 2, axis=-1)
            h = a * jax.nn.gelu(g, approximate=False)
            x = x + h @ w2 + b2
            return x
        key = jax.random.key(seed)
        ks = jax.random.split(key, 6)
        return {'x': jax.random.normal(ks[0], (B, N, DIM), jnp.float32), 'wqkv': jax.random.normal(ks[1], (DEPTH, DIM, 3 * INNER), jnp.float32) * 0.02, 'q_scale': jnp.ones((DEPTH, DIM_HEAD), jnp.float32), 'k_scale': jnp.ones((DEPTH, DIM_HEAD), jnp.float32), 'wo': jax.random.normal(ks[2], (DEPTH, INNER, DIM), jnp.float32) * 0.02, 'ln_g': jnp.ones((DEPTH, DIM), jnp.float32), 'ln_b': jnp.zeros((DEPTH, DIM), jnp.float32), 'w1': jax.random.normal(ks[3], (DEPTH, DIM, 2 * HID), jnp.float32) * 0.02, 'b1': jnp.zeros((DEPTH, 2 * HID), jnp.float32), 'w2': jax.random.normal(ks[4], (DEPTH, HID, DIM), jnp.float32) * 0.02, 'b2': jnp.zeros((DEPTH, DIM), jnp.float32)}
    _L0_ffn_in = _L0_ffn_setup()

    def _L1_attn_setup():
        import jax, jax.numpy as jnp
        import numpy as np
        B, S, D, DI = (2, 512, 128, 512)

        def _gelu(x):
            return jax.nn.gelu(x, approximate=False)

        def _ln(x, g, b, eps=1e-05):
            mu = jnp.mean(x, axis=-1, keepdims=True)
            var = jnp.mean((x - mu) ** 2, axis=-1, keepdims=True)
            return (x - mu) / jnp.sqrt(var + eps) * g + b

        def _mlp(x, w1, b1, w2, b2):
            return _gelu(x @ w1 + b1) @ w2 + b2
        key = jax.random.key(seed)
        ks = jax.random.split(key, 16)
        s = 0.02

        def W(k, shape):
            return jax.random.normal(k, shape, dtype=jnp.float32) * s
        return {'x': jax.random.normal(ks[0], (B, S, D), dtype=jnp.float32), 'ln_g': jnp.ones((D,), jnp.float32), 'ln_b': jnp.zeros((D,), jnp.float32), 'h1_w1': W(ks[1], (D, DI)), 'h1_b1': jnp.zeros((DI,), jnp.float32), 'h1_w2': W(ks[2], (DI, D)), 'h1_b2': jnp.zeros((D,), jnp.float32), 'h2_w1': W(ks[3], (D, DI)), 'h2_b1': jnp.zeros((DI,), jnp.float32), 'h2_w2': W(ks[4], (DI, D)), 'h2_b2': jnp.zeros((D,), jnp.float32), 'fm_w1': W(ks[5], (D, DI)), 'fm_b1': jnp.zeros((DI,), jnp.float32), 'fm_w2': W(ks[6], (DI, D)), 'fm_b2': jnp.zeros((D,), jnp.float32)}
    _L1_attn_in = _L1_attn_setup()

    def _L1_ffn_setup():
        import jax, jax.numpy as jnp
        import numpy as np
        S, B, H = (256, 1, 128)
        N_HEADS = 16
        HEAD_DIM = H // N_HEADS
        E, K, F = (8, 2, 256)
        EPS = 1e-05

        def layernorm(x, w, b):
            mu = jnp.mean(x, axis=-1, keepdims=True)
            var = jnp.mean(jnp.square(x - mu), axis=-1, keepdims=True)
            return (x - mu) * jax.lax.rsqrt(var + EPS) * w + b
        key = jax.random.key(seed)
        ks = jax.random.split(key, 8)
        std = 0.02
        return {'x': jax.random.normal(ks[0], (S, B, H), dtype=jnp.float32), 'ln1_w': jnp.ones((H,), jnp.float32), 'ln1_b': jnp.zeros((H,), jnp.float32), 'in_proj_w': jax.random.normal(ks[1], (3 * H, H), jnp.float32) * std, 'in_proj_b': jnp.zeros((3 * H,), jnp.float32), 'out_proj_w': jax.random.normal(ks[2], (H, H), jnp.float32) * std, 'out_proj_b': jnp.zeros((H,), jnp.float32), 'ln2_w': jnp.ones((H,), jnp.float32), 'ln2_b': jnp.zeros((H,), jnp.float32), 'router_w': jax.random.normal(ks[3], (E, H), jnp.float32) * std, 'w1': jax.random.normal(ks[4], (E, H, F), jnp.float32) * std, 'w2': jax.random.normal(ks[5], (E, F, H), jnp.float32) * std}
    _L1_ffn_in = _L1_ffn_setup()
    _d = {'L0_attn_x': _L0_attn_in['x'], 'L0_attn_W': _L0_attn_in['W'], 'L0_attn_b': _L0_attn_in['b'], 'L0_attn_A': _L0_attn_in['A'], 'L0_attn_D': _L0_attn_in['D'], 'L0_ffn_wqkv': _L0_ffn_in['wqkv'], 'L0_ffn_q_scale': _L0_ffn_in['q_scale'], 'L0_ffn_k_scale': _L0_ffn_in['k_scale'], 'L0_ffn_wo': _L0_ffn_in['wo'], 'L0_ffn_ln_g': _L0_ffn_in['ln_g'], 'L0_ffn_ln_b': _L0_ffn_in['ln_b'], 'L0_ffn_w1': _L0_ffn_in['w1'], 'L0_ffn_b1': _L0_ffn_in['b1'], 'L0_ffn_w2': _L0_ffn_in['w2'], 'L0_ffn_b2': _L0_ffn_in['b2'], 'L1_attn_ln_g': _L1_attn_in['ln_g'], 'L1_attn_ln_b': _L1_attn_in['ln_b'], 'L1_attn_h1_w1': _L1_attn_in['h1_w1'], 'L1_attn_h1_b1': _L1_attn_in['h1_b1'], 'L1_attn_h1_w2': _L1_attn_in['h1_w2'], 'L1_attn_h1_b2': _L1_attn_in['h1_b2'], 'L1_attn_h2_w1': _L1_attn_in['h2_w1'], 'L1_attn_h2_b1': _L1_attn_in['h2_b1'], 'L1_attn_h2_w2': _L1_attn_in['h2_w2'], 'L1_attn_h2_b2': _L1_attn_in['h2_b2'], 'L1_attn_fm_w1': _L1_attn_in['fm_w1'], 'L1_attn_fm_b1': _L1_attn_in['fm_b1'], 'L1_attn_fm_w2': _L1_attn_in['fm_w2'], 'L1_attn_fm_b2': _L1_attn_in['fm_b2'], 'L1_ffn_ln1_w': _L1_ffn_in['ln1_w'], 'L1_ffn_ln1_b': _L1_ffn_in['ln1_b'], 'L1_ffn_in_proj_w': _L1_ffn_in['in_proj_w'], 'L1_ffn_in_proj_b': _L1_ffn_in['in_proj_b'], 'L1_ffn_out_proj_w': _L1_ffn_in['out_proj_w'], 'L1_ffn_out_proj_b': _L1_ffn_in['out_proj_b'], 'L1_ffn_ln2_w': _L1_ffn_in['ln2_w'], 'L1_ffn_ln2_b': _L1_ffn_in['ln2_b'], 'L1_ffn_router_w': _L1_ffn_in['router_w'], 'L1_ffn_w1': _L1_ffn_in['w1'], 'L1_ffn_w2': _L1_ffn_in['w2']}
    _x0 = _d['L0_attn_x']
    _d['L0_attn_x'] = jax.random.normal(jax.random.fold_in(jax.random.key(seed), 1), (8, 512, 128), dtype=_x0.dtype)
    del _x0
    return _d

def reference(L0_attn_x, L0_attn_W, L0_attn_b, L0_attn_A, L0_attn_D, L0_ffn_wqkv, L0_ffn_q_scale, L0_ffn_k_scale, L0_ffn_wo, L0_ffn_ln_g, L0_ffn_ln_b, L0_ffn_w1, L0_ffn_b1, L0_ffn_w2, L0_ffn_b2, L1_attn_ln_g, L1_attn_ln_b, L1_attn_h1_w1, L1_attn_h1_b1, L1_attn_h1_w2, L1_attn_h1_b2, L1_attn_h2_w1, L1_attn_h2_b1, L1_attn_h2_w2, L1_attn_h2_b2, L1_attn_fm_w1, L1_attn_fm_b1, L1_attn_fm_w2, L1_attn_fm_b2, L1_ffn_ln1_w, L1_ffn_ln1_b, L1_ffn_in_proj_w, L1_ffn_in_proj_b, L1_ffn_out_proj_w, L1_ffn_out_proj_b, L1_ffn_ln2_w, L1_ffn_ln2_b, L1_ffn_router_w, L1_ffn_w1, L1_ffn_w2):

    def _L0_attn_ref(x, W, b, A, D):
        import math
        import jax, jax.numpy as jnp
        import numpy as np
        BATCH, SEQ, D_MODEL, D_STATE = (2, 256, 128, 16)
        PROJ = 2 * D_MODEL + 2 * D_MODEL * D_STATE
        bsz, seq, dm = x.shape
        ds = A.shape[1]
        xp = jnp.einsum('bsd,pd->bsp', x, W) + b
        u, delta, Bp, Cp = jnp.split(xp, [dm, 2 * dm, 2 * dm + dm * ds], axis=-1)
        delta = jax.nn.softplus(delta)
        Bm = Bp.reshape(bsz, seq, dm, ds)
        Cm = Cp.reshape(bsz, seq, dm, ds)
        Abar = jnp.exp(A * delta[..., None])

        def step(h, inp):
            Abar_t, B_t, C_t, u_t = inp
            h = Abar_t * h + B_t * u_t[..., None]
            y_t = jnp.sum(C_t * h, axis=-1)
            return (h, y_t)
        h0 = jnp.zeros((bsz, dm, ds), dtype=x.dtype)
        xs = (jnp.swapaxes(Abar, 0, 1), jnp.swapaxes(Bm, 0, 1), jnp.swapaxes(Cm, 0, 1), jnp.swapaxes(u, 0, 1))
        _, ys = jax.lax.scan(step, h0, xs)
        y = jnp.swapaxes(ys, 0, 1) + D * u
        return y

    def _L0_ffn_ref(x, wqkv, q_scale, k_scale, wo, ln_g, ln_b, w1, b1, w2, b2):
        import jax, jax.numpy as jnp
        import numpy as np
        DIM = 128
        DEPTH = 2
        HEADS = 8
        DIM_HEAD = 64
        WINDOW = 64
        INNER = HEADS * DIM_HEAD
        HID = int(DIM * 4 * 2 / 3)
        B, N = (2, 1024)
        QK_SCALE = 8.0

        def shift_token(t):
            t1, t2 = jnp.split(t, 2, axis=-1)
            t2 = jnp.pad(t2, ((0, 0), (1, 0), (0, 0)))[:, :-1]
            return jnp.concatenate([t1, t2], axis=-1)

        def l2norm(t):
            return t / jnp.clip(jnp.linalg.norm(t, axis=-1, keepdims=True), 1e-12)

        def rotate_half(x):
            x1, x2 = jnp.split(x, 2, axis=-1)
            return jnp.concatenate([-x2, x1], axis=-1)

        def rotary_xpos(q, k):
            n = q.shape[-2]
            half_idx = jnp.arange(0, DIM_HEAD, 2, dtype=jnp.float32)
            inv_freq = 1.0 / 10000.0 ** (half_idx / DIM_HEAD)
            t = jnp.arange(n, dtype=jnp.float32)
            freqs = t[:, None] * inv_freq[None, :]
            freqs = jnp.concatenate([freqs, freqs], axis=-1)
            base = (half_idx + 0.4 * DIM_HEAD) / (1.4 * DIM_HEAD)
            power = (t - n // 2) / float(WINDOW // 2)
            scale = base[None, :] ** power[:, None]
            scale = jnp.concatenate([scale, scale], axis=-1)
            cos, sin = (jnp.cos(freqs), jnp.sin(freqs))
            q = q * cos * scale + rotate_half(q) * sin * scale
            k = k * cos / scale + rotate_half(k) * sin / scale
            return (q, k)

        def local_attention(q, k, v):
            b, h, n, d = q.shape
            w = n // WINDOW
            bq = q.reshape(b, h, w, WINDOW, d) * QK_SCALE
            bk = k.reshape(b, h, w, WINDOW, d)
            bv = v.reshape(b, h, w, WINDOW, d)

            def look_around(t):
                p = jnp.pad(t, ((0, 0), (0, 0), (1, 0), (0, 0), (0, 0)))
                return jnp.concatenate([p[:, :, :w], p[:, :, 1:]], axis=3)
            bk, bv = (look_around(bk), look_around(bv))
            bt = jnp.arange(n).reshape(w, WINDOW)
            btp = jnp.pad(bt, ((1, 0), (0, 0)), constant_values=-1)
            btk = jnp.concatenate([btp[:w], btp[1:]], axis=1)
            sim = jnp.einsum('bhwid,bhwjd->bhwij', bq, bk)
            i = bt[:, :, None]
            j = btk[:, None, :]
            mask = (i < j) | (i > j + WINDOW) | (j == -1)
            sim = jnp.where(mask, -jnp.finfo(sim.dtype).max, sim)
            attn = jax.nn.softmax(sim, axis=-1)
            out = jnp.einsum('bhwij,bhwjd->bhwid', attn, bv)
            return out.reshape(b, h, n, d)

        def _layer(x, wqkv, qs, ksc, wo, lg, lb, w1, b1, w2, b2):
            b, n, _ = x.shape
            h = shift_token(x)
            qkv = h @ wqkv
            q, k, v = jnp.split(qkv, 3, axis=-1)
            to_heads = lambda t: t.reshape(b, n, HEADS, DIM_HEAD).transpose(0, 2, 1, 3)
            q, k, v = (to_heads(q), to_heads(k), to_heads(v))
            q = l2norm(q) * qs
            k = l2norm(k) * ksc
            q, k = rotary_xpos(q, k)
            o = local_attention(q, k, v)
            o = o.transpose(0, 2, 1, 3).reshape(b, n, INNER)
            x = x + o @ wo
            h = shift_token(x)
            mu = h.mean(-1, keepdims=True)
            var = h.var(-1, keepdims=True)
            h = (h - mu) / jnp.sqrt(var + 1e-05) * lg + lb
            h = h @ w1 + b1
            a, g = jnp.split(h, 2, axis=-1)
            h = a * jax.nn.gelu(g, approximate=False)
            x = x + h @ w2 + b2
            return x
        for l in range(DEPTH):
            x = _layer(x, wqkv[l], q_scale[l], k_scale[l], wo[l], ln_g[l], ln_b[l], w1[l], b1[l], w2[l], b2[l])
        return x

    def _L1_attn_ref(x, ln_g, ln_b, h1_w1, h1_b1, h1_w2, h1_b2, h2_w1, h2_b1, h2_w2, h2_b2, fm_w1, fm_b1, fm_w2, fm_b2):
        import jax, jax.numpy as jnp
        import numpy as np
        B, S, D, DI = (2, 512, 128, 512)

        def _gelu(x):
            return jax.nn.gelu(x, approximate=False)

        def _ln(x, g, b, eps=1e-05):
            mu = jnp.mean(x, axis=-1, keepdims=True)
            var = jnp.mean((x - mu) ** 2, axis=-1, keepdims=True)
            return (x - mu) / jnp.sqrt(var + eps) * g + b

        def _mlp(x, w1, b1, w2, b2):
            return _gelu(x @ w1 + b1) @ w2 + b2
        n = _ln(x, ln_g, ln_b)
        W1 = _mlp(n, h1_w1, h1_b1, h1_w2, h1_b2)
        W2 = _mlp(n, h2_w1, h2_b1, h2_w2, h2_b2)
        W3 = jnp.einsum('bzn,bsn->bzs', W1, W2)
        W3 = jnp.tril(W3)
        t = jnp.einsum('bzs,bsm->bzm', W3, n)
        t = _ln(_gelu(t), ln_g, ln_b)
        x1 = x + t
        out = x + _mlp(_ln(x1, ln_g, ln_b), fm_w1, fm_b1, fm_w2, fm_b2)
        return out

    def _L1_ffn_ref(x, ln1_w, ln1_b, in_proj_w, in_proj_b, out_proj_w, out_proj_b, ln2_w, ln2_b, router_w, w1, w2):
        import jax, jax.numpy as jnp
        import numpy as np
        S, B, H = (256, 1, 128)
        N_HEADS = 16
        HEAD_DIM = H // N_HEADS
        E, K, F = (8, 2, 256)
        EPS = 1e-05

        def layernorm(x, w, b):
            mu = jnp.mean(x, axis=-1, keepdims=True)
            var = jnp.mean(jnp.square(x - mu), axis=-1, keepdims=True)
            return (x - mu) * jax.lax.rsqrt(var + EPS) * w + b
        s, b, h = x.shape
        hn = layernorm(x, ln1_w, ln1_b)
        qkv = hn @ in_proj_w.T + in_proj_b
        q, k, v = jnp.split(qkv, 3, axis=-1)
        q = q.reshape(s, b, N_HEADS, HEAD_DIM)
        k = k.reshape(s, b, N_HEADS, HEAD_DIM)
        v = v.reshape(s, b, N_HEADS, HEAD_DIM)
        scores = jnp.einsum('sbnd,tbnd->bnst', q, k) / np.sqrt(HEAD_DIM)
        causal = jnp.tril(jnp.ones((s, s), bool))
        scores = jnp.where(causal[None, None], scores, -jnp.inf)
        probs = jax.nn.softmax(scores, axis=-1)
        attn = jnp.einsum('bnst,tbnd->sbnd', probs, v).reshape(s, b, h)
        attn = attn @ out_proj_w.T + out_proj_b
        x1 = x + attn
        hn2 = layernorm(x1, ln2_w, ln2_b).reshape(s * b, h)
        logits = hn2 @ router_w.T
        rp = jax.nn.softmax(logits, axis=-1)
        topw, topi = jax.lax.top_k(rp, K)
        gates = jnp.sum(jax.nn.one_hot(topi, E, dtype=hn2.dtype) * topw[..., None], axis=1)
        hmid = jax.nn.gelu(jnp.einsum('th,ehf->tef', hn2, w1), approximate=False)
        y = jnp.einsum('tef,efh->th', hmid * gates[:, :, None], w2)
        return x1 + y.reshape(s, b, h)
    x = L0_attn_x
    xn = _layernorm(x, axis=-1)
    s = _L0_attn_ref(xn, L0_attn_W, L0_attn_b, L0_attn_A, L0_attn_D)
    g = _silu(_L0_ffn_ref(xn, L0_ffn_wqkv, L0_ffn_q_scale, L0_ffn_k_scale, L0_ffn_wo, L0_ffn_ln_g, L0_ffn_ln_b, L0_ffn_w1, L0_ffn_b1, L0_ffn_w2, L0_ffn_b2))
    x = x + s * g
    xn = _layernorm(x, axis=-1)
    s = _L1_attn_ref(xn, L1_attn_ln_g, L1_attn_ln_b, L1_attn_h1_w1, L1_attn_h1_b1, L1_attn_h1_w2, L1_attn_h1_b2, L1_attn_h2_w1, L1_attn_h2_b1, L1_attn_h2_w2, L1_attn_h2_b2, L1_attn_fm_w1, L1_attn_fm_b1, L1_attn_fm_w2, L1_attn_fm_b2)
    g = _silu(_L1_ffn_ref(xn, L1_ffn_ln1_w, L1_ffn_ln1_b, L1_ffn_in_proj_w, L1_ffn_in_proj_b, L1_ffn_out_proj_w, L1_ffn_out_proj_b, L1_ffn_ln2_w, L1_ffn_ln2_b, L1_ffn_router_w, L1_ffn_w1, L1_ffn_w2))
    x = x + s * g
    return x

_drawn_inputs = setup_inputs


def setup_inputs(seed=0):
    import zlib

    import numpy as np

    out = dict(_drawn_inputs(seed))
    spreads = {'L0_attn_b': (0.0, 0.1),
     'L0_attn_D': (1.0, 0.2),
     'L0_ffn_q_scale': (1.0, 0.6),
     'L0_ffn_k_scale': (1.0, 0.6),
     'L0_ffn_ln_g': (1.0, 0.6),
     'L0_ffn_ln_b': (0.0, 0.8),
     'L0_ffn_b1': (0.0, 0.8),
     'L0_ffn_b2': (0.0, 0.491),
     'L1_attn_ln_g': (1.0, 0.6),
     'L1_attn_ln_b': (0.0, 0.618),
     'L1_attn_h1_b1': (0.0, 0.8),
     'L1_attn_h1_b2': (0.0, 1.064),
     'L1_attn_h2_b1': (0.0, 0.8),
     'L1_attn_h2_b2': (0.0, 0.487),
     'L1_attn_fm_b1': (0.0, 0.8),
     'L1_attn_fm_b2': (0.0, 0.439),
     'L1_ffn_ln1_w': (1.0, 0.6),
     'L1_ffn_ln1_b': (0.0, 0.8),
     'L1_ffn_in_proj_b': (0.0, 0.8),
     'L1_ffn_out_proj_b': (0.0, 0.1),
     'L1_ffn_ln2_w': (1.0, 0.6),
     'L1_ffn_ln2_b': (0.0, 0.8)}
    factors = {'L0_attn_A': 130.576,
     'L0_ffn_wqkv': 6.539,
     'L0_ffn_wo': 6.358,
     'L0_ffn_w1': 8.0,
     'L0_ffn_w2': 8.0,
     'L1_attn_h1_w1': 8.0,
     'L1_attn_h1_w2': 8.0,
     'L1_attn_h2_w1': 8.0,
     'L1_attn_h2_w2': 6.232,
     'L1_attn_fm_w1': 3.076,
     'L1_attn_fm_w2': 2.732,
     'L1_ffn_in_proj_w': 4.902,
     'L1_ffn_out_proj_w': 3.756,
     'L1_ffn_router_w': 8.0,
     'L1_ffn_w1': 8.0,
     'L1_ffn_w2': 8.0}
    for name, (base, spread) in spreads.items():
        noise = np.random.default_rng([zlib.crc32(name.encode()), seed]).standard_normal(out[name].shape)
        drawn = base * np.exp(spread * noise) if base else spread * noise
        out[name] = jnp.asarray(drawn.astype(out[name].dtype))
    for name, factor in factors.items():
        out[name] = (out[name] * factor).astype(out[name].dtype)
    return out
```

```python
from contextlib import ExitStack

import concourse.bass as bass
from concourse import mybir

F32 = mybir.dt.float32
BF16 = mybir.dt.bfloat16
ALU = mybir.AluOpType
ACT = mybir.ActivationFunctionType
AX = mybir.AxisListType

P = 128
NB, SEQ = 8, 512
MT = SEQ // P
LAYERS = 2
NS = 16
NSH = NS // LAYERS
HEADS, HD, WIN = 8, 64, 64
PAIRS = HEADS // 2
KEYS = 2 * WIN + WIN
HID = 341
FT = 3
DI = 512
KT = DI // P
EXP, FF = 8, 256
EPS = 1e-5
MASKED = -1e30
TOK = NB * SEQ
SCRATCH = 24000

R_BU, R_BD, R_D = 0, 1, 2
R_LAYER = 3
L_COLS = 2 * FT + 3
R_G, R_B = R_LAYER + LAYERS * L_COLS, R_LAYER + LAYERS * L_COLS + 1
R_H1B1, R_H1B2 = R_B + 1, R_B + 1 + KT
R_H2B1, R_H2B2 = R_H1B2 + 1, R_H1B2 + 1 + KT
R_FMB1 = R_H2B2 + 1
R_N1W, R_N1B, R_N2W, R_N2B = (R_FMB1 + KT + i for i in range(4))
N_ROWS = R_N2B + 1


class Count:

    def __init__(self, sem, per, ahead=False, base=0):
        self.sem, self.per, self.ahead, self.base = sem, per, int(ahead), base

    def at(self, turn, n):
        return (turn + self.ahead) * self.per + n + self.base

    def again(self, turns, per, ahead=False):
        return Count(self.sem, per, ahead, self.at(turns, 0))


def build(nc, I, out):
    with ExitStack() as ctx:
        def sb(name, shape, dt=F32):
            return ctx.enter_context(nc.sbuf_tensor(name, shape, dt))

        def sem(name):
            return ctx.enter_context(nc.semaphore(name))

        def count(name, per, ahead=False):
            return Count(sem(name), per, ahead)

        big = sb("big", [P, 6 * TOK])
        xt0 = big[:, 0:TOK]
        state = big[:, TOK:2 * TOK]
        u_all = big[:, 2 * TOK:3 * TOK]
        delta = big[:, 3 * TOK:4 * TOK]
        y_all = big[:, 4 * TOK:5 * TOK]
        x_tok = y_all
        work = big[:, 5 * TOK:6 * TOK]
        ident = sb("ident", [P, P])
        identb = sb("identb", [P, P], BF16)
        maskb = sb("maskb", [P, 2, KEYS], BF16)
        rows = sb("rows", [N_ROWS, P])
        cols = sb("cols", [P, N_ROWS])
        rot_raw = sb("rot_raw", [P, 4, MT, HD])
        abc_all = sb("abc_all", [P, 3, NS])
        upper = sb("upper", [P, P])
        before = sb("before", [P, EXP, EXP])
        pow_half = sb("pow_half", [P, NB * MT])

        scratch = sb("scratch", [P, SCRATCH])

        class Cut:
            def __init__(self):
                self.at = 0

            def __call__(self, *shape):
                n = 1
                for s in shape:
                    n *= s
                a = scratch[:, self.at:self.at + n]
                self.at += n
                assert self.at <= SCRATCH, self.at
                if len(shape) == 1:
                    return a
                names = " ".join(f"d{i}" for i in range(len(shape)))
                return a.rearrange(f"p ({names}) -> p {names}", **{f"d{i}": s for i, s in enumerate(shape)})

        bank = [ctx.enter_context(nc.psum_tensor(f"bank{i}", [P, 512], F32)) for i in range(8)]

        cut = Cut()
        wud_raw = cut(2, P)
        wud = cut(2, P)
        x_mv = cut(NB * MT, 2)
        x_stats = cut(2, 6)
        x_var = cut(NB * MT)
        x_rstd = cut(NB * MT)
        xn = cut(2, MT, P)
        cut = Cut()
        wbc_raw = cut(2, NSH, P)
        wbc = cut(2, NSH, P)
        abc = cut(3, NSH)
        lcol = cut(L_COLS)
        wqkv = cut(3, HEADS * HD)
        wo = cut(MT, P)
        w1 = cut(2, FT * P)
        w1s = cut(2, FT * P)
        w2 = cut(FT, P)
        b1s = cut(2 * FT)
        qk_scale = cut(2, HD)
        rot = cut(4, MT, HD)
        layer_end = cut.at
        hpad = cut(WIN + SEQ)
        squares = cut(2, HEADS * HD)
        sumsq = cut(2, 2 * HEADS)
        rnorm = cut(2, 2 * HEADS)
        sumsq_c = cut(2 * HEADS)
        k_n = cut(HEADS * HD)
        rot_q = cut(2, HEADS * HD)
        rot_k = cut(2, HEADS * HD)
        qT = cut(PAIRS, P)
        kT = cut(PAIRS, WIN + SEQ)
        vals = cut(MT + 1, 2, PAIRS, HD)
        edge = cut(MT, PAIRS, 2, HD)
        probs = cut(PAIRS, 2 * KEYS)
        probsT = cut(2, 2 * KEYS)
        wcut = [0]

        def wk(*shape):
            n = 1
            for s in shape:
                n *= s
            a = work[:, wcut[0]:wcut[0] + n]
            wcut[0] += n
            assert wcut[0] <= TOK
            if len(shape) == 1:
                return a
            names = " ".join(f"d{i}" for i in range(len(shape)))
            return a.rearrange(f"p ({names}) -> p {names}", **{f"d{i}": s for i, s in enumerate(shape)})

        mx = wk(HEADS)
        negmax = wk(HEADS)
        rowsum = wk(HEADS)
        rinv = wk(HEADS)
        o_tok = wk(HEADS * HD)
        oT = sb("oT", [P, MT, SEQ])
        abar = wk(2, SEQ)
        bu = wk(SEQ)
        hs = wk(SEQ)
        ch = wk(2, SEQ)
        cut.at = layer_end
        f_stats = cut(MT, 6)
        f_mv = cut(2, MT, 2)
        f_var = cut(MT)
        f_rstd = cut(2, MT)
        f_h = cut(2, SEQ)
        f_hn = cut(MT, P)
        f_hnT = cut(2, SEQ)
        f_gelu = cut(2, SEQ)
        f_act = cut(FT, SEQ)

        x1 = state
        xn1 = xt0
        qkv = big[:, 2 * TOK:5 * TOK].rearrange("p (m s c) -> p m s c", m=MT, s=NB)
        s_out = work
        cut = Cut()
        w_up = cut(3, DI)
        w_dn = cut(3, KT, P)
        inp_raw = cut(3, P)
        inpT = cut(3 * P)
        outp_raw = cut(P)
        outpT = cut(P)
        rout_raw = cut(P)
        routT = cut(EXP)
        m_up = cut(EXP, FF)
        m_dn = cut(EXP, 2, P)
        up_bias = cut(3 * KT + 2 * EXP)
        g_row, b_row, fm_b2_row, out_b_row = (cut(P) for _ in range(4))
        in_b_row = cut(3 * P)
        rout_b_row = cut(EXP)
        n1b_wide, n2b_wide = cut(P), cut(P)
        second_end = cut.at
        sg = cut(SEQ)
        l_stats = cut(MT, 6)
        l_mv = cut(MT, 2)
        l_var = cut(MT)
        l_rstd = cut(MT)
        z_tok = cut(MT, P)
        n_tok = cut(MT, P)
        n_scaled = cut(MT, P)
        zT = cut(SEQ)
        hid = cut(2, KT, SEQ)
        wT = cut(2, SEQ)
        w3 = cut(MT, SEQ)
        t_gelu = cut(MT, P)
        t_norm = cut(MT, P)
        t_gain = cut(MT, P)
        xn_b = cut(MT, P)
        xn_f = cut(MT, P)
        x_mid = cut(MT, P)
        z2 = cut(MT, P)
        z2T = cut(SEQ)
        cut.at = second_end
        prod = cut(NB * (NB + 1) // 2 * P)
        sc = cut(NB, NB, 16)
        pr = cut(NB, NB, 16)
        smax = cut(NB, 16)
        ssum = cut(NB, 16)
        sinv = cut(NB, 16)
        att = cut(NB, P)
        cut.at = second_end
        e_att = cut(MT, P)
        e_attT = cut(SEQ)
        e_in = cut(MT, P)
        e_acc = cut(MT, P)
        e_stats = cut(MT, 6)
        e_mv = cut(MT, 2)
        e_var = cut(MT)
        e_rstd = cut(MT)
        e_z = cut(MT, P)
        e_zT = cut(SEQ)
        lg = cut(MT, EXP)
        lmax = cut(MT)
        lsum = cut(MT)
        linv = cut(MT)
        pexp = cut(MT, EXP)
        prob = cut(MT, EXP)
        above = cut(MT, EXP, EXP)
        equal = cut(MT, EXP, EXP)
        rank = cut(MT, EXP)
        gates = cut(MT, EXP)
        e_hid = cut(2, 2, SEQ)
        cut.at = second_end
        fin = cut(2, NB, P)
        fo = cut(2, NB, P)

        s_x, s_rows, s_wud, s_tab, s_zero = (sem(n) for n in ("x_loaded", "rows_loaded", "wud_loaded", "tables_loaded", "rows_zeroed"))
        s_memset, s_const = sem("pool_memset"), sem("constants_made")
        s_cols_t, s_cols, s_wud_t, s_wud_c = sem("cols_turned"), sem("cols_copied"), sem("wud_turned"), sem("wud_copied")
        s_xstat, s_xvar, s_xrstd = sem("x_stats_done"), sem("x_var_done"), sem("x_rstd_done")
        met = {e: sem(f"{e}_met") for e in ("pe", "act", "dve", "pool", "sp")}

        def meet(eng, name, nth):
            eng.drain().then_inc(met[name], 1)
            for other in met:
                if other != name:
                    eng.wait_ge(met[other], nth)
            eng.sem_inc(passed, 1)

        passed = sem("waits_passed")

        def wait_alone(eng, semaphore, value):
            eng.wait_ge(semaphore, value)
            eng.sem_inc(passed, 1)

        c_xn = count("xn_ready", 1)
        c_xT_t = count("xT_turned", 1, True)
        c_xT = count("xT_copied", 1, True)
        c_ups = count("u_psum", 1)
        c_u = count("u_done", 1, True)
        c_dps = count("delta_psum", 1)
        c_dabs = count("delta_abs", 1)
        c_drelu = count("delta_relu", 1, True)
        c_st0 = count("state_copied", 1)
        c_dln = count("delta_ln", 1)
        s_dlt, s_y0, s_kz = sem("delta_done"), sem("y_started"), sem("pads_zeroed")

        s_lw = sem("layer_weights_loaded")
        NLW = 7
        p_wt = count("wbc_turned", 4, True)
        p_wc = count("wbc_copied", 4, True)
        p_lc = count("layer_columns", 2)
        p_rot = count("rot_scaled", 6)
        p_w1s = count("w1_scaled", 1)
        p_b1p = count("b1_product", 1)
        p_b1s = count("b1_scaled", 1)

        TU, SU = MT, NSH
        a_h = count("h_ready", 1)
        a_proj = count("proj_filled", TU, True)
        a_sq = count("squares_done", TU, True)
        a_ss = count("sumsq_done", TU, True)
        a_ssc = count("sumsq_clipped", TU)
        a_rn = count("rnorm_done", TU)
        a_kn = count("k_normed", TU)
        a_rq = count("q_rotated", TU)
        a_rk = count("k_rotated", TU, True)
        a_qkt = count("qkT_filled", TU, True)
        a_qke = count("qkT_copied", TU, True)
        a_edge = count("edge_values_copied", 1)
        a_sim = count("sim_filled", 2 * TU)
        a_max = count("max_done", 2 * TU)
        a_neg = count("negmax_done", 2 * TU)
        a_exp = count("exp_done", 2 * TU, True)
        RING = MT + 1 + TU * PAIRS + TU
        a_bf = count("turn_bank_filled", RING)
        a_be = count("turn_bank_emptied", RING, True)
        a_of = count("o_bank_filled", TU + 1)
        a_oe = count("o_bank_emptied", TU + 1, True)
        a_ri = count("rinv_done", TU)
        c_bps = count("b_filled", SU)
        c_cps = count("c_filled", SU)
        c_ab = count("abar_done", SU)
        c_bu = count("bu_done", SU, True)
        c_sc = count("scan_done", SU, True)
        c_ch = count("ch_done", SU, True)
        c_ya = count("y_added", SU, True)

        f_hc = count("f_h_ready", 1, True)
        f_zero = count("f_h_padded", 1)
        f_tf = count("f_h_turned", 1, True)
        f_st = count("aggr_done", 1, True)
        f_st2 = count("stats_done", 1)
        f_vr = count("var_done", 1)
        f_rs = count("rstd_done", 1)
        f_nm = count("f_normed", 1)
        f_nt = count("norm_turned", 1, True)
        f_ne = count("norm_turned_copied", 1, True)
        f_up = count("up_filled", FT)
        f_ge = count("gelu_done", FT, True)
        f_ac = count("f_act_done", FT, True)
        f_dn = count("f_down_filled", 1)
        f_ad = count("f_added", 1, True)

        x_view = I["L0_attn_x"].rearrange("b (m p) d -> p b m d", p=P)

        s_xr = sem("x_reloaded")
        s_w2nd = sem("second_weights_loaded")
        s_silu = sem("gate_silu_done")
        q_t, q_tc, q_wide, q_prod, q_pre, q_row = (sem(n) for n in ("projections_turned", "projections_copied", "norm_bias_widened", "bias_products", "biases_added", "weights_scaled"))
        l_sg = count("sg_ready", 1)
        l_sgt = count("sg_turned", 1, True)
        l_x1 = count("x1_done", 1, True)
        x_bn, x_ag, x_vr, x_rs = (c.again(LAYERS * NB, 1) for c in (f_st2, f_st, f_vr, f_rs))
        l_bn = x_bn.again(NB, 3)
        l_ag = x_ag.again(NB, 3)
        l_vr = x_vr.again(NB, 3)
        l_rs = x_rs.again(NB, 3)
        l_xn = count("xn1_done", 1)
        l_z = count("z_done", 1)
        l_zt = f_nt.again(LAYERS * NB, 1, True)
        l_zc = f_ne.again(LAYERS * NB, 1)
        l_ns = count("n_scaled", 1)
        l_n = count("n_done", 1)
        l_xb = count("xn_b_done", 1)
        l_xf = count("xn_f_done", 1)
        l_rf = count("two_bank_filled", 2 * MT)
        l_re = count("two_bank_emptied", 2 * MT, True)
        l_uf = f_up.again(LAYERS * NB, 3 * KT)
        l_ue = f_ge.again(LAYERS * NB, 3 * KT, True)
        l_wf = count("w_filled", 2)
        l_we = count("w_copied", 2, True)
        l_tf = count("t_filled", 1)
        l_tg = count("t_gelu_done", 1, True)
        l_tn = count("t_normed", 1)
        l_ta = count("t_gained", 1)
        l_xm = count("x_mid_done", 1)
        l_z2 = count("z2_done", 1)
        l_z2t = count("z2_turned", 1)
        l_z2c = count("z2T_copied", 1, True)
        l_ff = count("fm_filled", 1, True)
        l_so = count("s_out_done", 1, True)
        h_pd = count("h_products", NB)
        h_sc = count("h_scores", 1)
        h_mx = count("h_max", 1)
        h_sb = count("h_sub", 1)
        h_ex = count("h_exp", 1)
        h_sm = count("h_sum", 1)
        h_iv = count("h_inv", 1)
        h_pv = count("h_weighted", NB)
        h_at = count("h_att", 1)
        h_dn = count("h_done", 1)
        s_pads = sem("score_pads_set")
        e_ld = count("e_att_staged", 1)
        e_t1 = count("e_att_turned", 1, True)
        e_c1 = count("e_attT_copied", 1)
        e_ib = count("e_in_done", 1)
        e_pf = count("e_proj_filled", 1)
        e_x1 = count("e_x_done", 1)
        e_bn = l_bn.again(NB, 1)
        e_ag = l_ag.again(NB, 1)
        e_vr = l_vr.again(NB, 1)
        e_rs = l_rs.again(NB, 1)
        e_zd = l_z.again(NB, 1)
        e_t2 = l_zt.again(NB, 1)
        e_c2 = l_zc.again(NB, 1, True)
        e_rf = count("e_router_filled", 1)
        e_lg = count("e_logits", 2)
        e_sh = count("e_shifted", 1)
        e_ex = count("e_exp", 1)
        e_sm = count("e_sum", 2)
        e_pr = count("e_prob", 1)
        e_cm = count("e_compared", 4)
        e_rk = count("e_ranked", 1)
        e_gt = count("e_gates", 1)
        e_uf = l_uf.again(NB, 2 * EXP)
        e_ue = l_ue.again(NB, 2 * EXP, True)
        e_yf = count("e_y_filled", EXP, True)
        e_ya = count("e_y_added", EXP, True)
        e_st = count("e_stored", 1, True)
        z_si = count("z_silu_done", 1)
        z_pr = count("z_product_done", 1, True)
        z_fo = count("z_final_done", 1)
        z_dm = [sem("z_stored_even"), sem("z_stored_odd")]

        row_list = [(R_BU, I["L0_attn_b"][0:2 * P]), (R_D, I["L0_attn_D"])]
        for l in range(LAYERS):
            r = R_LAYER + l * L_COLS
            row_list += [(r, I["L0_ffn_b1"][l, 0:HID]), (r + FT, I["L0_ffn_b1"][l, HID:2 * HID]), (r + 2 * FT, I["L0_ffn_b2"][l]),
                         (r + 2 * FT + 1, I["L0_ffn_ln_g"][l]), (r + 2 * FT + 2, I["L0_ffn_ln_b"][l])]
        row_list += [(r, I["L1_" + name]) for r, name in (
            (R_G, "attn_ln_g"), (R_B, "attn_ln_b"), (R_H1B1, "attn_h1_b1"), (R_H1B2, "attn_h1_b2"), (R_H2B1, "attn_h2_b1"),
            (R_H2B2, "attn_h2_b2"), (R_FMB1, "attn_fm_b1"), (R_N1W, "ffn_ln1_w"), (R_N1B, "ffn_ln1_b"), (R_N2W, "ffn_ln2_w"),
            (R_N2B, "ffn_ln2_b"))]
        n_row_dmas = sum((ap.shape[0] >= P) + (ap.shape[0] % P > 0) for _, ap in row_list)
        oT_fill = [MT + 1 + 2 + (PAIRS + 1) * m + 3 for m in range(MT)]

        def oT_fill_check(m, n):
            assert oT_fill[m] == n, (m, n)

        second_list = [(w_up[:, k], I[f"L1_attn_{n}_w1"]) for k, n in enumerate(("h1", "h2", "fm"))]
        second_list += [(w_dn[:, k], I[f"L1_attn_{n}_w2"].rearrange("(t p) n -> p t n", p=P)) for k, n in enumerate(("h1", "h2", "fm"))]
        second_list += [
            (inp_raw, I["L1_ffn_in_proj_w"].rearrange("(t p) k -> p t k", p=P)), (outp_raw, I["L1_ffn_out_proj_w"]),
            (rout_raw[0:EXP], I["L1_ffn_router_w"]), (m_up, I["L1_ffn_w1"].rearrange("e p f -> p e f")),
            (m_dn, I["L1_ffn_w2"].rearrange("e (f p) n -> p e f n", p=P)),
            (g_row, I["L1_attn_ln_g"].unsqueeze(0).to_broadcast([P, P])), (b_row, I["L1_attn_ln_b"].unsqueeze(0).to_broadcast([P, P])),
            (fm_b2_row, I["L1_attn_fm_b2"].unsqueeze(0).to_broadcast([P, P])), (out_b_row, I["L1_ffn_out_proj_b"].unsqueeze(0).to_broadcast([P, P])),
            (in_b_row, I["L1_ffn_in_proj_b"].unsqueeze(0).to_broadcast([P, 3 * P]))]

        def qkv_b(b, m):
            return qkv[:, m, bass.ds(b, 1)].rearrange("p s c -> p (s c)")

        def batch(a, b):
            return a[:, bass.ds(b * SEQ, SEQ)]

        def split(a, **k):
            return a.rearrange("p (m d) -> p m d", d=P)

        block = ctx.enter_context(nc.Block())

        @block.sync
        def _(sp):
            xt = x_tok.rearrange("p (b m d) -> p b m d", b=NB, m=MT)
            for b in range(0, NB, 2):
                for h in range(2):
                    sp.dma_start(xt[:, b + h], x_view[:, b + h]).then_inc(s_x, 16)
            sp.dma_start(wud_raw, I["L0_attn_W"][0:2 * P].rearrange("(t p) k -> p t k", p=P)).then_inc(s_wud, 16)
            sp.wait_ge(s_zero, 1)

            def load_row(r, ap):
                full = ap.shape[0] // P
                if full:
                    sp.dma_start(rows[r:r + full, :], ap[0:full * P].rearrange("(t p) -> t p", p=P)).then_inc(s_rows, 16)
                if ap.shape[0] % P:
                    sp.dma_start(rows[r + full:r + full + 1, 0:ap.shape[0] % P], ap[full * P:ap.shape[0]].unsqueeze(0)).then_inc(s_rows, 16)

            for r, ap in row_list:
                load_row(r, ap)
            sp.dma_start(rot_raw[:], I["rotary"].rearrange("k (m p) d -> p k m d", p=P)).then_inc(s_tab, 16)
            bc0 = 2 * P + P * NS
            for i, src in enumerate((I["L0_attn_A"], I["L0_attn_b"][2 * P:bc0].rearrange("(d s) -> d s", s=NS),
                                     I["L0_attn_b"][bc0:bc0 + P * NS].rearrange("(d s) -> d s", s=NS))):
                sp.dma_start(abc_all[:, i], src).then_inc(s_tab, 16)
            meet(sp, "sp", 1)
            meet(sp, "sp", 2)
            with sp.Fori(0, LAYERS) as l:
                lay = bass.ds(l, 1)
                wbc_v = I["L0_attn_W"][2 * P:2 * P + 2 * P * NS].rearrange("(h d s) k -> d h s k", h=2, s=NS)
                for h in range(2):
                    sp.dma_start(wbc_raw[:, h], wbc_v[:, h, bass.ds(l * NSH, NSH)]).then_inc(s_lw, 16)
                sp.dma_start(wqkv, I["L0_ffn_wqkv"][lay].rearrange("a p (c n) -> p (a c) n", c=3)).then_inc(s_lw, 16)
                sp.dma_start(wo, I["L0_ffn_wo"][lay].rearrange("a (t p) n -> p (a t) n", p=P)).then_inc(s_lw, 16)
                sp.dma_start(w1[:, :, 0:HID], I["L0_ffn_w1"][lay].rearrange("a p (c n) -> p (a c) n", c=2)).then_inc(s_lw, 16)
                sp.dma_start(w2[:, 0:FT - 1], I["L0_ffn_w2"][lay, 0:(FT - 1) * P].rearrange("a (t p) n -> p (a t) n", p=P)).then_inc(s_lw, 16)
                sp.dma_start(w2[0:HID - (FT - 1) * P, FT - 1], I["L0_ffn_w2"][lay, (FT - 1) * P:HID].rearrange("a p n -> p (a n)")).then_inc(s_lw, 16)
                for i, nm in enumerate(("q", "k")):
                    sp.dma_start(qk_scale[:, i], I[f"L0_ffn_{nm}_scale"][lay].to_broadcast([P, HD])).then_inc(s_lw, 16)
                for k in range(3):
                    meet(sp, "sp", l * 3 + 3 + k)
            for b in range(NB):
                sp.dma_start(xn1.rearrange("p (b m d) -> p b m d", b=NB, m=MT)[:, b], x_view[:, b]).then_inc(s_xr, 16)
            for dst, src in second_list:
                sp.dma_start(dst, src).then_inc(s_w2nd, 16)
            for k in range(4):
                meet(sp, "sp", 9 + k)
            out_v = out.rearrange("b (m p) d -> p m b d", p=P)
            for m in range(MT):
                sp.wait_ge(z_fo.sem, z_fo.at(m, 1))
                sp.dma_start(out_v[:, m], fo[:, m % 2]).then_inc(z_dm[m % 2], 16)
            for s in z_dm:
                sp.wait_ge(s, 16 * MT // 2)

        @block.gpsimd
        def _(pool):
            pool.memset(ident[:], 0.0).then_inc(s_memset, 1)
            pool.memset(identb[:], 0.0).then_inc(s_memset, 1)
            pool.memset(maskb[:], 0.0).then_inc(s_memset, 1)
            pool.memset(pow_half[:], -0.5).then_inc(s_memset, 1)
            pool.memset(w1, 0.0).then_inc(s_memset, 1)
            pool.wait_ge(s_memset, 5)
            pool.memset(w2[HD:P, FT - 1], 0.0).then_inc(s_memset, 1)
            pool.wait_ge(s_memset, 6)
            for t in (ident, identb):
                pool.affine_select(out=t[:], in_=t[:], compare_op=ALU.not_equal, fill=1.0, base=0,
                                   pattern=[[-1, P]], channel_multiplier=1).then_inc(s_const, 1)
            n = 2
            for kind in range(2):
                for base, step, mult in ((0, 1, -1), (WIN, -1, 1), (-WIN, 1, 0))[:2 + kind]:
                    pool.wait_ge(s_const, n)
                    pool.affine_select(out=maskb[:, kind], in_=maskb[:, kind], compare_op=ALU.is_ge, fill=MASKED,
                                       base=base, pattern=[[step, KEYS]], channel_multiplier=mult).then_inc(s_const, 1)
                    n += 1
            pool.memset(upper[:], 1.0).then_inc(s_memset, 1)
            pool.memset(before[:], 0.0).then_inc(s_memset, 1)
            pool.wait_ge(s_memset, 8)
            pool.affine_select(out=upper[:], in_=upper[:], compare_op=ALU.is_ge, fill=0.0, base=0,
                               pattern=[[1, P]], channel_multiplier=-1).then_inc(s_const, 1)
            for e in range(1, EXP):
                pool.memset(before[:, e, 0:e], 1.0).then_inc(s_const, 1)
            wait_alone(pool, s_xstat, NB * MT)
            pool.tensor_scalar(x_var, x_mv[:, :, 1], EPS, 1.0, ALU.add, ALU.mult).then_inc(s_xvar, 1)
            pool.wait_ge(s_xvar, 1)
            pool.tensor_tensor(x_rstd, x_var, pow_half[:], ALU.pow).then_inc(s_xrstd, 1)
            with pool.Fori(0, NB) as b:
                wait_alone(pool, c_xT.sem, c_xT.at(b, 1))
                pool.tensor_copy(batch(state, b), batch(xt0, b)).then_inc(c_st0.sem, 1)
            meet(pool, "pool", 1)
            meet(pool, "pool", 2)
            for c in (a_rk, c_ya, e_st):
                pool.sem_inc(c.sem, c.per)
            with pool.Fori(0, LAYERS) as l:
                pool.memset(hpad[:, 0:WIN + 1], 0.0)
                pool.memset(kT[:, :, 0:WIN], 0.0)
                pool.memset(edge, 0.0)
                meet(pool, "pool", l * 3 + 3)
                with pool.Fori(0, NB) as b:
                    it = pool.snap(l * NB + b)

                    def rsqrt(m):
                        par = m % 2
                        if m >= 1:
                            pool.wait_ge(a_rn.sem, a_rn.at(it, m))
                        wait_alone(pool, a_ss.sem, a_ss.at(it, m + 1))
                        pool.tensor_scalar(sumsq_c, sumsq[:, par], 1e-24, 1.0, ALU.max, ALU.mult).then_inc(a_ssc.sem, 1)
                        pool.wait_ge(a_ssc.sem, a_ssc.at(it, m + 1))
                        n = 2 * (m - 1) if m >= 1 else 0
                        pool.wait_ge(a_exp.sem, a_exp.at(it, n))
                        pool.tensor_tensor(rnorm[:, par], sumsq_c, pow_half[:, 0:2 * HEADS], ALU.pow).then_inc(a_rn.sem, 1)

                    def rotate_k(m):
                        pool.wait_ge(a_kn.sem, a_kn.at(it, m + 1))
                        pool.wait_ge(a_qkt.sem, a_qkt.at(it, m))
                        kn = k_n.rearrange("p (h d) -> p h d", d=HD)
                        o = rot_k.rearrange("p a (h d) -> p a h d", d=HD)
                        H2 = HD // 2
                        pool.tensor_tensor(o[:, 0], kn, rot[:, 2, m].unsqueeze(1).to_broadcast([P, HEADS, HD]), ALU.mult)
                        pool.tensor_tensor(o[:, 1, :, 0:H2], kn[:, :, H2:HD], rot[:, 3, m, 0:H2].unsqueeze(1).to_broadcast([P, HEADS, H2]), ALU.mult)
                        pool.tensor_tensor(o[:, 1, :, H2:HD], kn[:, :, 0:H2], rot[:, 3, m, H2:HD].unsqueeze(1).to_broadcast([P, HEADS, H2]), ALU.mult).then_inc(a_rk.sem, 1)

                    def add_y(s):
                        pool.wait_ge(c_ch.sem, c_ch.at(it, s + 1))
                        wait_alone(pool, c_ya.sem, c_ya.at(it, s))
                        pool.tensor_tensor(batch(y_all, b), batch(y_all, b), ch[:, s % 2], ALU.add).then_inc(c_ya.sem, 1)

                    rsqrt(0)
                    rotate_k(0)
                    for m in range(MT):
                        if m + 1 < MT:
                            rsqrt(m + 1)
                        add_y(2 * m)
                        if m + 1 < MT:
                            rotate_k(m + 1)
                        add_y(2 * m + 1)
                meet(pool, "pool", l * 3 + 4)
                with pool.Fori(0, NB) as b:
                    it = pool.snap(l * NB + b)
                    wait_alone(pool, f_st.sem, f_st.at(it, 1))
                    pool.tensor_scalar(f_var, f_mv[:, 0, :, 1], EPS, 1.0, ALU.add, ALU.mult).then_inc(f_vr.sem, 1)
                    pool.wait_ge(f_vr.sem, f_vr.at(it, 1))
                    pool.tensor_tensor(f_rstd[:, 0], f_var, pow_half[:, 0:MT], ALU.pow).then_inc(f_rs.sem, 1)
                meet(pool, "pool", l * 3 + 5)
            meet(pool, "pool", 9)

            def rstd(b, k, ag, vr, rs):
                wait_alone(pool, ag.sem, ag.at(b, k + 1))
                pool.tensor_scalar(l_var, l_mv[:, :, 1], EPS, 1.0, ALU.add, ALU.mult).then_inc(vr.sem, 1)
                pool.wait_ge(vr.sem, vr.at(b, k + 1))
                pool.tensor_tensor(l_rstd, l_var, pow_half[:, 0:MT], ALU.pow).then_inc(rs.sem, 1)

            with pool.Fori(0, NB) as b:
                rstd(b, 0, x_ag, x_vr, x_rs)
            with pool.Fori(0, NB) as b:
                rstd(b, 0, l_ag, l_vr, l_rs)
                pool.wait_ge(l_z.sem, l_z.at(b, 1))
                pool.tensor_tensor(n_scaled, z_tok, g_row.unsqueeze(1).to_broadcast([P, MT, P]), ALU.mult).then_inc(l_ns.sem, 1)
                wait_alone(pool, l_ns.sem, l_ns.at(b, 1))
                pool.tensor_tensor(n_tok, n_scaled, b_row.unsqueeze(1).to_broadcast([P, MT, P]), ALU.add).then_inc(l_n.sem, 1)
                xb = xn1[:, bass.ds(b * SEQ, SEQ)].rearrange("p (m d) -> p m d", m=MT)
                pool.tensor_tensor(xn_b, xb, b_row.unsqueeze(1).to_broadcast([P, MT, P]), ALU.add).then_inc(l_xb.sem, 1)
                pool.tensor_tensor(xn_f, xb, fm_b2_row.unsqueeze(1).to_broadcast([P, MT, P]), ALU.add).then_inc(l_xf.sem, 1)
                rstd(b, 1, l_ag, l_vr, l_rs)
                rstd(b, 2, l_ag, l_vr, l_rs)
            meet(pool, "pool", 10)
            pool.memset(sc, MASKED).then_inc(s_pads, 1)
            with pool.Fori(0, MT) as m:
                for s in range(NB):
                    q = qkv[:, bass.ds(m, 1), s, 0:P].to_broadcast([P, s + 1, P])
                    k = qkv[:, bass.ds(m, 1), 0:s + 1, P:2 * P].rearrange("p a s c -> p (a s) c")
                    at = s * (s + 1) // 2 * P
                    if s == 0:
                        wait_alone(pool, h_dn.sem, m)
                    pool.tensor_tensor(prod[:, at:at + (s + 1) * P].rearrange("p (t c) -> p t c", c=P), q, k, ALU.mult).then_inc(h_pd.sem, 1)
                wait_alone(pool, h_ex.sem, h_ex.at(m, 1))
                for s in range(NB):
                    v = qkv[:, bass.ds(m, 1), 0:s + 1, 2 * P:3 * P].rearrange("p a s (h d) -> p (a s) h d", d=8)
                    w = pr[:, s, 0:s + 1].unsqueeze(3).to_broadcast([P, s + 1, 16, 8])
                    at = s * (s + 1) // 2 * P
                    pool.tensor_tensor(prod[:, at:at + (s + 1) * P].rearrange("p (t h d) -> p t h d", h=16, d=8), w, v, ALU.mult).then_inc(h_pv.sem, 1)
            meet(pool, "pool", 11)
            with pool.Fori(0, MT) as m:
                with pool.Fori(0, 2) as h:
                    g = pool.snap(m * 2 + h)
                    wait_alone(pool, e_t1.sem, e_t1.at(g - 1, 1))
                    pool.tensor_copy(e_att, qkv[:, bass.ds(m, 1), bass.ds(h * 4, 4), 0:P].rearrange("p a s c -> p (a s) c")).then_inc(e_ld.sem, 1)
                    xs = xn1.rearrange("p (s m c) -> p m s c", s=NB, m=MT)[:, bass.ds(m, 1), bass.ds(h * 4, 4)].rearrange("p a s c -> p (a s) c")
                    pool.tensor_tensor(e_in, xs, out_b_row.unsqueeze(1).to_broadcast([P, MT, P]), ALU.add).then_inc(e_ib.sem, 1)
                    wait_alone(pool, e_ag.sem, e_ag.at(g, 1))
                    pool.tensor_scalar(e_var, e_mv[:, :, 1], EPS, 1.0, ALU.add, ALU.mult).then_inc(e_vr.sem, 1)
                    pool.wait_ge(e_vr.sem, e_vr.at(g, 1))
                    pool.tensor_tensor(e_rstd, e_var, pow_half[:, 0:MT], ALU.pow).then_inc(e_rs.sem, 1)
                    wait_alone(pool, e_ya.sem, e_ya.at(g, EXP))
                    pool.tensor_copy(qkv[:, bass.ds(m, 1), bass.ds(h * 4, 4), P:2 * P].rearrange("p a s c -> p (a s) c"), e_acc).then_inc(e_st.sem, 1)
            meet(pool, "pool", 12)

        @block.scalar
        def _(act):
            act.wait_ge(s_cols_t, 1)
            act.activation(cols[:], bank[7][:, 0:N_ROWS], ACT.Copy).then_inc(s_cols, 1)
            act.wait_ge(s_wud_t, 1)
            act.activation(wud.rearrange("p t k -> p (t k)"), bank[6][:, 0:2 * P], ACT.Copy).then_inc(s_wud_c, 1)
            act.wait_ge(s_cols, 1)
            for c in (c_xT, c_u, c_drelu):
                act.sem_inc(c.sem, c.per)
            with act.Fori(0, NB) as b:
                wait_alone(act, c_xT_t.sem, c_xT_t.at(b, 1))
                act.activation(batch(xt0, b), bank[0][:, :], ACT.Copy).then_inc(c_xT.sem, 1)
                wait_alone(act, c_ups.sem, c_ups.at(b, 1))
                act.activation(batch(u_all, b), bank[1][:, :], ACT.Identity, bias=cols[:, R_BU:R_BU + 1]).then_inc(c_u.sem, 1)
                act.wait_ge(c_dps.sem, c_dps.at(b, 1))
                act.activation(batch(delta, b), bank[2][:, :], ACT.Abs, bias=cols[:, R_BD:R_BD + 1]).then_inc(c_dabs.sem, 1)
                act.activation(batch(y_all, b), bank[2][:, :], ACT.Relu, bias=cols[:, R_BD:R_BD + 1]).then_inc(c_drelu.sem, 1)
                wait_alone(act, c_dabs.sem, c_dabs.at(b, 1))
                act.activation(batch(delta, b), batch(delta, b), ACT.Exp, scale=-1.0)
            meet(act, "act", 1)
            with act.Fori(0, NB) as b:
                act.activation(batch(delta, b), batch(delta, b), ACT.Ln, bias=1.0).then_inc(c_dln.sem, 1)
            meet(act, "act", 2)
            for c in (p_wc, a_sq, a_qke, a_exp, a_be, f_hc, f_ne, f_ge):
                act.sem_inc(c.sem, c.per)
            with act.Fori(0, LAYERS) as l:
                for k in range(4):
                    act.wait_ge(p_wt.sem, p_wt.at(l, k + 1))
                    act.activation(wbc.rearrange("p h s k -> p (h s k)")[:, k * 512:(k + 1) * 512], bank[k][:, :], ACT.Copy).then_inc(p_wc.sem, 1)
                meet(act, "act", l * 3 + 3)
                with act.Fori(0, NB) as b:
                    it = act.snap(l * NB + b)
                    ring = [0]

                    def from_turn_bank(out_ap, in_ap, last=True):
                        if last:
                            ring[0] += 1
                        act.wait_ge(a_bf.sem, a_bf.at(it, ring[0] + (0 if last else 1)))
                        ins = act.activation(out_ap, in_ap, ACT.Copy)
                        if last:
                            ins.then_inc(a_be.sem, 1)

                    def square(m):
                        act.wait_ge(a_proj.sem, a_proj.at(it, m + 1))
                        act.wait_ge(a_ss.sem, a_ss.at(it, m))
                        act.activation(squares[:, 0], bank[0][:, :], ACT.Square)
                        act.activation(squares[:, 1], bank[1][:, :], ACT.Square).then_inc(a_sq.sem, 1)

                    def copy_qk(m):
                        act.wait_ge(a_qkt.sem, a_qkt.at(it, m + 1))
                        act.activation(qT.rearrange("p r t -> p (r t)"), bank[0][:, :], ACT.Copy)
                        act.activation(kT[:, :, WIN + m * P:WIN + (m + 1) * P], bank[1][:, :].rearrange("p (r t) -> p r t", t=P), ACT.Copy).then_inc(a_qke.sem, 1)

                    def decay(s):
                        wait_alone(act, c_sc.sem, c_sc.at(it, s - 1) if s >= 2 else c_sc.at(it - 1, SU - 1 + s))
                        act.activation(abar[:, s % 2], batch(delta, b), ACT.Exp, scale=abc[:, 0, s:s + 1]).then_inc(c_ab.sem, 1)

                    def softmax(m, step):
                        act.wait_ge(a_neg.sem, a_neg.at(it, 2 * m + step + 1))
                        for j in range(2):
                            for eo in range(2):
                                pair = 2 * step + j
                                h = 2 * pair + eo
                                ins = act.activation(probs[:, pair, eo * KEYS:(eo + 1) * KEYS], bank[4 + eo][:, j * KEYS:(j + 1) * KEYS], ACT.Exp,
                                                     scale=rnorm[:, m % 2, h:h + 1], bias=negmax[:, h:h + 1], accum_out=rowsum[:, h:h + 1])
                        ins.then_inc(a_exp.sem, 1)

                    def copy_probs(m, step):
                        for j in range(2):
                            from_turn_bank(probsT[:, j], bank[2][:, 0:2 * KEYS])

                    def copy_oT(m):
                        from_turn_bank(oT[:, :, m * P:(m + 1) * P], bank[2][:, :].rearrange("p (r t) -> p r t", t=P))

                    square(0)
                    from_turn_bank(vals[:, 0, 0].rearrange("p r d -> p (r d)"), bank[2][:, 0:256])
                    for i in range(1, MT):
                        from_turn_bank(vals[:, i].rearrange("p e r d -> p (e r d)"), bank[2][:, :])
                    from_turn_bank(vals[0:HD, MT, 0].rearrange("p r d -> p (r d)"), bank[2][0:HD, 0:256], last=False)
                    from_turn_bank(vals[:, MT, 1].rearrange("p r d -> p (r d)"), bank[2][:, 256:512])
                    for m in range(MT + 1):
                        if m < MT:
                            copy_qk(m)
                        if m:
                            copy_probs(m - 1, 1)
                        if m + 1 < MT:
                            square(m + 1)
                        if m < MT:
                            decay(2 * m)
                            softmax(m, 0)
                        if m:
                            copy_oT(m - 1)
                        if m < MT:
                            decay(2 * m + 1)
                            softmax(m, 1)
                            copy_probs(m, 0)
                meet(act, "act", l * 3 + 4)
                with act.Fori(0, NB) as b:
                    it = act.snap(l * NB + b)
                    wait_alone(act, f_tf.sem, f_tf.at(it - 1, 1))
                    act.activation(f_h[0:HD, 0], state[0:HD, bass.ds(b * SEQ, SEQ)], ACT.Copy)
                    act.activation(f_h[HD:P, 0, 1:SEQ], state[HD:P, bass.ds(b * SEQ, SEQ - 1)], ACT.Copy).then_inc(f_hc.sem, 1)
                    act.wait_ge(f_nt.sem, f_nt.at(it, 1))
                    act.activation(f_hnT[:, 0], bank[1][:, :], ACT.Copy).then_inc(f_ne.sem, 1)
                    for j in range(FT):
                        act.wait_ge(f_up.sem, f_up.at(it, j + 1))
                        act.wait_ge(f_ac.sem, f_ac.at(it, j - 1) if j >= 2 else f_ac.at(it - 1, FT - 1 + j))
                        act.activation(f_gelu[:, j % 2], bank[3 + 2 * (j % 2)][:, :], ACT.Gelu, bias=b1s[:, FT + j:FT + j + 1]).then_inc(f_ge.sem, 1)
                meet(act, "act", l * 3 + 5)
            with act.Fori(0, NB) as b:
                act.activation(batch(state, b), batch(state, b), ACT.Silu).then_inc(s_silu, 1)
            act.wait_ge(q_t, 1)
            act.activation(inpT, bank[0][:, 0:3 * P], ACT.Copy)
            act.activation(outpT, bank[1][:, 0:P], ACT.Copy)
            act.activation(routT, bank[2][:, 0:EXP], ACT.Copy).then_inc(q_tc, 1)
            meet(act, "act", 9)
            for c in (l_ue, l_we, l_tg, l_z2c):
                act.sem_inc(c.sem, c.per)
            with act.Fori(0, NB) as b:
                def gelu_up(k, j):
                    n = k * KT + j
                    act.wait_ge(l_uf.sem, l_uf.at(b, n + 1))
                    if j == 0:
                        if k == 2:
                            act.wait_ge(l_wf.sem, l_wf.at(b, 1))
                        elif k == 0:
                            act.wait_ge(l_ff.sem, l_ff.at(b - 1, 1))
                    act.activation(hid[:, k % 2, j], bank[4 + n % 2][:, :], ACT.Gelu, bias=up_bias[:, n:n + 1]).then_inc(l_ue.sem, 1)

                act.wait_ge(l_zt.sem, l_zt.at(b, 1))
                act.activation(zT, bank[1][:, :], ACT.Copy).then_inc(l_zc.sem, 1)
                for k, r in ((0, R_H1B2), (1, R_H2B2)):
                    for j in range(KT):
                        gelu_up(k, j)
                    act.wait_ge(l_wf.sem, l_wf.at(b, k + 1))
                    act.activation(wT[:, k], bank[6][:, :], ACT.Identity, bias=cols[:, r:r + 1]).then_inc(l_we.sem, 1)
                act.wait_ge(l_tf.sem, l_tf.at(b, 1))
                act.activation(t_gelu.rearrange("p m d -> p (m d)"), bank[7][:, :], ACT.Gelu).then_inc(l_tg.sem, 1)
                act.wait_ge(l_z2t.sem, l_z2t.at(b, 1))
                act.activation(z2T, bank[0][:, :], ACT.Copy).then_inc(l_z2c.sem, 1)
                for j in range(KT):
                    gelu_up(2, j)
            meet(act, "act", 10)
            with act.Fori(0, MT) as m:
                act.wait_ge(h_sb.sem, h_sb.at(m, 1))
                act.activation(pr, sc, ACT.Exp, scale=float(8) ** -0.5).then_inc(h_ex.sem, 1)
            meet(act, "act", 11)
            for c in (e_c2, e_ue):
                act.sem_inc(c.sem, c.per)
            with act.Fori(0, MT * 2) as g:
                act.wait_ge(e_t1.sem, e_t1.at(g, 1))
                act.activation(e_attT, bank[0][:, :], ACT.Copy).then_inc(e_c1.sem, 1)
                act.wait_ge(e_t2.sem, e_t2.at(g, 1))
                act.activation(e_zT, bank[0][:, :], ACT.Copy).then_inc(e_c2.sem, 1)
                act.wait_ge(e_sh.sem, e_sh.at(g, 1))
                act.activation(pexp, lg, ACT.Exp).then_inc(e_ex.sem, 1)
                for e in range(EXP):
                    for f in range(2):
                        n = 2 * e + f
                        act.wait_ge(e_uf.sem, e_uf.at(g, n + 1))
                        if f == 0:
                            act.wait_ge(e_yf.sem, e_yf.at(g, e - 1) if e >= 2 else e_yf.at(g - 1, EXP - 1 + e))
                        act.activation(e_hid[:, e % 2, f], bank[4 + n % 2][:, :], ACT.Gelu, bias=up_bias[:, 3 * KT + n:3 * KT + n + 1]).then_inc(e_ue.sem, 1)
            meet(act, "act", 12)
            with act.Fori(0, MT) as m:
                v = qkv[:, bass.ds(m, 1), :, P:2 * P].rearrange("p a s c -> p (a s) c")
                act.activation(v, v, ACT.Silu).then_inc(z_si.sem, 1)

        @block.vector
        def _(dve):
            dve.memset(rows[:], 0.0).then_inc(s_zero, 1)
            dve.wait_ge(s_x, 16 * NB)
            for i in range(NB * MT):
                if i >= 2:
                    dve.wait_ge(s_xstat, i - 1)
                dve.bn_stats(x_stats[:, i % 2], x_tok[:, i * P:(i + 1) * P]).then_inc(c_xn.sem, 1)
                if i >= 1:
                    dve.wait_ge(c_xn.sem, i)
                    dve.bn_aggr(x_mv[:, i - 1], x_stats[:, (i - 1) % 2]).then_inc(s_xstat, 1)
            dve.wait_ge(c_xn.sem, NB * MT)
            dve.bn_aggr(x_mv[:, NB * MT - 1], x_stats[:, 1]).then_inc(s_xstat, 1)
            dve.wait_ge(s_xrstd, 1)
            wait_alone(dve, s_xstat, NB * MT)
            with dve.Fori(0, NB) as b:
                dve.wait_ge(c_xT_t.sem, c_xT_t.at(b - 1, 1))
                for m in range(MT):
                    i = b * MT + m
                    ins = dve.tensor_scalar(xn[:, 0, m], x_tok[:, bass.ds(i * P, P)], x_mv[:, bass.ds(i, 1), 0], x_rstd[:, bass.ds(i, 1)],
                                            ALU.subtract, ALU.mult)
                ins.then_inc(c_xn.sem, 1)
            meet(dve, "dve", 1)
            with dve.Fori(0, NB) as b:
                dve.wait_ge(c_dln.sem, b + 1)
                dve.tensor_tensor(batch(delta, b), batch(delta, b), batch(y_all, b), ALU.add).then_inc(s_dlt, 1)
                dve.wait_ge(s_dlt, b + 1)
                dve.tensor_scalar(batch(y_all, b), batch(u_all, b), cols[:, R_D:R_D + 1], None, ALU.mult).then_inc(s_y0, 1)
            meet(dve, "dve", 2)
            for c in (a_ss, a_oe, c_bu, c_sc, c_ch, f_st, f_ac, f_ad):
                dve.sem_inc(c.sem, c.per)
            with dve.Fori(0, LAYERS) as l:
                dve.wait_ge(s_tab, 16 * 4)
                dve.tensor_copy(abc, abc_all[:, :, bass.ds(l * NSH, NSH)]).then_inc(p_lc.sem, 1)
                dve.tensor_copy(lcol, cols[:, bass.ds(l * L_COLS + R_LAYER, L_COLS)]).then_inc(p_lc.sem, 1)
                dve.wait_ge(p_lc.sem, p_lc.at(l, 2))
                dve.wait_ge(s_lw, l * 144 + 144)
                H2 = HD // 2
                for t in range(4):
                    s = qk_scale[:, t // 2]
                    for a, c in (((0, HD),) if t % 2 == 0 else ((0, H2), (H2, HD))):
                        w = c - a
                        src = a if t % 2 == 0 else (H2 if a == 0 else 0)
                        dve.tensor_tensor(rot[:, t, :, a:c], rot_raw[:, t, :, a:c], s[:, src:src + w].unsqueeze(1).to_broadcast([P, MT, w]),
                                          ALU.mult).then_inc(p_rot.sem, 1)
                dve.tensor_scalar(w1s, w1, lcol[:, 2 * FT + 1:2 * FT + 2], None, ALU.mult).then_inc(p_w1s.sem, 1)
                dve.wait_ge(p_b1p.sem, p_b1p.at(l, 1))
                dve.tensor_tensor(b1s, bank[5][:, 0:2 * FT], lcol[:, 0:2 * FT], ALU.add).then_inc(p_b1s.sem, 1)
                meet(dve, "dve", l * 3 + 3)
                with dve.Fori(0, NB) as b:
                    it = dve.snap(l * NB + b)

                    def sum_squares(m):
                        dve.wait_ge(a_sq.sem, a_sq.at(it, m + 1))
                        n = m - 1 if m >= 2 else None
                        if m >= 2:
                            dve.wait_ge(a_ssc.sem, a_ssc.at(it, m - 1))
                        dve.tensor_reduce(sumsq[:, m % 2], squares.rearrange("p a (h d) -> p (a h) d", d=HD), AX.X, ALU.add).then_inc(a_ss.sem, 1)

                    def rotate(m):
                        par = m % 2
                        dve.wait_ge(a_rn.sem, a_rn.at(it, m + 1))
                        dve.wait_ge(a_rk.sem, a_rk.at(it, m))
                        kb = bank[1][:, :].rearrange("p (h d) -> p h d", d=HD)
                        dve.tensor_tensor(k_n.rearrange("p (h d) -> p h d", d=HD), kb, rnorm[:, par, HEADS:2 * HEADS].unsqueeze(2).to_broadcast([P, HEADS, HD]),
                                          ALU.mult).then_inc(a_kn.sem, 1)
                        dve.wait_ge(a_qkt.sem, a_qkt.at(it, m))
                        qb = bank[0][:, :].rearrange("p (h d) -> p h d", d=HD)
                        o = rot_q.rearrange("p a (h d) -> p a h d", d=HD)
                        dve.tensor_tensor(o[:, 0], qb, rot[:, 0, m].unsqueeze(1).to_broadcast([P, HEADS, HD]), ALU.mult)
                        dve.tensor_tensor(o[:, 1, :, 0:H2], qb[:, :, H2:HD], rot[:, 1, m, 0:H2].unsqueeze(1).to_broadcast([P, HEADS, H2]), ALU.mult)
                        dve.tensor_tensor(o[:, 1, :, H2:HD], qb[:, :, 0:H2], rot[:, 1, m, H2:HD].unsqueeze(1).to_broadcast([P, HEADS, H2]), ALU.mult).then_inc(a_rq.sem, 1)

                    def maxima(m, step):
                        n = 2 * m + step + 1
                        dve.wait_ge(a_sim.sem, a_sim.at(it, n))
                        mxs = mx[:, 4 * step:4 * step + 4].rearrange("p (j e) -> p e j", e=2)
                        for eo in range(2):
                            ins = dve.tensor_reduce(mxs[:, eo], bank[4 + eo][:, 0:2 * KEYS].rearrange("p (j k) -> p j k", k=KEYS), AX.X, ALU.max)
                        ins.then_inc(a_max.sem, 1)
                        dve.wait_ge(a_max.sem, a_max.at(it, n))
                        h4 = slice(4 * step, 4 * step + 4)
                        dve.scalar_tensor_tensor(out=negmax[:, h4], in0=mx[:, h4], scalar=-1.0, in1=rnorm[:, m % 2, h4], op0=ALU.mult, op1=ALU.mult).then_inc(a_neg.sem, 1)

                    def scan(s):
                        dve.wait_ge(c_bps.sem, c_bps.at(it, s + 1))
                        dve.wait_ge(c_sc.sem, c_sc.at(it, s))
                        dve.scalar_tensor_tensor(out=bu, in0=bank[6][:, :], scalar=abc[:, 1, s:s + 1], in1=batch(u_all, b), op0=ALU.add, op1=ALU.mult).then_inc(c_bu.sem, 1)
                        dve.wait_ge(c_bu.sem, c_bu.at(it, s + 1))
                        dve.wait_ge(c_ab.sem, c_ab.at(it, s + 1))
                        dve.wait_ge(c_ch.sem, c_ch.at(it, s))
                        dve.tensor_tensor_scan(hs, abar[:, s % 2], bu, 0.0, ALU.mult, ALU.add).then_inc(c_sc.sem, 1)
                        dve.wait_ge(c_sc.sem, c_sc.at(it, s + 1))
                        dve.wait_ge(c_cps.sem, c_cps.at(it, s + 1))
                        dve.wait_ge(c_ya.sem, c_ya.at(it, s - 1) if s >= 2 else c_ya.at(it - 1, SU - 1 + s))
                        dve.scalar_tensor_tensor(out=ch[:, s % 2], in0=bank[7][:, :], scalar=abc[:, 2, s:s + 1], in1=hs, op0=ALU.add, op1=ALU.mult).then_inc(c_ch.sem, 1)

                    def normalise(m):
                        dve.wait_ge(a_exp.sem, a_exp.at(it, 2 * m + 2))
                        dve.reciprocal(rinv, rowsum).then_inc(a_ri.sem, 1)
                        dve.wait_ge(a_ri.sem, a_ri.at(it, m + 1))
                        dve.wait_ge(a_of.sem, a_of.at(it, m + 1))
                        if m:
                            dve.wait_ge(a_bf.sem, a_bf.at(it, oT_fill[m - 1]))
                        dve.tensor_tensor(o_tok.rearrange("p (h d) -> p h d", d=HD), bank[3][:, :].rearrange("p (h d) -> p h d", d=HD),
                                          rinv.unsqueeze(2).to_broadcast([P, HEADS, HD]), ALU.mult).then_inc(a_oe.sem, 1)

                    dve.wait_ge(a_proj.sem, a_proj.at(it, 0))
                    dve.tensor_copy(hpad[0:HD, WIN:WIN + SEQ], state[0:HD, bass.ds(b * SEQ, SEQ)])
                    dve.tensor_copy(hpad[HD:P, WIN + 1:WIN + SEQ], state[HD:P, bass.ds(b * SEQ, SEQ - 1)]).then_inc(a_h.sem, 1)
                    sum_squares(0)
                    dve.wait_ge(a_be.sem, a_be.at(it, MT + 1))
                    dve.tensor_copy(edge[0:HD, :, :, 0], vals[0:HD, 1:MT + 1, 0])
                    dve.tensor_copy(edge[HD:P, 1:MT, :, 1], vals[HD:P, 1:MT, 1]).then_inc(a_edge.sem, 1)
                    rotate(0)
                    for m in range(MT + 1):
                        if m:
                            normalise(m - 1)
                        if m + 1 < MT:
                            sum_squares(m + 1)
                        if m < MT:
                            maxima(m, 0)
                            scan(2 * m)
                        if m + 1 < MT:
                            rotate(m + 1)
                        if m < MT:
                            maxima(m, 1)
                            scan(2 * m + 1)
                    dve.wait_ge(a_of.sem, a_of.at(it, TU + 1))
                    dve.tensor_tensor(batch(state, b), bank[3][:, :], batch(state, b), ALU.add).then_inc(a_oe.sem, 1)
                meet(dve, "dve", l * 3 + 4)
                dve.memset(f_h[HD:P, 0, 0:1], 0.0).then_inc(f_zero.sem, 1)
                with dve.Fori(0, NB) as b:
                    it = dve.snap(l * NB + b)
                    dve.wait_ge(f_tf.sem, f_tf.at(it, 1))
                    for m in range(MT):
                        ins = dve.bn_stats(f_stats[:, m], bank[0][:, m * P:(m + 1) * P])
                    ins.then_inc(f_st2.sem, 1)
                    wait_alone(dve, f_st2.sem, f_st2.at(it, 1))
                    for m in range(MT):
                        ins = dve.bn_aggr(f_mv[:, 0, m], f_stats[:, m])
                    ins.then_inc(f_st.sem, 1)
                    dve.wait_ge(f_st.sem, f_st.at(it, 1))
                    dve.wait_ge(f_rs.sem, f_rs.at(it, 1))
                    for m in range(MT):
                        ins = dve.tensor_scalar(f_hn[:, m], bank[0][:, m * P:(m + 1) * P], f_mv[:, 0, m, 0:1], f_rstd[:, 0, m:m + 1], ALU.subtract, ALU.mult)
                    ins.then_inc(f_nm.sem, 1)
                    for j in range(FT):
                        dve.wait_ge(f_ge.sem, f_ge.at(it, j + 1))
                        if j == 0:
                            dve.wait_ge(f_dn.sem, it)
                        dve.scalar_tensor_tensor(out=f_act[:, j], in0=bank[2 + 2 * (j % 2)][:, :], scalar=b1s[:, j:j + 1], in1=f_gelu[:, j % 2],
                                                 op0=ALU.add, op1=ALU.mult).then_inc(f_ac.sem, 1)
                    dve.wait_ge(f_dn.sem, f_dn.at(it, 1))
                    dve.scalar_tensor_tensor(out=batch(state, b), in0=bank[6][:, :], scalar=lcol[:, 2 * FT:2 * FT + 1], in1=batch(state, b),
                                             op0=ALU.add, op1=ALU.add).then_inc(f_ad.sem, 1)
                meet(dve, "dve", l * 3 + 5)
            dve.tensor_copy(n1b_wide, cols[:, R_N1B:R_N1B + 1].to_broadcast([P, P]))
            dve.tensor_copy(n2b_wide, cols[:, R_N2B:R_N2B + 1].to_broadcast([P, P])).then_inc(q_wide, 1)
            dve.wait_ge(q_prod, 1)
            dve.wait_ge(s_w2nd, 16 * len(second_list))
            for k, r in enumerate((R_H1B1, R_H2B1, R_FMB1)):
                dve.tensor_tensor(up_bias[:, k * KT:(k + 1) * KT], bank[5][:, k * KT:(k + 1) * KT], cols[:, r:r + KT], ALU.add)
            dve.tensor_copy(up_bias[:, 3 * KT:], bank[5][:, 3 * KT:3 * KT + 2 * EXP])
            dve.tensor_tensor(in_b_row, bank[6][:, 0:3 * P], in_b_row, ALU.add)
            dve.tensor_copy(rout_b_row, bank[7][:, 0:EXP])
            dve.tensor_scalar(w_up, w_up, cols[:, R_G:R_G + 1], None, ALU.mult)
            dve.tensor_scalar(inpT, inpT, cols[:, R_N1W:R_N1W + 1], None, ALU.mult)
            dve.tensor_scalar(routT, routT, cols[:, R_N2W:R_N2W + 1], None, ALU.mult)
            dve.tensor_scalar(m_up, m_up, cols[:, R_N2W:R_N2W + 1], None, ALU.mult).then_inc(q_row, 1)
            meet(dve, "dve", 9)
            dve.wait_ge(s_xr, 16 * NB)
            for c in (l_x1, l_re, l_so, z_pr, e_ya):
                dve.sem_inc(c.sem, c.per)

            def tile_of(a, b):
                return lambda m: a[:, bass.ds(b * SEQ + m * P, P)]

            def layernorm(b, k, bn, ag, rs, src, dst, done):
                for m in range(MT):
                    ins = dve.bn_stats(l_stats[:, m], src(m))
                ins.then_inc(bn.sem, 1)
                wait_alone(dve, bn.sem, bn.at(b, k + 1))
                for m in range(MT):
                    ins = dve.bn_aggr(l_mv[:, m], l_stats[:, m])
                ins.then_inc(ag.sem, 1)
                dve.wait_ge(ag.sem, ag.at(b, k + 1))
                dve.wait_ge(rs.sem, rs.at(b, k + 1))
                for m in range(MT):
                    ins = dve.tensor_scalar(dst(m), src(m), l_mv[:, m, 0:1], l_rstd[:, m:m + 1], ALU.subtract, ALU.mult)
                ins.then_inc(done.sem, 1)

            with dve.Fori(0, NB) as b:
                dve.wait_ge(l_sgt.sem, l_sgt.at(b - 1, 1))
                dve.tensor_tensor(sg, batch(y_all, b), batch(state, b), ALU.mult).then_inc(l_sg.sem, 1)
                dve.wait_ge(l_sgt.sem, l_sgt.at(b, 1))
                dve.tensor_tensor(batch(x1, b), bank[0][:, :], batch(xn1, b), ALU.add).then_inc(l_x1.sem, 1)
                wait_alone(dve, l_x1.sem, l_x1.at(b, 1))
                layernorm(b, 0, x_bn, x_ag, x_rs, tile_of(x1, b), tile_of(xn1, b), l_xn)
            wait_alone(dve, l_xn.sem, NB)
            with dve.Fori(0, NB) as b:
                layernorm(b, 0, l_bn, l_ag, l_rs, tile_of(xn1, b), lambda m: z_tok[:, m], l_z)
                for m in range(MT):
                    dve.wait_ge(l_rf.sem, l_rf.at(b, m + 1))
                    dve.tensor_tensor(qkv_b(b, m), bank[2 + m % 2][:, 0:3 * P], in_b_row, ALU.add).then_inc(l_re.sem, 1)
                for j in range(MT):
                    n = MT + j
                    dve.wait_ge(l_rf.sem, l_rf.at(b, n + 1))
                    dve.wait_ge(l_tg.sem, l_tg.at(b - 1, 1))
                    ins = dve.tensor_tensor(w3[:, j, 0:P], bank[2 + n % 2][:, 0:P], upper[:], ALU.mult)
                    if j < MT - 1:
                        ins = dve.tensor_copy(w3[:, j, P:(MT - j) * P], bank[2 + n % 2][:, P:(MT - j) * P])
                    ins.then_inc(l_re.sem, 1)
                wait_alone(dve, l_tg.sem, l_tg.at(b, 1))
                layernorm(b, 1, l_bn, l_ag, l_rs, lambda m: t_gelu[:, m], lambda m: t_norm[:, m], l_tn)
                dve.wait_ge(l_tn.sem, l_tn.at(b, 1))
                dve.tensor_tensor(t_gain, t_norm, g_row.unsqueeze(1).to_broadcast([P, MT, P]), ALU.mult).then_inc(l_ta.sem, 1)
                dve.wait_ge(l_ta.sem, l_ta.at(b, 1))
                dve.wait_ge(l_xb.sem, l_xb.at(b, 1))
                dve.tensor_tensor(x_mid, t_gain, xn_b, ALU.add).then_inc(l_xm.sem, 1)
                wait_alone(dve, l_xm.sem, l_xm.at(b, 1))
                layernorm(b, 2, l_bn, l_ag, l_rs, lambda m: x_mid[:, m], lambda m: z2[:, m], l_z2)
                dve.wait_ge(l_ff.sem, l_ff.at(b, 1))
                dve.wait_ge(l_xf.sem, l_xf.at(b, 1))
                dve.tensor_tensor(batch(s_out, b), bank[1][:, :], xn_f.rearrange("p m d -> p (m d)"), ALU.add).then_inc(l_so.sem, 1)
            meet(dve, "dve", 10)
            wait_alone(dve, s_pads, 1)
            with dve.Fori(0, MT) as m:
                for s in range(NB):
                    at = s * (s + 1) // 2 * P
                    dve.wait_ge(h_pd.sem, h_pd.at(m, s + 1))
                    ins = dve.tensor_reduce(sc[:, s, 0:s + 1].rearrange("p t h -> p (t h)"), prod[:, at:at + (s + 1) * P].rearrange("p (g d) -> p g d", d=8), AX.X, ALU.add)
                ins.then_inc(h_sc.sem, 1)
                dve.wait_ge(h_sc.sem, h_sc.at(m, 1))
                dve.tensor_reduce(smax, sc.rearrange("p s t h -> p s h t"), AX.X, ALU.max).then_inc(h_mx.sem, 1)
                dve.wait_ge(h_mx.sem, h_mx.at(m, 1))
                dve.tensor_tensor(sc, sc, smax.unsqueeze(2).to_broadcast([P, NB, NB, 16]), ALU.subtract).then_inc(h_sb.sem, 1)
                dve.wait_ge(h_ex.sem, h_ex.at(m, 1))
                dve.tensor_reduce(ssum, pr.rearrange("p s t h -> p s h t"), AX.X, ALU.add).then_inc(h_sm.sem, 1)
                dve.wait_ge(h_sm.sem, h_sm.at(m, 1))
                dve.reciprocal(sinv, ssum).then_inc(h_iv.sem, 1)
                for s in range(NB):
                    at = s * (s + 1) // 2 * P
                    dve.wait_ge(h_pv.sem, h_pv.at(m, s + 1))
                    ins = dve.tensor_reduce(att[:, s], prod[:, at:at + (s + 1) * P].rearrange("p (t c) -> p c t", c=P), AX.X, ALU.add)
                ins.then_inc(h_at.sem, 1)
                dve.wait_ge(h_at.sem, h_at.at(m, 1))
                dve.tensor_tensor(qkv[:, bass.ds(m, 1), :, 0:P].rearrange("p a s (h d) -> p (a s) h d", d=8), att.rearrange("p s (h d) -> p s h d", d=8),
                                  sinv.unsqueeze(3).to_broadcast([P, NB, 16, 8]), ALU.mult).then_inc(h_dn.sem, 1)
            meet(dve, "dve", 11)
            with dve.Fori(0, MT * 2) as g:
                dve.wait_ge(e_pf.sem, e_pf.at(g, 1))
                dve.wait_ge(e_ib.sem, e_ib.at(g, 1))
                dve.wait_ge(e_st.sem, e_st.at(g - 1, 1))
                dve.tensor_tensor(e_acc.rearrange("p m d -> p (m d)"), bank[1][:, :], e_in.rearrange("p m d -> p (m d)"), ALU.add).then_inc(e_x1.sem, 1)
                wait_alone(dve, e_x1.sem, e_x1.at(g, 1))
                for i in range(MT):
                    ins = dve.bn_stats(e_stats[:, i], e_acc[:, i])
                ins.then_inc(e_bn.sem, 1)
                wait_alone(dve, e_bn.sem, e_bn.at(g, 1))
                for i in range(MT):
                    ins = dve.bn_aggr(e_mv[:, i], e_stats[:, i])
                ins.then_inc(e_ag.sem, 1)
                dve.wait_ge(e_ag.sem, e_ag.at(g, 1))
                dve.wait_ge(e_rs.sem, e_rs.at(g, 1))
                for i in range(MT):
                    ins = dve.tensor_scalar(e_z[:, i], e_acc[:, i], e_mv[:, i, 0:1], e_rstd[:, i:i + 1], ALU.subtract, ALU.mult)
                ins.then_inc(e_zd.sem, 1)
                dve.wait_ge(e_rf.sem, e_rf.at(g, 1))
                dve.tensor_tensor(lg, bank[2][:, 0:MT * EXP].rearrange("p (i e) -> p i e", e=EXP), rout_b_row.unsqueeze(1).to_broadcast([P, MT, EXP]), ALU.add).then_inc(e_lg.sem, 1)
                dve.wait_ge(e_lg.sem, e_lg.at(g, 1))
                dve.tensor_reduce(lmax, lg, AX.X, ALU.max).then_inc(e_lg.sem, 1)
                dve.wait_ge(e_lg.sem, e_lg.at(g, 2))
                dve.tensor_tensor(lg, lg, lmax.unsqueeze(2).to_broadcast([P, MT, EXP]), ALU.subtract).then_inc(e_sh.sem, 1)
                dve.wait_ge(e_ex.sem, e_ex.at(g, 1))
                dve.tensor_reduce(lsum, pexp, AX.X, ALU.add).then_inc(e_sm.sem, 1)
                dve.wait_ge(e_sm.sem, e_sm.at(g, 1))
                dve.reciprocal(linv, lsum).then_inc(e_sm.sem, 1)
                dve.wait_ge(e_sm.sem, e_sm.at(g, 2))
                dve.tensor_tensor(prob, pexp, linv.unsqueeze(2).to_broadcast([P, MT, EXP]), ALU.mult).then_inc(e_pr.sem, 1)
                dve.wait_ge(e_pr.sem, e_pr.at(g, 1))
                other = prob.unsqueeze(2).to_broadcast([P, MT, EXP, EXP])
                own = prob.unsqueeze(3).to_broadcast([P, MT, EXP, EXP])
                dve.tensor_tensor(above, other, own, ALU.is_gt).then_inc(e_cm.sem, 1)
                dve.tensor_tensor(equal, other, own, ALU.is_equal).then_inc(e_cm.sem, 1)
                dve.wait_ge(e_cm.sem, e_cm.at(g, 2))
                dve.tensor_tensor(equal, equal, before[:].unsqueeze(1).to_broadcast([P, MT, EXP, EXP]), ALU.mult).then_inc(e_cm.sem, 1)
                dve.wait_ge(e_cm.sem, e_cm.at(g, 3))
                dve.tensor_tensor(above, above, equal, ALU.add).then_inc(e_cm.sem, 1)
                dve.wait_ge(e_cm.sem, e_cm.at(g, 4))
                dve.tensor_reduce(rank, above, AX.X, ALU.add).then_inc(e_rk.sem, 1)
                dve.wait_ge(e_rk.sem, e_rk.at(g, 1))
                dve.scalar_tensor_tensor(out=gates, in0=rank, scalar=2.0, in1=prob, op0=ALU.is_lt, op1=ALU.mult).then_inc(e_gt.sem, 1)
                dve.wait_ge(e_gt.sem, e_gt.at(g, 1))
                for e in range(EXP):
                    dve.wait_ge(e_yf.sem, e_yf.at(g, e + 1))
                    if e:
                        dve.wait_ge(e_ya.sem, e_ya.at(g, e))
                    for i in range(MT):
                        ins = dve.scalar_tensor_tensor(out=e_acc[:, i], in0=bank[6 + e % 2][:, i * P:(i + 1) * P], scalar=gates[:, i, e:e + 1], in1=e_acc[:, i], op0=ALU.mult, op1=ALU.add)
                    ins.then_inc(e_ya.sem, 1)
            meet(dve, "dve", 12)
            for m in range(MT):
                dve.wait_ge(z_si.sem, m + 1)
                if m >= 2:
                    dve.wait_ge(z_dm[m % 2], 16 * (m // 2))
                so = s_out.rearrange("p (s m c) -> p m s c", s=NB, m=MT)[:, m]
                xo = x1.rearrange("p (s m c) -> p m s c", s=NB, m=MT)[:, m]
                dve.tensor_tensor(fin[:, m % 2], so, qkv[:, m, :, P:2 * P], ALU.mult).then_inc(z_pr.sem, 1)
                dve.wait_ge(z_pr.sem, z_pr.at(m, 1))
                dve.tensor_tensor(fo[:, m % 2], fin[:, m % 2], xo, ALU.add).then_inc(z_fo.sem, 1)

        @block.tensor
        def _(pe):
            pe.wait_ge(s_const, 2 + 5)
            pe.wait_ge(s_rows, 16 * n_row_dmas)
            pe.transpose(bank[7][:, 0:N_ROWS], rows[:], ident[0:N_ROWS, 0:N_ROWS]).then_inc(s_cols_t, 1)
            pe.wait_ge(s_wud, 16)
            for t in range(2):
                ins = pe.transpose(bank[6][:, t * P:(t + 1) * P], wud_raw[:, t], ident[:])
            ins.then_inc(s_wud_t, 1)
            pe.wait_ge(s_wud_c, 1)
            pe.sem_inc(c_xT_t.sem, 1)
            with pe.Fori(0, NB) as b:
                pe.wait_ge(c_xn.sem, b + NB * MT + 1)
                pe.wait_ge(c_xT.sem, c_xT.at(b, 0))
                for m in range(MT):
                    ins = pe.transpose(bank[0][:, m * P:(m + 1) * P], xn[:, 0, m], ident[:])
                ins.then_inc(c_xT_t.sem, 1)
                pe.wait_ge(c_xT.sem, c_xT.at(b, 1))
                pe.wait_ge(c_u.sem, c_u.at(b, 0))
                pe.matmul(bank[1][:, :], wud[:, 0], batch(xt0, b), start=True, stop=True).then_inc(c_ups.sem, 1)
                pe.wait_ge(c_drelu.sem, c_drelu.at(b, 0))
                pe.matmul(bank[2][:, :], wud[:, 1], batch(xt0, b), start=True, stop=True).then_inc(c_dps.sem, 1)
            meet(pe, "pe", 1)
            meet(pe, "pe", 2)
            for c in (p_wt, a_proj, a_qkt, f_tf, f_nt):
                pe.sem_inc(c.sem, c.per)
            with pe.Fori(0, LAYERS) as l:
                pe.wait_ge(s_lw, l * 144 + 144)
                wr = wbc_raw.rearrange("p h s k -> p (h s) k")
                for i in range(2 * NSH):
                    ins = pe.transpose(bank[i // 4][:, (i % 4) * P:(i % 4 + 1) * P], wr[:, i], ident[:])
                    if i % 4 == 3:
                        ins.then_inc(p_wt.sem, 1)
                pe.wait_ge(p_lc.sem, p_lc.at(l, 2))
                for j in range(2 * FT):
                    ins = pe.matmul(bank[5][:, j:j + 1], w1[:, j // FT, (j % FT) * P:(j % FT + 1) * P], lcol[:, 2 * FT + 2:2 * FT + 3], start=True, stop=True)
                ins.then_inc(p_b1p.sem, 1)
                meet(pe, "pe", l * 3 + 3)
                with pe.Fori(0, NB) as b:
                    it = pe.snap(l * NB + b)
                    ring = [0]

                    def turn_bank_free():
                        pe.wait_ge(a_be.sem, a_be.at(it, ring[0]))
                        ring[0] += 1

                    def project(m):
                        pe.wait_ge(a_qke.sem, a_qke.at(it, m))
                        lhs = hpad[:, WIN + m * P:WIN + (m + 1) * P]
                        pe.matmul(bank[0][:, :], lhs, wqkv[:, 0], start=True, stop=True)
                        pe.matmul(bank[1][:, :], lhs, wqkv[:, 1], start=True, stop=True).then_inc(a_proj.sem, 1)

                    def values(i):
                        turn_bank_free()
                        wv = wqkv[:, 2].rearrange("p (r e d) -> p e r d", e=2, d=HD)
                        n = P if i < MT else HD
                        ins = pe.matmul(bank[2][0:n, 0:256], hpad[:, i * P:i * P + n], wv[:, 0], start=True, stop=True)
                        if i:
                            ins = pe.matmul(bank[2][:, 256:512], hpad[:, WIN + (i - 1) * P:WIN + i * P], wv[:, 1], start=True, stop=True)
                        ins.then_inc(a_bf.sem, 1)

                    def turn_qk(m):
                        pe.wait_ge(a_rq.sem, a_rq.at(it, m + 1))
                        pe.wait_ge(a_rk.sem, a_rk.at(it, m + 1))
                        for w, t in enumerate((rot_q, rot_k)):
                            for r in range(PAIRS):
                                for i in range(2):
                                    ins = pe.matmul(bank[w][:, r * P:(r + 1) * P], t[:, i, r * P:(r + 1) * P], ident[:], is_transpose=True, start=(i == 0), stop=(i == 1))
                        ins.then_inc(a_qkt.sem, 1)

                    def scores(m, step):
                        pe.wait_ge(a_qke.sem, a_qke.at(it, m + 1))
                        n = 2 * m + step
                        pe.wait_ge(a_exp.sem, a_exp.at(it, n))
                        mask = maskb[:, 1 if m == 0 else 0].unsqueeze(1).to_broadcast([P, 2, KEYS])
                        for eo in range(2):
                            pe.matmul(bank[4 + eo][:, 0:2 * KEYS], identb[:], mask, start=True, stop=False)
                        for j in range(2):
                            for eo in range(2):
                                ps = slice(eo * HD, (eo + 1) * HD)
                                ins = pe.matmul(bank[4 + eo][:, j * KEYS:(j + 1) * KEYS], qT[ps, 2 * step + j], kT[ps, 2 * step + j, m * P:m * P + KEYS],
                                                start=False, stop=(j == 1))
                        ins.then_inc(a_sim.sem, 1)

                    def attend(m, step):
                        for j in range(2):
                            pair = 2 * step + j
                            if j == 0:
                                pe.wait_ge(a_exp.sem, a_exp.at(it, 2 * m + step + 1))
                            turn_bank_free()
                            for i in range(3):
                                ins = pe.transpose(bank[2][:, i * P:(i + 1) * P], probs[:, pair, i * P:(i + 1) * P], ident[:])
                            ins.then_inc(a_bf.sem, 1)
                            pe.wait_ge(a_be.sem, a_be.at(it, ring[0]))
                            if pair == 0 and m == 0:
                                pe.wait_ge(a_edge.sem, a_edge.at(it, 1))
                            if pair == 0:
                                pe.wait_ge(a_oe.sem, a_oe.at(it, m))
                            pt = probsT[:, j]
                            o = bank[3][:, pair * P:(pair + 1) * P]
                            pe.matmul(o, pt[:, P:2 * P], edge[:, m, pair], start=True, stop=False)
                            pe.matmul(o[:, 0:HD], pt[:, 0:P], vals[:, m, 0, pair], start=False, stop=False)
                            ins = pe.matmul(o[:, HD:P], pt[:, 2 * P:3 * P], vals[:, m + 1, 1, pair], start=False, stop=True)
                        if step == 1:
                            ins.then_inc(a_of.sem, 1)

                    def turn_o(m):
                        pe.wait_ge(a_oe.sem, a_oe.at(it, m + 1))
                        turn_bank_free()
                        for r in range(MT):
                            ins = pe.transpose(bank[2][:, r * P:(r + 1) * P], o_tok[:, r * P:(r + 1) * P], ident[:])
                        ins.then_inc(a_bf.sem, 1)

                    def scan_inputs(s):
                        pe.wait_ge(c_bu.sem, c_bu.at(it, s))
                        pe.matmul(bank[6][:, :], wbc[:, 0, s], batch(xt0, b), start=True, stop=True).then_inc(c_bps.sem, 1)
                        pe.wait_ge(c_ch.sem, c_ch.at(it, s))
                        pe.matmul(bank[7][:, :], wbc[:, 1, s], batch(xt0, b), start=True, stop=True).then_inc(c_cps.sem, 1)

                    pe.wait_ge(a_h.sem, a_h.at(it, 1))
                    project(0)
                    for i in range(MT + 1):
                        values(i)
                    for m in range(MT + 1):
                        if m < MT:
                            turn_qk(m)
                        if m:
                            attend(m - 1, 1)
                        if m + 1 < MT:
                            project(m + 1)
                        if m < MT:
                            scores(m, 0)
                            scan_inputs(2 * m)
                        if m:
                            turn_o(m - 1)
                            oT_fill_check(m - 1, ring[0])
                        if m < MT:
                            scores(m, 1)
                            scan_inputs(2 * m + 1)
                            attend(m, 0)
                    pe.wait_ge(a_be.sem, a_be.at(it, RING))
                    for r in range(MT):
                        ins = pe.matmul(bank[3][:, :], wo[:, r], oT[:, r], start=(r == 0), stop=(r == MT - 1))
                    ins.then_inc(a_of.sem, 1)
                meet(pe, "pe", l * 3 + 4)
                wait_alone(pe, f_zero.sem, f_zero.at(l, 1))
                with pe.Fori(0, NB) as b:
                    it = pe.snap(l * NB + b)
                    pe.wait_ge(f_hc.sem, f_hc.at(it, 1))
                    pe.wait_ge(f_nm.sem, it)
                    for m in range(MT):
                        ins = pe.transpose(bank[0][:, m * P:(m + 1) * P], f_h[:, 0, m * P:(m + 1) * P], ident[:])
                    ins.then_inc(f_tf.sem, 1)
                    pe.wait_ge(f_nm.sem, f_nm.at(it, 1))
                    pe.wait_ge(f_ne.sem, f_ne.at(it, 0))
                    for m in range(MT):
                        ins = pe.transpose(bank[1][:, m * P:(m + 1) * P], f_hn[:, m], ident[:])
                    ins.then_inc(f_nt.sem, 1)
                    pe.wait_ge(f_ne.sem, f_ne.at(it, 1))
                    for j in range(FT):
                        pe.wait_ge(f_ac.sem, f_ac.at(it, j - 1) if j >= 2 else f_ac.at(it - 1, FT - (1 if j else 0)))
                        pe.matmul(bank[2 + 2 * (j % 2)][:, :], w1s[:, 0, j * P:(j + 1) * P], f_hnT[:, 0], start=True, stop=True)
                        pe.matmul(bank[3 + 2 * (j % 2)][:, :], w1s[:, 1, j * P:(j + 1) * P], f_hnT[:, 0], start=True, stop=True).then_inc(f_up.sem, 1)
                    for j in range(FT):
                        pe.wait_ge(f_ac.sem, f_ac.at(it, j + 1))
                        if j == 0:
                            pe.wait_ge(f_ad.sem, f_ad.at(it, 0))
                        ins = pe.matmul(bank[6][:, :], w2[:, j], f_act[:, j], start=(j == 0), stop=(j == FT - 1))
                    ins.then_inc(f_dn.sem, 1)
                meet(pe, "pe", l * 3 + 5)
            pe.wait_ge(s_w2nd, 16 * len(second_list))
            for t in range(3):
                pe.transpose(bank[0][:, t * P:(t + 1) * P], inp_raw[:, t], ident[:])
            pe.transpose(bank[1][:, 0:P], outp_raw, ident[:])
            pe.transpose(bank[2][:, 0:EXP], rout_raw[0:EXP], ident[0:EXP, 0:EXP]).then_inc(q_t, 1)
            for k in range(3):
                for j in range(KT):
                    n = k * KT + j
                    pe.matmul(bank[5][:, n:n + 1], w_up[:, k, j * P:(j + 1) * P], cols[:, R_B:R_B + 1], start=True, stop=True)
            for e in range(EXP):
                for f in range(2):
                    n = 3 * KT + 2 * e + f
                    pe.matmul(bank[5][:, n:n + 1], m_up[:, e, f * P:(f + 1) * P], cols[:, R_N2B:R_N2B + 1], start=True, stop=True)
            pe.wait_ge(q_wide, 1)
            pe.wait_ge(q_tc, 1)
            pe.matmul(bank[6][:, 0:3 * P], n1b_wide, inpT, start=True, stop=True)
            pe.matmul(bank[7][:, 0:EXP], n2b_wide, routT, start=True, stop=True).then_inc(q_prod, 1)
            meet(pe, "pe", 9)
            for c in (l_sgt, l_zt, l_ff, e_t1, e_yf):
                pe.sem_inc(c.sem, c.per)
            with pe.Fori(0, NB) as b:
                pe.wait_ge(l_sg.sem, l_sg.at(b, 1))
                pe.wait_ge(l_x1.sem, l_x1.at(b - 1, 1))
                for m in range(MT):
                    ins = pe.transpose(bank[0][:, m * P:(m + 1) * P], sg[:, m * P:(m + 1) * P], ident[:])
                ins.then_inc(l_sgt.sem, 1)
            with pe.Fori(0, NB) as b:
                def up(k, j, src):
                    n = k * KT + j
                    pe.wait_ge(l_ue.sem, l_ue.at(b, n - 1) if n >= 2 else l_ue.at(b - 1, 3 * KT - 1 + n))
                    pe.matmul(bank[4 + n % 2][:, :], w_up[:, k, j * P:(j + 1) * P], src, start=True, stop=True).then_inc(l_uf.sem, 1)

                pe.wait_ge(l_z.sem, l_z.at(b, 1))
                pe.wait_ge(l_so.sem, l_so.at(b - 1, 1))
                for m in range(MT):
                    ins = pe.transpose(bank[1][:, m * P:(m + 1) * P], z_tok[:, m], ident[:])
                ins.then_inc(l_zt.sem, 1)
                pe.wait_ge(l_zc.sem, l_zc.at(b, 1))
                for m in range(MT):
                    pe.wait_ge(l_re.sem, l_re.at(b, m - 1) if m >= 2 else l_re.at(b - 1, 2 * MT - 1 + m))
                    pe.matmul(bank[2 + m % 2][:, 0:3 * P], zT[:, m * P:(m + 1) * P], inpT, start=True, stop=True).then_inc(l_rf.sem, 1)
                for k in range(2):
                    for j in range(KT):
                        up(k, j, zT)
                    pe.wait_ge(l_we.sem, l_we.at(b, k))
                    for j in range(KT):
                        pe.wait_ge(l_ue.sem, l_ue.at(b, k * KT + j + 1))
                        ins = pe.matmul(bank[6][:, :], w_dn[:, k, j], hid[:, k, j], start=(j == 0), stop=(j == KT - 1))
                    ins.then_inc(l_wf.sem, 1)
                pe.wait_ge(l_we.sem, l_we.at(b, 2))
                for j in range(MT):
                    n = MT + j
                    pe.wait_ge(l_re.sem, l_re.at(b, n - 1))
                    pe.matmul(bank[2 + n % 2][:, 0:(MT - j) * P], wT[:, 1, j * P:(j + 1) * P], wT[:, 0, j * P:], start=True, stop=True).then_inc(l_rf.sem, 1)
                pe.wait_ge(l_n.sem, l_n.at(b, 1))
                pe.wait_ge(l_re.sem, l_re.at(b, 2 * MT))
                for i in range(MT):
                    for j in range(i + 1):
                        ins = pe.matmul(bank[7][:, i * P:(i + 1) * P], w3[:, j, (i - j) * P:(i - j + 1) * P], n_tok[:, j], start=(j == 0), stop=(j == i))
                ins.then_inc(l_tf.sem, 1)
                pe.wait_ge(l_z2.sem, l_z2.at(b, 1))
                for m in range(MT):
                    ins = pe.transpose(bank[0][:, m * P:(m + 1) * P], z2[:, m], ident[:])
                ins.then_inc(l_z2t.sem, 1)
                pe.wait_ge(l_z2c.sem, l_z2c.at(b, 1))
                for j in range(KT):
                    up(2, j, z2T)
                pe.wait_ge(l_ue.sem, l_ue.at(b, 3 * KT))
                for m in range(MT):
                    for j in range(KT):
                        ins = pe.matmul(bank[1][:, m * P:(m + 1) * P], hid[:, 0, j, m * P:(m + 1) * P], w_dn[:, 2, j], start=(j == 0), stop=(j == KT - 1))
                ins.then_inc(l_ff.sem, 1)
            meet(pe, "pe", 10)
            meet(pe, "pe", 11)
            with pe.Fori(0, MT * 2) as g:
                pe.wait_ge(e_ld.sem, e_ld.at(g, 1))
                pe.wait_ge(e_c2.sem, e_c2.at(g - 1, 1))
                for i in range(MT):
                    ins = pe.transpose(bank[0][:, i * P:(i + 1) * P], e_att[:, i], ident[:])
                ins.then_inc(e_t1.sem, 1)
                pe.wait_ge(e_c1.sem, e_c1.at(g, 1))
                for i in range(MT):
                    ins = pe.matmul(bank[1][:, i * P:(i + 1) * P], e_attT[:, i * P:(i + 1) * P], outpT, start=True, stop=True)
                ins.then_inc(e_pf.sem, 1)
                pe.wait_ge(e_zd.sem, e_zd.at(g, 1))
                for i in range(MT):
                    ins = pe.transpose(bank[0][:, i * P:(i + 1) * P], e_z[:, i], ident[:])
                ins.then_inc(e_t2.sem, 1)
                pe.wait_ge(e_c2.sem, e_c2.at(g, 1))
                for i in range(MT):
                    ins = pe.matmul(bank[2][:, i * EXP:(i + 1) * EXP], e_zT[:, i * P:(i + 1) * P], routT, start=True, stop=True)
                ins.then_inc(e_rf.sem, 1)

                def e_up(e):
                    for f in range(2):
                        n = 2 * e + f
                        pe.wait_ge(e_ue.sem, e_ue.at(g, n - 1) if n >= 2 else e_ue.at(g - 1, 2 * EXP - 1 + n))
                        pe.matmul(bank[4 + n % 2][:, :], m_up[:, e, f * P:(f + 1) * P], e_zT, start=True, stop=True).then_inc(e_uf.sem, 1)

                def e_down(e):
                    pe.wait_ge(e_ue.sem, e_ue.at(g, 2 * e + 2))
                    pe.wait_ge(e_ya.sem, e_ya.at(g, e - 1) if e >= 2 else e_ya.at(g - 1, EXP - 1 + e))
                    for i in range(MT):
                        for f in range(2):
                            ins = pe.matmul(bank[6 + e % 2][:, i * P:(i + 1) * P], e_hid[:, e % 2, f, i * P:(i + 1) * P], m_dn[:, e, f], start=(f == 0), stop=(f == 1))
                    ins.then_inc(e_yf.sem, 1)

                for e in range(EXP + 1):
                    if e < EXP:
                        e_up(e)
                    if e:
                        e_down(e - 1)
            meet(pe, "pe", 12)


def rotary_tables():
    import numpy as np
    half = np.arange(0, HD, 2, dtype=np.float64)
    freqs = np.arange(SEQ)[:, None] * (1.0 / 10000.0 ** (half / HD))[None]
    base = (half + 0.4 * HD) / (1.4 * HD)
    scale = base[None] ** ((np.arange(SEQ) - SEQ // 2) / float(WIN // 2))[:, None]
    two = lambda a, b: np.concatenate([a, b], axis=-1)
    cos, sin, scale = two(np.cos(freqs), np.cos(freqs)), two(-np.sin(freqs), np.sin(freqs)), two(scale, scale)
    return np.stack([8.0 * cos * scale, 8.0 * sin * scale, cos / scale, sin / scale]).astype(np.float32)


_INS = ["L0_attn_x", "L0_attn_W", "L0_attn_b", "L0_attn_A", "L0_attn_D", "L0_ffn_wqkv", "L0_ffn_q_scale", "L0_ffn_k_scale",
        "L0_ffn_wo", "L0_ffn_ln_g", "L0_ffn_ln_b", "L0_ffn_w1", "L0_ffn_b1", "L0_ffn_w2", "L0_ffn_b2", "L1_attn_ln_g", "L1_attn_ln_b",
        "L1_attn_h1_w1", "L1_attn_h1_b1", "L1_attn_h1_w2", "L1_attn_h1_b2", "L1_attn_h2_w1", "L1_attn_h2_b1", "L1_attn_h2_w2",
        "L1_attn_h2_b2", "L1_attn_fm_w1", "L1_attn_fm_b1", "L1_attn_fm_w2", "L1_attn_fm_b2", "L1_ffn_ln1_w", "L1_ffn_ln1_b",
        "L1_ffn_in_proj_w", "L1_ffn_in_proj_b", "L1_ffn_out_proj_w", "L1_ffn_out_proj_b", "L1_ffn_ln2_w", "L1_ffn_ln2_b",
        "L1_ffn_router_w", "L1_ffn_w1", "L1_ffn_w2"]


def kernel(**inputs):
    import numpy as np
    import concourse.bacc as bacc
    from concourse.bass_utils import run_bass_kernel_spmd as run

    nc = bacc.Bacc("TRN2", target_bir_lowering=False, num_devices=1)
    arrays, aps = {}, {}
    given = {name: np.ascontiguousarray(inputs[name]) for name in _INS} | {"rotary": rotary_tables()}
    for name, a in given.items():
        arrays[f"in_{name}"] = a
        aps[name] = nc.dram_tensor(f"in_{name}", a.shape, mybir.dt.from_np(a.dtype), kind="ExternalInput").ap()
    out = nc.dram_tensor("out_0", (NB, SEQ, P), F32, kind="ExternalOutput").ap()
    build(nc, aps, out)
    return run(nc, [arrays], core_ids=[0]).results[0]["out_0"]
```

```python
from contextlib import ExitStack

import concourse.bass as bass
from concourse import mybir

F32 = mybir.dt.float32
BF16 = mybir.dt.bfloat16
ALU = mybir.AluOpType
ACT = mybir.ActivationFunctionType
AX = mybir.AxisListType

P = 128
NB, SEQ = 8, 512
MT = SEQ // P
LAYERS = 2
NS = 16
NSH = NS // LAYERS
HEADS, HD, WIN = 8, 64, 64
PAIRS = HEADS // 2
KEYS = 2 * WIN + WIN
HID = 341
FT = 3
DI = 512
KT = DI // P
EXP, FF = 8, 256
EPS = 1e-5
MASKED = -1e30
TOK = NB * SEQ
SCRATCH = 24000

R_BU, R_BD, R_D = 0, 1, 2
R_LAYER = 3
L_COLS = 2 * FT + 3
R_G, R_B = R_LAYER + LAYERS * L_COLS, R_LAYER + LAYERS * L_COLS + 1
R_H1B1, R_H1B2 = R_B + 1, R_B + 1 + KT
R_H2B1, R_H2B2 = R_H1B2 + 1, R_H1B2 + 1 + KT
R_FMB1 = R_H2B2 + 1
R_N1W, R_N1B, R_N2W, R_N2B = (R_FMB1 + KT + i for i in range(4))
N_ROWS = R_N2B + 1


class Count:

    def __init__(self, sem, per, ahead=False, base=0):
        self.sem, self.per, self.ahead, self.base = sem, per, int(ahead), base

    def at(self, turn, n):
        return (turn + self.ahead) * self.per + n + self.base

    def again(self, turns, per, ahead=False):
        return Count(self.sem, per, ahead, self.at(turns, 0))


def build(nc, I, out):
    with ExitStack() as ctx:
        def sb(name, shape, dt=F32):
            return ctx.enter_context(nc.sbuf_tensor(name, shape, dt))

        def sem(name):
            return ctx.enter_context(nc.semaphore(name))

        def count(name, per, ahead=False):
            return Count(sem(name), per, ahead)

        big = sb("big", [P, 6 * TOK])
        xt0 = big[:, 0:TOK]
        state = big[:, TOK:2 * TOK]
        u_all = big[:, 2 * TOK:3 * TOK]
        delta = big[:, 3 * TOK:4 * TOK]
        y_all = big[:, 4 * TOK:5 * TOK]
        x_tok = y_all
        work = big[:, 5 * TOK:6 * TOK]
        ident = sb("ident", [P, P])
        identb = sb("identb", [P, P], BF16)
        maskb = sb("maskb", [P, 2, KEYS], BF16)
        rows = sb("rows", [N_ROWS, P])
        cols = sb("cols", [P, N_ROWS])
        rot_raw = sb("rot_raw", [P, 4, MT, HD])
        abc_all = sb("abc_all", [P, 3, NS])
        upper = sb("upper", [P, P])
        before = sb("before", [P, EXP, EXP])
        pow_half = sb("pow_half", [P, NB * MT])

        scratch = sb("scratch", [P, SCRATCH])

        class Cut:
            def __init__(self):
                self.at = 0

            def __call__(self, *shape):
                n = 1
                for s in shape:
                    n *= s
                a = scratch[:, self.at:self.at + n]
                self.at += n
                assert self.at <= SCRATCH, self.at
                if len(shape) == 1:
                    return a
                names = " ".join(f"d{i}" for i in range(len(shape)))
                return a.rearrange(f"p ({names}) -> p {names}", **{f"d{i}": s for i, s in enumerate(shape)})

        bank = [ctx.enter_context(nc.psum_tensor(f"bank{i}", [P, 512], F32)) for i in range(8)]

        cut = Cut()
        wud_raw = cut(2, P)
        wud = cut(2, P)
        x_mv = cut(NB * MT, 2)
        x_stats = cut(2, 6)
        x_var = cut(NB * MT)
        x_rstd = cut(NB * MT)
        xn = cut(2, MT, P)
        cut = Cut()
        wbc_raw = cut(2, NSH, P)
        wbc = cut(2, NSH, P)
        abc = cut(3, NSH)
        lcol = cut(L_COLS)
        wqkv = cut(3, HEADS * HD)
        wo = cut(MT, P)
        w1 = cut(2, FT * P)
        w1s = cut(2, FT * P)
        w2 = cut(FT, P)
        b1s = cut(2 * FT)
        qk_scale = cut(2, HD)
        rot = cut(4, MT, HD)
        layer_end = cut.at
        hpad = cut(WIN + SEQ)
        squares = cut(2, HEADS * HD)
        sumsq = cut(2, 2 * HEADS)
        rnorm = cut(2, 2 * HEADS)
        sumsq_c = cut(2 * HEADS)
        k_n = cut(HEADS * HD)
        rot_q = cut(2, HEADS * HD)
        rot_k = cut(2, HEADS * HD)
        qT = cut(PAIRS, P)
        kT = cut(PAIRS, WIN + SEQ)
        vals = cut(MT + 1, 2, PAIRS, HD)
        edge = cut(MT, PAIRS, 2, HD)
        probs = cut(PAIRS, 2 * KEYS)
        probsT = cut(2, 2 * KEYS)
        wcut = [0]

        def wk(*shape):
            n = 1
            for s in shape:
                n *= s
            a = work[:, wcut[0]:wcut[0] + n]
            wcut[0] += n
            assert wcut[0] <= TOK
            if len(shape) == 1:
                return a
            names = " ".join(f"d{i}" for i in range(len(shape)))
            return a.rearrange(f"p ({names}) -> p {names}", **{f"d{i}": s for i, s in enumerate(shape)})

        mx = wk(HEADS)
        negmax = wk(HEADS)
        rowsum = wk(HEADS)
        rinv = wk(HEADS)
        o_tok = wk(HEADS * HD)
        oT = sb("oT", [P, MT, SEQ])
        abar = wk(2, SEQ)
        bu = wk(SEQ)
        hs = wk(SEQ)
        ch = wk(2, SEQ)
        cut.at = layer_end
        f_stats = cut(MT, 6)
        f_mv = cut(MT, 2)
        f_var = cut(MT)
        f_rstd = cut(MT)
        f_h = cut(SEQ)
        f_hn = cut(MT, P)
        f_hnT = cut(SEQ)
        f_gelu = cut(2, SEQ)
        f_act = cut(FT, SEQ)

        x1 = state
        xn1 = xt0
        qkv = big[:, 2 * TOK:5 * TOK].rearrange("p (m s c) -> p m s c", m=MT, s=NB)
        s_out = work
        cut = Cut()
        w_up = cut(3, DI)
        w_dn = cut(3, KT, P)
        inp_raw = cut(3, P)
        inpT = cut(3 * P)
        outp_raw = cut(P)
        outpT = cut(P)
        rout_raw = cut(P)
        routT = cut(EXP)
        m_up = cut(EXP, FF)
        m_dn = cut(EXP, 2, P)
        up_bias = cut(3 * KT + 2 * EXP)
        g_row, b_row, fm_b2_row, out_b_row = (cut(P) for _ in range(4))
        in_b_row = cut(3 * P)
        rout_b_row = cut(EXP)
        n1b_wide, n2b_wide = cut(P), cut(P)
        second_end = cut.at
        sg = cut(SEQ)
        l_stats = cut(2, MT, 6)
        l_mv = cut(2, MT, 2)
        l_var = cut(2, MT)
        l_rstd = cut(2, MT)
        z_tok = cut(MT, P)
        n_tok = cut(MT, P)
        n_scaled = cut(MT, P)
        zT = cut(SEQ)
        hid = cut(2, KT, SEQ)
        wT = cut(2, SEQ)
        w3 = cut(MT, SEQ)
        t_gelu = cut(MT, P)
        t_norm = cut(MT, P)
        t_gain = cut(MT, P)
        xn_b = cut(MT, P)
        xn_f = cut(MT, P)
        x_mid = cut(MT, P)
        z2 = cut(MT, P)
        z2T = cut(SEQ)
        cut.at = second_end
        prod = cut(NB * (NB + 1) // 2 * P)
        sc = cut(NB, NB, 16)
        pr = cut(NB, NB, 16)
        smax = cut(NB, 16)
        ssum = cut(NB, 16)
        sinv = cut(NB, 16)
        att = pr.rearrange("p s t h -> p s (t h)")
        sc_d = sc
        e_att = cut(MT, P)
        e_attT = cut(SEQ)
        e_in = cut(MT, P)
        e_acc = cut(2, MT, P)
        e_stats = cut(MT, 6)
        e_mv = cut(MT, 2)
        e_var = cut(MT)
        e_rstd = cut(MT)
        e_z = cut(MT, P)
        e_zT = cut(2, SEQ)
        lg = cut(MT, EXP)
        lmax = cut(MT)
        lsum = cut(MT)
        linv = cut(MT)
        pexp = cut(MT, EXP)
        prob = cut(MT, EXP)
        above = cut(MT, EXP, EXP)
        equal = cut(MT, EXP, EXP)
        rank = cut(MT, EXP)
        gates = cut(2, MT, EXP)
        e_hid = cut(2, 2, SEQ)
        cut.at = second_end
        fin = cut(2, NB, P)
        fo = cut(2, NB, P)

        s_x, s_rows, s_wud, s_tab, s_zero = (sem(n) for n in ("x_loaded", "rows_loaded", "wud_loaded", "tables_loaded", "rows_zeroed"))
        s_memset, s_const = sem("pool_memset"), sem("constants_made")
        s_cols_t, s_cols, s_wud_t, s_wud_c = sem("cols_turned"), sem("cols_copied"), sem("wud_turned"), sem("wud_copied")
        s_xstat, s_xvar, s_xrstd = sem("x_stats_done"), sem("x_var_done"), sem("x_rstd_done")
        met = {e: sem(f"{e}_met") for e in ("pe", "act", "dve", "pool", "sp")}

        def meet(eng, name, nth):
            eng.drain().then_inc(met[name], 1)
            for other in met:
                if other != name:
                    eng.wait_ge(met[other], nth)
            eng.sem_inc(passed, 1)

        passed = sem("waits_passed")

        def wait_alone(eng, semaphore, value):
            eng.wait_ge(semaphore, value)
            eng.sem_inc(passed, 1)

        c_xn = count("xn_ready", 1)
        c_xT_t = count("xT_turned", 1, True)
        c_xT = count("xT_copied", 1, True)
        c_ups = count("u_psum", 1)
        c_u = count("u_done", 1, True)
        c_dps = count("delta_psum", 1)
        c_dabs = count("delta_abs", 1)
        c_drelu = count("delta_relu", 1, True)
        c_st0 = count("state_copied", 1)
        c_dln = count("delta_ln", 1)
        s_dlt, s_y0, s_kz = sem("delta_done"), sem("y_started"), sem("pads_zeroed")

        s_lw = sem("layer_weights_loaded")
        NLW = 7
        p_wt = count("wbc_turned", 4, True)
        p_wc = count("wbc_copied", 4, True)
        p_lc = count("layer_columns", 2)
        p_rot = count("rot_scaled", 6)
        p_w1s = count("w1_scaled", 1)
        p_b1p = count("b1_product", 1)
        p_b1s = count("b1_scaled", 1)

        TU, SU = MT, NSH
        a_h = count("h_ready", 1)
        a_proj = count("proj_filled", TU, True)
        a_sq = count("squares_done", TU, True)
        a_ss = count("sumsq_done", TU, True)
        a_ssc = count("sumsq_clipped", TU)
        a_rn = count("rnorm_done", TU)
        a_kn = count("k_normed", TU)
        a_rq = count("q_rotated", TU)
        a_rk = count("k_rotated", TU, True)
        a_qkt = count("qkT_filled", TU, True)
        a_qke = count("qkT_copied", TU, True)
        a_edge = count("edge_values_copied", 2)
        a_sim = count("sim_filled", 2 * TU)
        a_max = count("max_done", 2 * TU)
        a_neg = count("negmax_done", 2 * TU)
        a_exp = count("exp_done", 2 * TU, True)
        RING = MT + 1 + TU * PAIRS + TU
        TAIL = 3
        a_bf = count("turn_bank_filled", RING)
        a_be = count("turn_bank_emptied", RING, True)
        a_of = count("o_bank_filled", TU + 1)
        a_oe = count("o_bank_emptied", TU + 1, True)
        a_ri = count("rinv_done", TU)
        c_bps = count("b_filled", SU)
        c_cps = count("c_filled", SU)
        c_ab = count("abar_done", SU)
        c_bu = count("bu_done", SU, True)
        c_sc = count("scan_done", SU, True)
        c_ch = count("ch_done", SU, True)
        c_ya = count("y_added", SU, True)

        f_hc = count("f_h_ready", 1, True)
        f_zero = count("f_h_padded", 1)
        f_tf = count("f_h_turned", 1, True)
        f_st = count("aggr_done", 1, True)
        f_st2 = count("stats_done", 1)
        f_vr = count("var_done", 1)
        f_rs = count("rstd_done", 1)
        f_nm = count("f_normed", 1, True)
        f_nt = count("norm_turned", 1, True)
        f_ne = count("norm_turned_copied", 1, True)
        f_up = count("up_filled", FT)
        f_ge = count("gelu_done", FT, True)
        f_ac = count("f_act_done", FT, True)
        f_dn = count("f_down_filled", 1, True)
        f_ad = count("f_added", 1, True)

        x_view = I["L0_attn_x"].rearrange("b (m p) d -> p b m d", p=P)

        s_xr = sem("x_reloaded")
        s_w2nd = sem("second_weights_loaded")
        s_silu = sem("gate_silu_done")
        q_t, q_tc, q_wide, q_prod, q_pre, q_row = (sem(n) for n in ("projections_turned", "projections_copied", "norm_bias_widened", "bias_products", "biases_added", "weights_scaled"))
        l_sg = count("sg_ready", 1)
        l_sgt = count("sg_turned", 1, True)
        l_x1 = count("x1_done", 1, True)
        x_bn, x_ag, x_vr, x_rs = (c.again(LAYERS * NB, 1) for c in (f_st2, f_st, f_vr, f_rs))
        z_bn, z_ag, z_vr, z_rs = (c.again(NB, 1) for c in (x_bn, x_ag, x_vr, x_rs))
        l_bn = count("mid_stats_done", 2)
        l_ag = count("mid_aggr_done", 2)
        l_vr = count("mid_var_done", 2)
        l_rs = count("mid_rstd_done", 2)
        l_xn = count("xn1_done", 1)
        l_z = count("z_done", 1)
        l_zt = f_nt.again(LAYERS * NB, 1, True)
        l_zc = f_ne.again(LAYERS * NB, 1)
        l_ns = count("n_scaled", 1)
        l_n = count("n_done", 1)
        l_xb = count("xn_b_done", 1)
        l_xf = count("xn_f_done", 1)
        l_rf = count("two_bank_filled", 2 * MT)
        l_re = count("two_bank_emptied", 2 * MT, True)
        l_uf = f_up.again(LAYERS * NB, 3 * KT)
        l_ue = f_ge.again(LAYERS * NB, 3 * KT, True)
        l_wf = count("w_filled", 2)
        l_we = count("w_copied", 2, True)
        l_tf = count("t_filled", 1, True)
        l_tg = count("t_gelu_done", 1, True)
        l_tn = count("t_normed", 1)
        l_ta = count("t_gained", 1)
        l_xm = count("x_mid_done", 1, True)
        l_z2 = count("z2_done", 1)
        l_z2t = count("z2_turned", 1)
        l_z2c = count("z2T_copied", 1, True)
        l_ff = count("fm_filled", 1, True)
        l_so = count("s_out_done", 1, True)
        h_pd = count("h_products", NB)
        h_sc = count("h_scores", 1)
        h_mx = count("h_max", 1)
        h_sb = count("h_sub", 1)
        h_ex = count("h_exp", 1)
        h_sm = count("h_sum", 1)
        h_iv = count("h_inv", 1)
        h_pv = count("h_weighted", NB)
        h_at = count("h_att", 1)
        h_dn = count("h_done", 1, True)
        s_pads = sem("score_pads_set")
        e_ld = count("e_att_staged", 1)
        e_t1 = count("e_att_turned", 1, True)
        e_c1 = count("e_attT_copied", 1)
        e_ib = count("e_in_done", 1)
        e_pf = count("e_proj_filled", 1)
        e_x1 = count("e_x_done", 1)
        e_bn = z_bn.again(NB, 1)
        e_ag = z_ag.again(NB, 1)
        e_vr = z_vr.again(NB, 1)
        e_rs = z_rs.again(NB, 1)
        e_zd = l_z.again(NB, 1)
        e_t2 = l_zt.again(NB, 1)
        e_c2 = l_zc.again(NB, 1, True)
        e_rf = count("e_router_filled", 1)
        e_lg = count("e_logits", 2)
        e_sh = count("e_shifted", 1)
        e_ex = count("e_exp", 1)
        e_sm = count("e_sum", 2)
        e_pr = count("e_prob", 1)
        e_cm = count("e_compared", 4)
        e_rk = count("e_ranked", 1)
        e_gt = count("e_gates", 1)
        e_uf = l_uf.again(NB, 2 * EXP)
        e_ue = l_ue.again(NB, 2 * EXP, True)
        e_yf = count("e_y_filled", EXP, True)
        e_ya = count("e_y_added", EXP, True)
        e_st = count("e_stored", 1, True)
        STEP = (1, 3)
        QK_SUMS = {0: range(0, 3), 1: range(3, 5), 2: range(5, 6), 3: range(6, NB)}
        PV_SUMS = {6: range(0, 5), 7: range(5, NB)}
        z_si = count("z_silu_done", 1)
        z_pr = count("z_product_done", 1, True)
        z_fo = count("z_final_done", 1)
        z_dm = [sem("z_stored_even"), sem("z_stored_odd")]

        row_list = [(R_BU, I["L0_attn_b"][0:2 * P]), (R_D, I["L0_attn_D"])]
        for l in range(LAYERS):
            r = R_LAYER + l * L_COLS
            row_list += [(r, I["L0_ffn_b1"][l, 0:HID]), (r + FT, I["L0_ffn_b1"][l, HID:2 * HID]), (r + 2 * FT, I["L0_ffn_b2"][l]),
                         (r + 2 * FT + 1, I["L0_ffn_ln_g"][l]), (r + 2 * FT + 2, I["L0_ffn_ln_b"][l])]
        row_list += [(r, I["L1_" + name]) for r, name in (
            (R_G, "attn_ln_g"), (R_B, "attn_ln_b"), (R_H1B1, "attn_h1_b1"), (R_H1B2, "attn_h1_b2"), (R_H2B1, "attn_h2_b1"),
            (R_H2B2, "attn_h2_b2"), (R_FMB1, "attn_fm_b1"), (R_N1W, "ffn_ln1_w"), (R_N1B, "ffn_ln1_b"), (R_N2W, "ffn_ln2_w"),
            (R_N2B, "ffn_ln2_b"))]
        n_row_dmas = sum((ap.shape[0] >= P) + (ap.shape[0] % P > 0) for _, ap in row_list)
        second_list = [(w_up[:, k], I[f"L1_attn_{n}_w1"]) for k, n in enumerate(("h1", "h2", "fm"))]
        second_list += [(w_dn[:, k], I[f"L1_attn_{n}_w2"].rearrange("(t p) n -> p t n", p=P)) for k, n in enumerate(("h1", "h2", "fm"))]
        second_list += [
            (inp_raw, I["L1_ffn_in_proj_w"].rearrange("(t p) k -> p t k", p=P)), (outp_raw, I["L1_ffn_out_proj_w"]),
            (rout_raw[0:EXP], I["L1_ffn_router_w"]), (m_up, I["L1_ffn_w1"].rearrange("e p f -> p e f")),
            (m_dn, I["L1_ffn_w2"].rearrange("e (f p) n -> p e f n", p=P)),
            (g_row, I["L1_attn_ln_g"].unsqueeze(0).to_broadcast([P, P])), (b_row, I["L1_attn_ln_b"].unsqueeze(0).to_broadcast([P, P])),
            (fm_b2_row, I["L1_attn_fm_b2"].unsqueeze(0).to_broadcast([P, P])), (out_b_row, I["L1_ffn_out_proj_b"].unsqueeze(0).to_broadcast([P, P])),
            (in_b_row, I["L1_ffn_in_proj_b"].unsqueeze(0).to_broadcast([P, 3 * P]))]

        def qkv_b(b, m):
            return qkv[:, m, bass.ds(b, 1)].rearrange("p s c -> p (s c)")

        def batch(a, b):
            return a[:, bass.ds(b * SEQ, SEQ)]

        def split(a, **k):
            return a.rearrange("p (m d) -> p m d", d=P)

        block = ctx.enter_context(nc.Block())

        @block.sync
        def _(sp):
            xt = x_tok.rearrange("p (b m d) -> p b m d", b=NB, m=MT)
            for b in range(0, NB, 2):
                for h in range(2):
                    sp.dma_start(xt[:, b + h], x_view[:, b + h]).then_inc(s_x, 16)
            sp.dma_start(wud_raw, I["L0_attn_W"][0:2 * P].rearrange("(t p) k -> p t k", p=P)).then_inc(s_wud, 16)
            sp.wait_ge(s_zero, 1)

            def load_row(r, ap):
                full = ap.shape[0] // P
                if full:
                    sp.dma_start(rows[r:r + full, :], ap[0:full * P].rearrange("(t p) -> t p", p=P)).then_inc(s_rows, 16)
                if ap.shape[0] % P:
                    sp.dma_start(rows[r + full:r + full + 1, 0:ap.shape[0] % P], ap[full * P:ap.shape[0]].unsqueeze(0)).then_inc(s_rows, 16)

            for r, ap in row_list:
                load_row(r, ap)
            sp.dma_start(rot_raw[:], I["rotary"].rearrange("k (m p) d -> p k m d", p=P)).then_inc(s_tab, 16)
            bc0 = 2 * P + P * NS
            for i, src in enumerate((I["L0_attn_A"], I["L0_attn_b"][2 * P:bc0].rearrange("(d s) -> d s", s=NS),
                                     I["L0_attn_b"][bc0:bc0 + P * NS].rearrange("(d s) -> d s", s=NS))):
                sp.dma_start(abc_all[:, i], src).then_inc(s_tab, 16)
            meet(sp, "sp", 1)
            meet(sp, "sp", 2)
            with sp.Fori(0, LAYERS) as l:
                lay = bass.ds(l, 1)
                wbc_v = I["L0_attn_W"][2 * P:2 * P + 2 * P * NS].rearrange("(h d s) k -> d h s k", h=2, s=NS)
                for h in range(2):
                    sp.dma_start(wbc_raw[:, h], wbc_v[:, h, bass.ds(l * NSH, NSH)]).then_inc(s_lw, 16)
                sp.dma_start(wqkv, I["L0_ffn_wqkv"][lay].rearrange("a p (c n) -> p (a c) n", c=3)).then_inc(s_lw, 16)
                sp.dma_start(wo, I["L0_ffn_wo"][lay].rearrange("a (t p) n -> p (a t) n", p=P)).then_inc(s_lw, 16)
                sp.dma_start(w1[:, :, 0:HID], I["L0_ffn_w1"][lay].rearrange("a p (c n) -> p (a c) n", c=2)).then_inc(s_lw, 16)
                sp.dma_start(w2[:, 0:FT - 1], I["L0_ffn_w2"][lay, 0:(FT - 1) * P].rearrange("a (t p) n -> p (a t) n", p=P)).then_inc(s_lw, 16)
                sp.dma_start(w2[0:HID - (FT - 1) * P, FT - 1], I["L0_ffn_w2"][lay, (FT - 1) * P:HID].rearrange("a p n -> p (a n)")).then_inc(s_lw, 16)
                for i, nm in enumerate(("q", "k")):
                    sp.dma_start(qk_scale[:, i], I[f"L0_ffn_{nm}_scale"][lay].to_broadcast([P, HD])).then_inc(s_lw, 16)
                for k in range(3):
                    meet(sp, "sp", l * 3 + 3 + k)
            for b in range(NB):
                sp.dma_start(xn1.rearrange("p (b m d) -> p b m d", b=NB, m=MT)[:, b], x_view[:, b]).then_inc(s_xr, 16)
            for dst, src in second_list:
                sp.dma_start(dst, src).then_inc(s_w2nd, 16)
            for k in range(3):
                meet(sp, "sp", 9 + k)
            out_v = out.rearrange("b (m p) d -> p m b d", p=P)
            for m in range(MT):
                sp.wait_ge(z_fo.sem, z_fo.at(m, 1))
                sp.dma_start(out_v[:, m], fo[:, m % 2]).then_inc(z_dm[m % 2], 16)
            for s in z_dm:
                sp.wait_ge(s, 16 * MT // 2)

        @block.gpsimd
        def _(pool):
            pool.memset(ident[:], 0.0).then_inc(s_memset, 1)
            pool.memset(identb[:], 0.0).then_inc(s_memset, 1)
            pool.memset(maskb[:], 0.0).then_inc(s_memset, 1)
            pool.memset(pow_half[:], -0.5).then_inc(s_memset, 1)
            pool.memset(w1, 0.0).then_inc(s_memset, 1)
            pool.wait_ge(s_memset, 5)
            pool.memset(w2[HD:P, FT - 1], 0.0).then_inc(s_memset, 1)
            pool.wait_ge(s_memset, 6)
            for t in (ident, identb):
                pool.affine_select(out=t[:], in_=t[:], compare_op=ALU.not_equal, fill=1.0, base=0,
                                   pattern=[[-1, P]], channel_multiplier=1).then_inc(s_const, 1)
            n = 2
            for kind in range(2):
                for base, step, mult in ((0, 1, -1), (WIN, -1, 1), (-WIN, 1, 0))[:2 + kind]:
                    pool.wait_ge(s_const, n)
                    pool.affine_select(out=maskb[:, kind], in_=maskb[:, kind], compare_op=ALU.is_ge, fill=MASKED,
                                       base=base, pattern=[[step, KEYS]], channel_multiplier=mult).then_inc(s_const, 1)
                    n += 1
            pool.memset(upper[:], 1.0).then_inc(s_memset, 1)
            pool.memset(before[:], 0.0).then_inc(s_memset, 1)
            pool.wait_ge(s_memset, 8)
            pool.affine_select(out=upper[:], in_=upper[:], compare_op=ALU.is_ge, fill=0.0, base=0,
                               pattern=[[1, P]], channel_multiplier=-1).then_inc(s_const, 1)
            for e in range(1, EXP):
                pool.memset(before[:, e, 0:e], 1.0).then_inc(s_const, 1)
            wait_alone(pool, s_xstat, NB * MT)
            pool.tensor_scalar(x_var, x_mv[:, :, 1], EPS, 1.0, ALU.add, ALU.mult).then_inc(s_xvar, 1)
            pool.wait_ge(s_xvar, 1)
            pool.tensor_tensor(x_rstd, x_var, pow_half[:], ALU.pow).then_inc(s_xrstd, 1)
            with pool.Fori(0, NB) as b:
                wait_alone(pool, c_xT.sem, c_xT.at(b, 1))
                pool.tensor_copy(batch(state, b), batch(xt0, b)).then_inc(c_st0.sem, 1)
            meet(pool, "pool", 1)
            meet(pool, "pool", 2)
            for c in (a_rk, c_ya, e_st):
                pool.sem_inc(c.sem, c.per)
            with pool.Fori(0, LAYERS) as l:
                pool.memset(hpad[:, 0:WIN + 1], 0.0)
                pool.memset(kT[:, :, 0:WIN], 0.0)
                pool.memset(edge, 0.0)
                meet(pool, "pool", l * 3 + 3)

                def rsqrt(it, m):
                    par = m % 2
                    if m >= 1:
                        pool.wait_ge(a_rn.sem, a_rn.at(it, m))
                    wait_alone(pool, a_ss.sem, a_ss.at(it, m + 1))
                    pool.tensor_scalar(sumsq_c, sumsq[:, par], 1e-24, 1.0, ALU.max, ALU.mult).then_inc(a_ssc.sem, 1)
                    pool.wait_ge(a_ssc.sem, a_ssc.at(it, m + 1))
                    pool.wait_ge(a_exp.sem, a_exp.at(it, 2 * (m - 1)))
                    pool.tensor_tensor(rnorm[:, par], sumsq_c, pow_half[:, 0:2 * HEADS], ALU.pow).then_inc(a_rn.sem, 1)

                def rotate_k(it, m):
                    t = m % MT
                    pool.wait_ge(a_kn.sem, a_kn.at(it, m + 1))
                    pool.wait_ge(a_qkt.sem, a_qkt.at(it, m))
                    kn = k_n.rearrange("p (h d) -> p h d", d=HD)
                    o = rot_k.rearrange("p a (h d) -> p a h d", d=HD)
                    H2 = HD // 2
                    pool.tensor_tensor(o[:, 0], kn, rot[:, 2, t].unsqueeze(1).to_broadcast([P, HEADS, HD]), ALU.mult)
                    pool.tensor_tensor(o[:, 1, :, 0:H2], kn[:, :, H2:HD], rot[:, 3, t, 0:H2].unsqueeze(1).to_broadcast([P, HEADS, H2]), ALU.mult)
                    pool.tensor_tensor(o[:, 1, :, H2:HD], kn[:, :, 0:H2], rot[:, 3, t, H2:HD].unsqueeze(1).to_broadcast([P, HEADS, H2]), ALU.mult).then_inc(a_rk.sem, 1)

                def start(it):
                    rsqrt(it, 0)
                    rotate_k(it, 0)

                def turn(b, it, prev, nxt):
                    def add_y(s):
                        pool.wait_ge(c_ch.sem, c_ch.at(it, s + 1))
                        wait_alone(pool, c_ya.sem, c_ya.at(it, s))
                        pool.tensor_tensor(batch(y_all, b), batch(y_all, b), ch[:, s % 2], ALU.add).then_inc(c_ya.sem, 1)

                    for m in range(MT):
                        if m + 1 < MT or nxt:
                            rsqrt(it, m + 1)
                            rotate_k(it, m + 1)
                        add_y(2 * m)
                        add_y(2 * m + 1)

                it0 = pool.snap(l * NB)
                start(it0)
                turn(0, it0, False, True)
                with pool.Fori(1, NB - 1) as b:
                    turn(b, pool.snap(l * NB + b), True, True)
                it_last = pool.snap(l * NB + NB - 1)
                turn(NB - 1, it_last, True, False)
                meet(pool, "pool", l * 3 + 4)
                with pool.Fori(0, NB) as b:
                    it = pool.snap(l * NB + b)
                    wait_alone(pool, f_st.sem, f_st.at(it, 1))
                    pool.tensor_scalar(f_var, f_mv[:, :, 1], EPS, 1.0, ALU.add, ALU.mult).then_inc(f_vr.sem, 1)
                    pool.wait_ge(f_vr.sem, f_vr.at(it, 1))
                    pool.tensor_tensor(f_rstd, f_var, pow_half[:, 0:MT], ALU.pow).then_inc(f_rs.sem, 1)
                meet(pool, "pool", l * 3 + 5)
            meet(pool, "pool", 9)

            def rstd(b, k, ag, vr, rs):
                i = 1 if ag is z_ag else 0
                wait_alone(pool, ag.sem, ag.at(b, k + 1))
                pool.tensor_scalar(l_var[:, i], l_mv[:, i, :, 1], EPS, 1.0, ALU.add, ALU.mult).then_inc(vr.sem, 1)
                pool.wait_ge(vr.sem, vr.at(b, k + 1))
                pool.tensor_tensor(l_rstd[:, i], l_var[:, i], pow_half[:, 0:MT], ALU.pow).then_inc(rs.sem, 1)

            with pool.Fori(0, NB) as b:
                rstd(b, 0, x_ag, x_vr, x_rs)

            def scale_n(b, n):
                pool.wait_ge(l_z.sem, l_z.at(b, n + 1))
                if n:
                    pool.wait_ge(l_n.sem, l_n.at(b, n))
                pool.tensor_tensor(n_scaled, z_tok, g_row.unsqueeze(1).to_broadcast([P, MT, P]), ALU.mult).then_inc(l_ns.sem, 1)

            def l1_turn(b, prev, nxt):
                wait_alone(pool, l_ns.sem, l_ns.at(b, 1))
                wait_alone(pool, l_tf.sem, l_tf.at(b, 0))
                pool.tensor_tensor(n_tok, n_scaled, b_row.unsqueeze(1).to_broadcast([P, MT, P]), ALU.add).then_inc(l_n.sem, 1)
                if nxt:
                    rstd(b, 1, z_ag, z_vr, z_rs)
                if prev:
                    rstd(b, -2, l_ag, l_vr, l_rs)
                    rstd(b, -1, l_ag, l_vr, l_rs)
                if nxt:
                    scale_n(b, 1)
                xb = xn1[:, bass.ds(b * SEQ, SEQ)].rearrange("p (m d) -> p m d", m=MT)
                wait_alone(pool, l_xm.sem, l_xm.at(b, 0))
                pool.tensor_tensor(xn_b, xb, b_row.unsqueeze(1).to_broadcast([P, MT, P]), ALU.add).then_inc(l_xb.sem, 1)
                wait_alone(pool, l_so.sem, l_so.at(b, 0))
                pool.tensor_tensor(xn_f, xb, fm_b2_row.unsqueeze(1).to_broadcast([P, MT, P]), ALU.add).then_inc(l_xf.sem, 1)

            rstd(0, 0, z_ag, z_vr, z_rs)
            scale_n(0, 0)
            l1_turn(0, False, True)
            with pool.Fori(1, NB - 1) as b:
                l1_turn(b, True, True)
            l1_turn(NB - 1, True, False)
            rstd(NB, -2, l_ag, l_vr, l_rs)
            rstd(NB, -1, l_ag, l_vr, l_rs)
            meet(pool, "pool", 10)
            pool.memset(sc, MASKED).then_inc(s_pads, 1)

            def products_qk(m, states):
                for s in states:
                    q = qkv[:, bass.ds(m, 1), s, 0:P].to_broadcast([P, s + 1, P])
                    k = qkv[:, bass.ds(m, 1), 0:s + 1, P:2 * P].rearrange("p a s c -> p (a s) c")
                    at = s * (s + 1) // 2 * P
                    if s == 0:
                        wait_alone(pool, h_dn.sem, h_dn.at(m, 0))
                    pool.tensor_tensor(prod[:, at:at + (s + 1) * P].rearrange("p (t c) -> p t c", c=P), q, k, ALU.mult).then_inc(h_pd.sem, 1)

            def products_pv(m):
                wait_alone(pool, h_ex.sem, h_ex.at(m, 1))
                for s in range(NB):
                    v = qkv[:, bass.ds(m, 1), 0:s + 1, 2 * P:3 * P].rearrange("p a s (h d) -> p (a s) h d", d=8)
                    w = pr[:, s, 0:s + 1].unsqueeze(3).to_broadcast([P, s + 1, 16, 8])
                    at = s * (s + 1) // 2 * P
                    pool.tensor_tensor(prod[:, at:at + (s + 1) * P].rearrange("p (t h d) -> p t h d", h=16, d=8), w, v, ALU.mult).then_inc(h_pv.sem, 1)

            def stage(g, m, h, first=False):
                wait_alone(pool, e_t1.sem, e_t1.at(g - 1, 1))
                wait_alone(pool, h_dn.sem, h_dn.at(m, 1))
                pool.tensor_copy(e_att, qkv[:, bass.ds(m, 1), bass.ds(h * 4, 4), 0:P].rearrange("p a s c -> p (a s) c")).then_inc(e_ld.sem, 1)
                xs = xn1.rearrange("p (s m c) -> p m s c", s=NB, m=MT)[:, bass.ds(m, 1), bass.ds(h * 4, 4)].rearrange("p a s c -> p (a s) c")
                if not first:
                    wait_alone(pool, e_x1.sem, e_x1.at(g - 1, 1))
                pool.tensor_tensor(e_in, xs, out_b_row.unsqueeze(1).to_broadcast([P, MT, P]), ALU.add).then_inc(e_ib.sem, 1)

            def e_rstd_of(g):
                wait_alone(pool, e_ag.sem, e_ag.at(g, 1))
                pool.tensor_scalar(e_var, e_mv[:, :, 1], EPS, 1.0, ALU.add, ALU.mult).then_inc(e_vr.sem, 1)
                pool.wait_ge(e_vr.sem, e_vr.at(g, 1))
                pool.tensor_tensor(e_rstd, e_var, pow_half[:, 0:MT], ALU.pow).then_inc(e_rs.sem, 1)

            def store(g, m, h):
                wait_alone(pool, e_ya.sem, e_ya.at(g, EXP))
                pool.tensor_copy(qkv[:, bass.ds(m, 1), bass.ds(h * 4, 4), P:2 * P].rearrange("p a s c -> p (a s) c"), e_acc[:, h]).then_inc(e_st.sem, 1)

            def two_groups(m, nxt):
                g = m * 2
                stage(g + 1, m, 1)
                if nxt:
                    products_qk(m + 1, range(5))
                e_rstd_of(g + 1)
                if nxt:
                    products_qk(m + 1, range(5, NB))
                    products_pv(m + 1)
                store(g, m, 0)
                if nxt:
                    stage(g + 2, m + 1, 0)
                    e_rstd_of(g + 2)
                store(g + 1, m, 1)

            products_qk(0, range(NB))
            products_pv(0)
            stage(0, 0, 0, True)
            e_rstd_of(0)
            with pool.Fori(0, MT - 1) as m:
                two_groups(m, True)
            two_groups(MT - 1, False)
            meet(pool, "pool", 11)

        @block.scalar
        def _(act):
            act.wait_ge(s_cols_t, 1)
            act.activation(cols[:], bank[7][:, 0:N_ROWS], ACT.Copy).then_inc(s_cols, 1)
            act.wait_ge(s_wud_t, 1)
            act.activation(wud.rearrange("p t k -> p (t k)"), bank[6][:, 0:2 * P], ACT.Copy).then_inc(s_wud_c, 1)
            act.wait_ge(s_cols, 1)
            for c in (c_xT, c_u, c_drelu):
                act.sem_inc(c.sem, c.per)
            with act.Fori(0, NB) as b:
                wait_alone(act, c_xT_t.sem, c_xT_t.at(b, 1))
                act.activation(batch(xt0, b), bank[0][:, :], ACT.Copy).then_inc(c_xT.sem, 1)
                wait_alone(act, c_ups.sem, c_ups.at(b, 1))
                act.activation(batch(u_all, b), bank[1][:, :], ACT.Identity, bias=cols[:, R_BU:R_BU + 1]).then_inc(c_u.sem, 1)
                act.wait_ge(c_dps.sem, c_dps.at(b, 1))
                act.activation(batch(delta, b), bank[2][:, :], ACT.Abs, bias=cols[:, R_BD:R_BD + 1]).then_inc(c_dabs.sem, 1)
                act.activation(batch(y_all, b), bank[2][:, :], ACT.Relu, bias=cols[:, R_BD:R_BD + 1]).then_inc(c_drelu.sem, 1)
                wait_alone(act, c_dabs.sem, c_dabs.at(b, 1))
                act.activation(batch(delta, b), batch(delta, b), ACT.Exp, scale=-1.0)
            meet(act, "act", 1)
            with act.Fori(0, NB) as b:
                act.activation(batch(delta, b), batch(delta, b), ACT.Ln, bias=1.0).then_inc(c_dln.sem, 1)
            meet(act, "act", 2)
            for c in (p_wc, a_sq, a_qke, a_exp, a_be, f_ne, f_ge):
                act.sem_inc(c.sem, c.per)
            with act.Fori(0, LAYERS) as l:
                for k in range(4):
                    act.wait_ge(p_wt.sem, p_wt.at(l, k + 1))
                    act.activation(wbc.rearrange("p h s k -> p (h s k)")[:, k * 512:(k + 1) * 512], bank[k][:, :], ACT.Copy).then_inc(p_wc.sem, 1)
                meet(act, "act", l * 3 + 3)

                def square(it, m):
                    act.wait_ge(a_proj.sem, a_proj.at(it, m + 1))
                    act.wait_ge(a_ss.sem, a_ss.at(it, m))
                    act.activation(squares[:, 0], bank[0][:, :], ACT.Square)
                    act.activation(squares[:, 1], bank[1][:, :], ACT.Square).then_inc(a_sq.sem, 1)

                def from_turn_bank(it, ring, out_ap, in_ap, last=True):
                    act.wait_ge(a_bf.sem, a_bf.at(it, ring[0] + 1))
                    ins = act.activation(out_ap, in_ap, ACT.Copy)
                    if last:
                        ins.then_inc(a_be.sem, 1)
                        ring[0] += 1

                def copy_probs(it, ring, pair):
                    from_turn_bank(it, ring, probsT[:, pair % 2], bank[2][:, 0:2 * KEYS])

                def copy_oT(it, ring, m):
                    m %= MT
                    from_turn_bank(it, ring, oT[:, :, m * P:(m + 1) * P], bank[2][:, :].rearrange("p (r t) -> p r t", t=P))

                def start(it):
                    square(it, 0)

                def turn(b, it, prev, nxt):
                    ring = [-TAIL if prev else 0]

                    def copy_qk(m):
                        act.wait_ge(a_qkt.sem, a_qkt.at(it, m + 1))
                        act.activation(qT.rearrange("p r t -> p (r t)"), bank[0][:, :], ACT.Copy)
                        act.activation(kT[:, :, WIN + m * P:WIN + (m + 1) * P], bank[1][:, :].rearrange("p (r t) -> p r t", t=P), ACT.Copy).then_inc(a_qke.sem, 1)

                    def decay(s):
                        wait_alone(act, c_sc.sem, c_sc.at(it, s - 1))
                        act.activation(abar[:, s % 2], batch(delta, b), ACT.Exp, scale=abc[:, 0, s:s + 1]).then_inc(c_ab.sem, 1)

                    def softmax(m, step):
                        act.wait_ge(a_neg.sem, a_neg.at(it, 2 * m + step + 1))
                        for j in range(2):
                            for eo in range(2):
                                pair = 2 * step + j
                                h = 2 * pair + eo
                                ins = act.activation(probs[:, pair, eo * KEYS:(eo + 1) * KEYS], bank[4 + eo][:, j * KEYS:(j + 1) * KEYS], ACT.Exp,
                                                     scale=rnorm[:, m % 2, h:h + 1], bias=negmax[:, h:h + 1], accum_out=rowsum[:, h:h + 1])
                        ins.then_inc(a_exp.sem, 1)

                    def values(i):
                        if i == 0:
                            from_turn_bank(it, ring, vals[:, 0, 0].rearrange("p r d -> p (r d)"), bank[2][:, 0:256])
                        elif i < MT:
                            from_turn_bank(it, ring, vals[:, i].rearrange("p e r d -> p (e r d)"), bank[2][:, :])
                        else:
                            from_turn_bank(it, ring, vals[0:HD, MT, 0].rearrange("p r d -> p (r d)"), bank[2][0:HD, 0:256], last=False)
                            from_turn_bank(it, ring, vals[:, MT, 1].rearrange("p r d -> p (r d)"), bank[2][:, 256:512])

                    for m in range(MT):
                        behind = m or prev
                        copy_qk(m)
                        if behind:
                            copy_probs(it, ring, 2)
                        decay(2 * m)
                        if m + 1 < MT or nxt:
                            square(it, m + 1)
                        if behind:
                            copy_probs(it, ring, 3)
                        if m == 0:
                            values(0)
                        softmax(m, 0)
                        decay(2 * m + 1)
                        if behind:
                            copy_oT(it, ring, m - 1)
                        if m == 0:
                            for i in range(1, MT + 1):
                                values(i)
                        copy_probs(it, ring, 0)
                        softmax(m, 1)
                        copy_probs(it, ring, 1)

                it0 = act.snap(l * NB)
                start(it0)
                turn(0, it0, False, True)
                with act.Fori(1, NB - 1) as b:
                    turn(b, act.snap(l * NB + b), True, True)
                it_last = act.snap(l * NB + NB - 1)
                turn(NB - 1, it_last, True, False)
                ring = [MT * PAIRS + 2 * MT + 1 - TAIL]
                copy_probs(it_last, ring, 2)
                copy_probs(it_last, ring, 3)
                copy_oT(it_last, ring, MT - 1)
                meet(act, "act", l * 3 + 4)

                def copy_normed(it, n):
                    act.wait_ge(f_nt.sem, f_nt.at(it, n + 1))
                    act.activation(f_hnT, bank[1][:, :], ACT.Copy).then_inc(f_ne.sem, 1)

                def ffn(b, it, nxt):
                    for j in range(FT):
                        act.wait_ge(f_up.sem, f_up.at(it, j + 1))
                        act.wait_ge(f_ac.sem, f_ac.at(it, j - 1))
                        act.activation(f_gelu[:, j % 2], bank[3 + 2 * (j % 2)][:, :], ACT.Gelu, bias=b1s[:, FT + j:FT + j + 1]).then_inc(f_ge.sem, 1)
                    if nxt:
                        copy_normed(it, 1)

                it_first = act.snap(l * NB)
                copy_normed(it_first, 0)
                with act.Fori(0, NB - 1) as b:
                    ffn(b, act.snap(l * NB + b), True)
                it_last = act.snap(l * NB + NB - 1)
                ffn(NB - 1, it_last, False)
                meet(act, "act", l * 3 + 5)
            with act.Fori(0, NB) as b:
                act.activation(batch(state, b), batch(state, b), ACT.Silu).then_inc(s_silu, 1)
            act.wait_ge(q_t, 1)
            act.activation(inpT, bank[0][:, 0:3 * P], ACT.Copy)
            act.activation(outpT, bank[1][:, 0:P], ACT.Copy)
            act.activation(routT, bank[2][:, 0:EXP], ACT.Copy).then_inc(q_tc, 1)
            meet(act, "act", 9)
            for c in (l_ue, l_we, l_tg, l_z2c):
                act.sem_inc(c.sem, c.per)

            def gelu_up(b, n, k, j):
                act.wait_ge(l_uf.sem, l_uf.at(b, n + 1))
                act.activation(hid[:, k % 2, j], bank[4 + n % 2][:, :], ACT.Gelu, bias=up_bias[:, k * KT + j:k * KT + j + 1]).then_inc(l_ue.sem, 1)

            def copy_z(b, n):
                act.wait_ge(l_zt.sem, l_zt.at(b, n + 1))
                act.activation(zT, bank[0][:, :], ACT.Copy).then_inc(l_zc.sem, 1)

            def gelu_t(b):
                act.wait_ge(l_tf.sem, l_tf.at(b, 0))
                act.activation(t_gelu.rearrange("p m d -> p (m d)"), bank[7][:, :], ACT.Gelu).then_inc(l_tg.sem, 1)

            def last_mlp(b, n):
                act.wait_ge(l_z2t.sem, l_z2t.at(b, 0))
                act.activation(z2T, bank[1][:, :], ACT.Copy).then_inc(l_z2c.sem, 1)
                for j in range(KT):
                    gelu_up(b, n + j, 2, j)

            def l1_turn(b, prev, nxt):
                first = -KT if prev else 0
                if prev:
                    gelu_t(b)
                for k, r in ((0, R_H1B2), (1, R_H2B2)):
                    for j in range(KT):
                        gelu_up(b, first + k * KT + j, k, j)
                    act.wait_ge(l_wf.sem, l_wf.at(b, k + 1))
                    act.activation(wT[:, k], bank[6][:, :], ACT.Identity, bias=cols[:, r:r + 1]).then_inc(l_we.sem, 1)
                if nxt:
                    copy_z(b, 1)
                if prev:
                    last_mlp(b, first + 2 * KT)

            copy_z(0, 0)
            l1_turn(0, False, True)
            with act.Fori(1, NB - 1) as b:
                l1_turn(b, True, True)
            l1_turn(NB - 1, True, False)
            gelu_t(NB)
            last_mlp(NB, -KT)
            meet(act, "act", 10)
            for c in (e_c2, e_ue):
                act.sem_inc(c.sem, c.per)

            def attention_exp(m):
                act.wait_ge(h_sb.sem, h_sb.at(m, 1))
                act.activation(pr, sc, ACT.Exp, scale=float(8) ** -0.5).then_inc(h_ex.sem, 1)

            def router_exp(g):
                act.wait_ge(e_sh.sem, e_sh.at(g, 1))
                act.activation(pexp, lg, ACT.Exp).then_inc(e_ex.sem, 1)

            def copy_att(g):
                act.wait_ge(e_t1.sem, e_t1.at(g, 1))
                act.activation(e_attT, bank[0][:, :], ACT.Copy).then_inc(e_c1.sem, 1)

            def copy_e_z(g, h):
                act.wait_ge(e_t2.sem, e_t2.at(g, 1))
                act.activation(e_zT[:, h], bank[0][:, :], ACT.Copy).then_inc(e_c2.sem, 1)

            def two_groups(m, nxt):
                for h in range(2):
                    g = m * 2 + h
                    ahead = h == 0 or nxt
                    for e in range(EXP):
                        for f in range(2):
                            n = 2 * e + f
                            act.wait_ge(e_uf.sem, e_uf.at(g, n + 1))
                            if f == 0:
                                act.wait_ge(e_yf.sem, e_yf.at(g, e - 1))
                            act.activation(e_hid[:, e % 2, f], bank[4 + n % 2][:, :], ACT.Gelu, bias=up_bias[:, 3 * KT + n:3 * KT + n + 1]).then_inc(e_ue.sem, 1)
                        if ahead:
                            if e == STEP[h]:
                                copy_att(g + 1)
                            if e == STEP[h] + 3:
                                copy_e_z(g + 1, (h + 1) % 2)
                            if e == min(STEP[h] + 4, EXP - 1):
                                if h == 0 and nxt:
                                    attention_exp(m + 1)
                                router_exp(g + 1)

            attention_exp(0)
            copy_att(0)
            copy_e_z(0, 0)
            router_exp(0)
            with act.Fori(0, MT - 1) as m:
                two_groups(m, True)
            two_groups(MT - 1, False)
            meet(act, "act", 11)
            with act.Fori(0, MT) as m:
                v = qkv[:, bass.ds(m, 1), :, P:2 * P].rearrange("p a s c -> p (a s) c")
                act.activation(v, v, ACT.Silu).then_inc(z_si.sem, 1)

        @block.vector
        def _(dve):
            dve.memset(rows[:], 0.0).then_inc(s_zero, 1)
            dve.wait_ge(s_x, 16 * NB)
            for i in range(NB * MT):
                if i >= 2:
                    dve.wait_ge(s_xstat, i - 1)
                dve.bn_stats(x_stats[:, i % 2], x_tok[:, i * P:(i + 1) * P]).then_inc(c_xn.sem, 1)
                if i >= 1:
                    dve.wait_ge(c_xn.sem, i)
                    dve.bn_aggr(x_mv[:, i - 1], x_stats[:, (i - 1) % 2]).then_inc(s_xstat, 1)
            dve.wait_ge(c_xn.sem, NB * MT)
            dve.bn_aggr(x_mv[:, NB * MT - 1], x_stats[:, 1]).then_inc(s_xstat, 1)
            dve.wait_ge(s_xrstd, 1)
            wait_alone(dve, s_xstat, NB * MT)
            with dve.Fori(0, NB) as b:
                dve.wait_ge(c_xT_t.sem, c_xT_t.at(b - 1, 1))
                for m in range(MT):
                    i = b * MT + m
                    ins = dve.tensor_scalar(xn[:, 0, m], x_tok[:, bass.ds(i * P, P)], x_mv[:, bass.ds(i, 1), 0], x_rstd[:, bass.ds(i, 1)],
                                            ALU.subtract, ALU.mult)
                ins.then_inc(c_xn.sem, 1)
            meet(dve, "dve", 1)
            with dve.Fori(0, NB) as b:
                dve.wait_ge(c_dln.sem, b + 1)
                dve.tensor_tensor(batch(delta, b), batch(delta, b), batch(y_all, b), ALU.add).then_inc(s_dlt, 1)
                dve.wait_ge(s_dlt, b + 1)
                dve.tensor_scalar(batch(y_all, b), batch(u_all, b), cols[:, R_D:R_D + 1], None, ALU.mult).then_inc(s_y0, 1)
            meet(dve, "dve", 2)
            for c in (a_ss, a_oe, c_bu, c_sc, c_ch, f_hc, f_st, f_ac, f_ad, f_nm, h_dn):
                dve.sem_inc(c.sem, c.per)
            with dve.Fori(0, LAYERS) as l:
                dve.wait_ge(s_tab, 16 * 4)
                dve.tensor_copy(abc, abc_all[:, :, bass.ds(l * NSH, NSH)]).then_inc(p_lc.sem, 1)
                dve.tensor_copy(lcol, cols[:, bass.ds(l * L_COLS + R_LAYER, L_COLS)]).then_inc(p_lc.sem, 1)
                dve.wait_ge(p_lc.sem, p_lc.at(l, 2))
                dve.wait_ge(s_lw, l * 144 + 144)
                H2 = HD // 2
                for t in range(4):
                    s = qk_scale[:, t // 2]
                    for a, c in (((0, HD),) if t % 2 == 0 else ((0, H2), (H2, HD))):
                        w = c - a
                        src = a if t % 2 == 0 else (H2 if a == 0 else 0)
                        dve.tensor_tensor(rot[:, t, :, a:c], rot_raw[:, t, :, a:c], s[:, src:src + w].unsqueeze(1).to_broadcast([P, MT, w]),
                                          ALU.mult).then_inc(p_rot.sem, 1)
                dve.tensor_scalar(w1s, w1, lcol[:, 2 * FT + 1:2 * FT + 2], None, ALU.mult).then_inc(p_w1s.sem, 1)
                dve.wait_ge(p_b1p.sem, p_b1p.at(l, 1))
                dve.tensor_tensor(b1s, bank[5][:, 0:2 * FT], lcol[:, 0:2 * FT], ALU.add).then_inc(p_b1s.sem, 1)
                meet(dve, "dve", l * 3 + 3)

                def shift(it, b, n):
                    if n:
                        dve.wait_ge(a_proj.sem, a_proj.at(it, MT))
                    dve.tensor_copy(hpad[0:HD, WIN:WIN + SEQ], state[0:HD, bass.ds((b + n) * SEQ, SEQ)])
                    dve.tensor_copy(hpad[HD:P, WIN + 1:WIN + SEQ], state[HD:P, bass.ds((b + n) * SEQ, SEQ - 1)]).then_inc(a_h.sem, 1)

                def sum_squares(it, m):
                    dve.wait_ge(a_sq.sem, a_sq.at(it, m + 1))
                    dve.tensor_reduce(sumsq[:, m % 2], squares.rearrange("p a (h d) -> p (a h) d", d=HD), AX.X, ALU.add).then_inc(a_ss.sem, 1)

                def rotate(it, m):
                    par, t = m % 2, m % MT
                    dve.wait_ge(a_rn.sem, a_rn.at(it, m + 1))
                    dve.wait_ge(a_rk.sem, a_rk.at(it, m))
                    kb = bank[1][:, :].rearrange("p (h d) -> p h d", d=HD)
                    dve.tensor_tensor(k_n.rearrange("p (h d) -> p h d", d=HD), kb, rnorm[:, par, HEADS:2 * HEADS].unsqueeze(2).to_broadcast([P, HEADS, HD]),
                                      ALU.mult).then_inc(a_kn.sem, 1)
                    dve.wait_ge(a_qkt.sem, a_qkt.at(it, m))
                    qb = bank[0][:, :].rearrange("p (h d) -> p h d", d=HD)
                    o = rot_q.rearrange("p a (h d) -> p a h d", d=HD)
                    dve.tensor_tensor(o[:, 0], qb, rot[:, 0, t].unsqueeze(1).to_broadcast([P, HEADS, HD]), ALU.mult)
                    dve.tensor_tensor(o[:, 1, :, 0:H2], qb[:, :, H2:HD], rot[:, 1, t, 0:H2].unsqueeze(1).to_broadcast([P, HEADS, H2]), ALU.mult)
                    dve.tensor_tensor(o[:, 1, :, H2:HD], qb[:, :, 0:H2], rot[:, 1, t, H2:HD].unsqueeze(1).to_broadcast([P, HEADS, H2]), ALU.mult).then_inc(a_rq.sem, 1)

                def invert_sums(it, m):
                    dve.wait_ge(a_exp.sem, a_exp.at(it, 2 * m + 2))
                    dve.reciprocal(rinv, rowsum).then_inc(a_ri.sem, 1)

                def normalise(it, m):
                    dve.wait_ge(a_ri.sem, a_ri.at(it, m + 1))
                    dve.wait_ge(a_of.sem, a_of.at(it, m + 1 if m >= 0 else -1))
                    dve.tensor_tensor(o_tok.rearrange("p (h d) -> p h d", d=HD), bank[3][:, :].rearrange("p (h d) -> p h d", d=HD),
                                      rinv.unsqueeze(2).to_broadcast([P, HEADS, HD]), ALU.mult).then_inc(a_oe.sem, 1)

                def residual(it, b):
                    dve.wait_ge(a_of.sem, a_of.at(it, 0))
                    at = bass.ds((b - 1) * SEQ, SEQ)
                    dve.tensor_tensor(state[:, at], bank[3][:, :], state[:, at], ALU.add).then_inc(a_oe.sem, 1)

                def start(it):
                    shift(it, 0, 0)
                    sum_squares(it, 0)
                    rotate(it, 0)

                def turn(b, it, prev, nxt):
                    def maxima(m, step):
                        n = 2 * m + step + 1
                        dve.wait_ge(a_sim.sem, a_sim.at(it, n))
                        mxs = mx[:, 4 * step:4 * step + 4].rearrange("p (j e) -> p e j", e=2)
                        for eo in range(2):
                            ins = dve.tensor_reduce(mxs[:, eo], bank[4 + eo][:, 0:2 * KEYS].rearrange("p (j k) -> p j k", k=KEYS), AX.X, ALU.max)
                        ins.then_inc(a_max.sem, 1)
                        dve.wait_ge(a_max.sem, a_max.at(it, n))
                        h4 = slice(4 * step, 4 * step + 4)
                        dve.scalar_tensor_tensor(out=negmax[:, h4], in0=mx[:, h4], scalar=-1.0, in1=rnorm[:, m % 2, h4], op0=ALU.mult, op1=ALU.mult).then_inc(a_neg.sem, 1)

                    def scan_in(s):
                        dve.wait_ge(c_bps.sem, c_bps.at(it, s + 1))
                        dve.wait_ge(c_sc.sem, c_sc.at(it, s))
                        dve.scalar_tensor_tensor(out=bu, in0=bank[6][:, :], scalar=abc[:, 1, s:s + 1], in1=batch(u_all, b), op0=ALU.add, op1=ALU.mult).then_inc(c_bu.sem, 1)

                    def scan(s):
                        dve.wait_ge(c_bu.sem, c_bu.at(it, s + 1))
                        dve.wait_ge(c_ab.sem, c_ab.at(it, s + 1))
                        dve.wait_ge(c_ch.sem, c_ch.at(it, s))
                        dve.tensor_tensor_scan(hs, abar[:, s % 2], bu, 0.0, ALU.mult, ALU.add).then_inc(c_sc.sem, 1)

                    def scan_out(s):
                        dve.wait_ge(c_sc.sem, c_sc.at(it, s + 1))
                        dve.wait_ge(c_cps.sem, c_cps.at(it, s + 1))
                        dve.wait_ge(c_ya.sem, c_ya.at(it, s - 1))
                        dve.scalar_tensor_tensor(out=ch[:, s % 2], in0=bank[7][:, :], scalar=abc[:, 2, s:s + 1], in1=hs, op0=ALU.add, op1=ALU.mult).then_inc(c_ch.sem, 1)

                    values_from = TAIL if prev else 0

                    def edges(part):
                        lo, hi = (0, 2) if part == 0 else (2, MT)
                        dve.wait_ge(a_be.sem, a_be.at(it, 3 if part == 0 else MT + 1))
                        dve.tensor_copy(edge[0:HD, lo:hi, :, 0], vals[0:HD, lo + 1:hi + 1, 0])
                        lo = max(lo, 1)
                        dve.tensor_copy(edge[HD:P, lo:hi, :, 1], vals[HD:P, lo:hi, 1]).then_inc(a_edge.sem, 1)

                    for m in range(MT):
                        behind = m or prev
                        if behind:
                            invert_sums(it, m - 1)
                        scan_in(2 * m)
                        scan(2 * m)
                        if m + 1 < MT or nxt:
                            sum_squares(it, m + 1)
                        maxima(m, 0)
                        scan_out(2 * m)
                        if behind:
                            normalise(it, m - 1)
                        if m == MT - 2 and nxt:
                            shift(it, b, 1)
                        scan_in(2 * m + 1)
                        if m + 1 < MT or nxt:
                            rotate(it, m + 1)
                        scan(2 * m + 1)
                        maxima(m, 1)
                        if m == 0:
                            edges(0)
                            edges(1)
                            if prev:
                                residual(it, b)
                        scan_out(2 * m + 1)

                it0 = dve.snap(l * NB)
                start(it0)
                turn(0, it0, False, True)
                with dve.Fori(1, NB - 1) as b:
                    turn(b, dve.snap(l * NB + b), True, True)
                it_last = dve.snap(l * NB + NB - 1)
                turn(NB - 1, it_last, True, False)
                invert_sums(it_last, MT - 1)
                normalise(it_last, MT - 1)
                it_end = dve.snap(l * NB + NB)
                residual(it_end, NB)
                meet(dve, "dve", l * 3 + 4)
                dve.memset(f_h[HD:P, 0:1], 0.0).then_inc(f_zero.sem, 1)

                def shift_h(it, b, n):
                    dve.wait_ge(f_tf.sem, f_tf.at(it, n))
                    dve.tensor_copy(f_h[0:HD], state[0:HD, bass.ds((b + n) * SEQ, SEQ)])
                    dve.tensor_copy(f_h[HD:P, 1:SEQ], state[HD:P, bass.ds((b + n) * SEQ, SEQ - 1)]).then_inc(f_hc.sem, 1)

                def statistics(it, n):
                    dve.wait_ge(f_tf.sem, f_tf.at(it, n + 1))
                    for m in range(MT):
                        ins = dve.bn_stats(f_stats[:, m], bank[0][:, m * P:(m + 1) * P])
                    ins.then_inc(f_st2.sem, 1)

                def aggregate(it, n):
                    wait_alone(dve, f_st2.sem, f_st2.at(it, n + 1))
                    for m in range(MT):
                        ins = dve.bn_aggr(f_mv[:, m], f_stats[:, m])
                    ins.then_inc(f_st.sem, 1)

                def normed(it, n):
                    dve.wait_ge(f_st.sem, f_st.at(it, n + 1))
                    dve.wait_ge(f_rs.sem, f_rs.at(it, n + 1))
                    dve.wait_ge(f_nt.sem, f_nt.at(it, n))
                    for m in range(MT):
                        ins = dve.tensor_scalar(f_hn[:, m], bank[0][:, m * P:(m + 1) * P], f_mv[:, m, 0:1], f_rstd[:, m:m + 1], ALU.subtract, ALU.mult)
                    ins.then_inc(f_nm.sem, 1)

                def ffn(b, it, nxt):
                    if nxt:
                        shift_h(it, b, 1)
                        statistics(it, 1)
                    for j in range(FT):
                        dve.wait_ge(f_ge.sem, f_ge.at(it, j + 1))
                        if j == 0:
                            dve.wait_ge(f_dn.sem, f_dn.at(it, 0))
                        dve.scalar_tensor_tensor(out=f_act[:, j], in0=bank[2 + 2 * (j % 2)][:, :], scalar=b1s[:, j:j + 1], in1=f_gelu[:, j % 2],
                                                 op0=ALU.add, op1=ALU.mult).then_inc(f_ac.sem, 1)
                        if j == 0 and nxt:
                            aggregate(it, 1)
                        if j == 1 and nxt:
                            normed(it, 1)
                    dve.wait_ge(f_dn.sem, f_dn.at(it, 1))
                    dve.scalar_tensor_tensor(out=batch(state, b), in0=bank[6][:, :], scalar=lcol[:, 2 * FT:2 * FT + 1], in1=batch(state, b),
                                             op0=ALU.add, op1=ALU.add).then_inc(f_ad.sem, 1)

                it_first = dve.snap(l * NB)
                shift_h(it_first, 0, 0)
                statistics(it_first, 0)
                aggregate(it_first, 0)
                normed(it_first, 0)
                with dve.Fori(0, NB - 1) as b:
                    ffn(b, dve.snap(l * NB + b), True)
                it_last = dve.snap(l * NB + NB - 1)
                ffn(NB - 1, it_last, False)
                meet(dve, "dve", l * 3 + 5)
            dve.tensor_copy(n1b_wide, cols[:, R_N1B:R_N1B + 1].to_broadcast([P, P]))
            dve.tensor_copy(n2b_wide, cols[:, R_N2B:R_N2B + 1].to_broadcast([P, P])).then_inc(q_wide, 1)
            dve.wait_ge(q_prod, 1)
            dve.wait_ge(s_w2nd, 16 * len(second_list))
            for k, r in enumerate((R_H1B1, R_H2B1, R_FMB1)):
                dve.tensor_tensor(up_bias[:, k * KT:(k + 1) * KT], bank[5][:, k * KT:(k + 1) * KT], cols[:, r:r + KT], ALU.add)
            dve.tensor_copy(up_bias[:, 3 * KT:], bank[5][:, 3 * KT:3 * KT + 2 * EXP])
            dve.tensor_tensor(in_b_row, bank[6][:, 0:3 * P], in_b_row, ALU.add)
            dve.tensor_copy(rout_b_row, bank[7][:, 0:EXP])
            dve.tensor_scalar(w_up, w_up, cols[:, R_G:R_G + 1], None, ALU.mult)
            dve.tensor_scalar(inpT, inpT, cols[:, R_N1W:R_N1W + 1], None, ALU.mult)
            dve.tensor_scalar(routT, routT, cols[:, R_N2W:R_N2W + 1], None, ALU.mult)
            dve.tensor_scalar(m_up, m_up, cols[:, R_N2W:R_N2W + 1], None, ALU.mult).then_inc(q_row, 1)
            meet(dve, "dve", 9)
            dve.wait_ge(s_xr, 16 * NB)
            for c in (l_x1, l_re, l_so, l_xm, z_pr, e_ya):
                dve.sem_inc(c.sem, c.per)

            def tile_of(a, b):
                return lambda m: a[:, bass.ds(b * SEQ + m * P, P)]

            def statistics(b, k, i, bn, ag, src):
                for m in range(MT):
                    ins = dve.bn_stats(l_stats[:, i, m], src(m))
                ins.then_inc(bn.sem, 1)
                wait_alone(dve, bn.sem, bn.at(b, k + 1))
                for m in range(MT):
                    ins = dve.bn_aggr(l_mv[:, i, m], l_stats[:, i, m])
                ins.then_inc(ag.sem, 1)

            def normed(b, k, i, ag, rs, src, dst, done):
                dve.wait_ge(ag.sem, ag.at(b, k + 1))
                dve.wait_ge(rs.sem, rs.at(b, k + 1))
                for m in range(MT):
                    ins = dve.tensor_scalar(dst(m), src(m), l_mv[:, i, m, 0:1], l_rstd[:, i, m:m + 1], ALU.subtract, ALU.mult)
                ins.then_inc(done.sem, 1)

            with dve.Fori(0, NB) as b:
                dve.wait_ge(l_sgt.sem, l_sgt.at(b - 1, 1))
                dve.tensor_tensor(sg, batch(y_all, b), batch(state, b), ALU.mult).then_inc(l_sg.sem, 1)
                dve.wait_ge(l_sgt.sem, l_sgt.at(b, 1))
                dve.tensor_tensor(batch(x1, b), bank[0][:, :], batch(xn1, b), ALU.add).then_inc(l_x1.sem, 1)
                wait_alone(dve, l_x1.sem, l_x1.at(b, 1))
                statistics(b, 0, 0, x_bn, x_ag, tile_of(x1, b))
                normed(b, 0, 0, x_ag, x_rs, tile_of(x1, b), tile_of(xn1, b), l_xn)
            dve.wait_ge(l_xn.sem, NB)

            def z_statistics(b, n):
                statistics(b, n, 1, z_bn, z_ag, tile_of(xn1, b + n))

            def z_normed(b, n):
                if n:
                    dve.wait_ge(l_ns.sem, l_ns.at(b, 1))
                normed(b, n, 1, z_ag, z_rs, tile_of(xn1, b + n), lambda m: z_tok[:, m], l_z)

            def project_qkv(b, n, first):
                for m in range(MT):
                    dve.wait_ge(l_rf.sem, l_rf.at(b, first + m + 1))
                    dve.tensor_tensor(qkv_b(b + n, m), bank[2 + m % 2][:, 0:3 * P], in_b_row, ALU.add).then_inc(l_re.sem, 1)

            def norm_t(b):
                wait_alone(dve, l_tg.sem, l_tg.at(b, 0))
                statistics(b, -2, 0, l_bn, l_ag, lambda m: t_gelu[:, m])

            def norm_x_mid(b):
                normed(b, -2, 0, l_ag, l_rs, lambda m: t_gelu[:, m], lambda m: t_norm[:, m], l_tn)
                dve.wait_ge(l_tn.sem, l_tn.at(b, 0))
                dve.tensor_tensor(t_gain, t_norm, g_row.unsqueeze(1).to_broadcast([P, MT, P]), ALU.mult).then_inc(l_ta.sem, 1)
                dve.wait_ge(l_ta.sem, l_ta.at(b, 0))
                dve.wait_ge(l_xb.sem, l_xb.at(b, 0))
                dve.tensor_tensor(x_mid, t_gain, xn_b, ALU.add).then_inc(l_xm.sem, 1)
                wait_alone(dve, l_xm.sem, l_xm.at(b, 0))
                statistics(b, -1, 0, l_bn, l_ag, lambda m: x_mid[:, m])
                normed(b, -1, 0, l_ag, l_rs, lambda m: x_mid[:, m], lambda m: z2[:, m], l_z2)

            def finish(b):
                dve.wait_ge(l_ff.sem, l_ff.at(b, 0))
                dve.wait_ge(l_xf.sem, l_xf.at(b, 0))
                dve.tensor_tensor(s_out[:, bass.ds((b - 1) * SEQ, SEQ)], bank[1][:, :], xn_f.rearrange("p m d -> p (m d)"), ALU.add).then_inc(l_so.sem, 1)

            def l1_turn(b, prev, nxt):
                if nxt:
                    z_statistics(b, 1)
                if prev:
                    norm_t(b)
                if nxt:
                    z_normed(b, 1)
                if prev:
                    norm_x_mid(b)
                if nxt:
                    project_qkv(b, 1, MT)
                if prev:
                    finish(b)
                for j in range(MT):
                    n = (2 if nxt else 1) * MT + j
                    dve.wait_ge(l_rf.sem, l_rf.at(b, n + 1))
                    ins = dve.tensor_tensor(w3[:, j, 0:P], bank[2 + n % 2][:, 0:P], upper[:], ALU.mult)
                    if j < MT - 1:
                        ins = dve.tensor_copy(w3[:, j, P:(MT - j) * P], bank[2 + n % 2][:, P:(MT - j) * P])
                    ins.then_inc(l_re.sem, 1)

            z_statistics(0, 0)
            z_normed(0, 0)
            project_qkv(0, 0, 0)
            l1_turn(0, False, True)
            with dve.Fori(1, NB - 1) as b:
                l1_turn(b, True, True)
            l1_turn(NB - 1, True, False)
            norm_t(NB)
            norm_x_mid(NB)
            finish(NB)
            meet(dve, "dve", 10)
            dve.wait_ge(s_pads, 1)

            def sum_qk(m, batches):
                for s in batches:
                    at = s * (s + 1) // 2 * P
                    dve.wait_ge(h_pd.sem, h_pd.at(m, s + 1))
                    ins = dve.tensor_reduce(sc[:, s, 0:s + 1].rearrange("p t h -> p (t h)"), prod[:, at:at + (s + 1) * P].rearrange("p (g d) -> p g d", d=8), AX.X, ALU.add)
                    if s == NB - 1:
                        ins.then_inc(h_sc.sem, 1)

            def score_max(m):
                dve.wait_ge(h_sc.sem, h_sc.at(m, 1))
                dve.tensor_reduce(smax, sc.rearrange("p s t h -> p s h t"), AX.X, ALU.max).then_inc(h_mx.sem, 1)
                dve.wait_ge(h_mx.sem, h_mx.at(m, 1))
                dve.tensor_tensor(sc_d, sc, smax.unsqueeze(2).to_broadcast([P, NB, NB, 16]), ALU.subtract).then_inc(h_sb.sem, 1)

            def score_sum(m):
                dve.wait_ge(h_ex.sem, h_ex.at(m, 1))
                dve.tensor_reduce(ssum, pr.rearrange("p s t h -> p s h t"), AX.X, ALU.add).then_inc(h_sm.sem, 1)
                dve.wait_ge(h_sm.sem, h_sm.at(m, 1))
                dve.reciprocal(sinv, ssum).then_inc(h_iv.sem, 1)

            def sum_pv(m, batches):
                for s in batches:
                    at = s * (s + 1) // 2 * P
                    dve.wait_ge(h_pv.sem, h_pv.at(m, s + 1))
                    ins = dve.tensor_reduce(att[:, s], prod[:, at:at + (s + 1) * P].rearrange("p (t c) -> p c t", c=P), AX.X, ALU.add)
                    if s == NB - 1:
                        ins.then_inc(h_at.sem, 1)

            def attention_out(m):
                dve.wait_ge(h_at.sem, h_at.at(m, 1))
                dve.wait_ge(h_iv.sem, h_iv.at(m, 1))
                dve.tensor_tensor(qkv[:, bass.ds(m, 1), :, 0:P].rearrange("p a s (h d) -> p (a s) h d", d=8), att.rearrange("p s (h d) -> p s h d", d=8),
                                  sinv.unsqueeze(3).to_broadcast([P, NB, 16, 8]), ALU.mult).then_inc(h_dn.sem, 1)

            def project_att(g, h, first=False):
                dve.wait_ge(e_pf.sem, e_pf.at(g, 1))
                dve.wait_ge(e_ib.sem, e_ib.at(g, 1))
                if not first:
                    dve.wait_ge(e_st.sem, e_st.at(g - 2, 1))
                acc = e_acc[:, h]
                dve.tensor_tensor(acc.rearrange("p m d -> p (m d)"), bank[1][:, :], e_in.rearrange("p m d -> p (m d)"), ALU.add).then_inc(e_x1.sem, 1)
                wait_alone(dve, e_x1.sem, e_x1.at(g, 1))
                for i in range(MT):
                    ins = dve.bn_stats(e_stats[:, i], acc[:, i])
                ins.then_inc(e_bn.sem, 1)
                wait_alone(dve, e_bn.sem, e_bn.at(g, 1))
                for i in range(MT):
                    ins = dve.bn_aggr(e_mv[:, i], e_stats[:, i])
                ins.then_inc(e_ag.sem, 1)

            def e_normed(g, h):
                dve.wait_ge(e_ag.sem, e_ag.at(g, 1))
                dve.wait_ge(e_rs.sem, e_rs.at(g, 1))
                for i in range(MT):
                    ins = dve.tensor_scalar(e_z[:, i], e_acc[:, h, i], e_mv[:, i, 0:1], e_rstd[:, i:i + 1], ALU.subtract, ALU.mult)
                ins.then_inc(e_zd.sem, 1)

            def router_logits(g):
                dve.wait_ge(e_rf.sem, e_rf.at(g, 1))
                dve.tensor_tensor(lg, bank[2][:, 0:MT * EXP].rearrange("p (i e) -> p i e", e=EXP), rout_b_row.unsqueeze(1).to_broadcast([P, MT, EXP]), ALU.add).then_inc(e_lg.sem, 1)
                dve.wait_ge(e_lg.sem, e_lg.at(g, 1))
                dve.tensor_reduce(lmax, lg, AX.X, ALU.max).then_inc(e_lg.sem, 1)
                dve.wait_ge(e_lg.sem, e_lg.at(g, 2))
                dve.tensor_tensor(lg, lg, lmax.unsqueeze(2).to_broadcast([P, MT, EXP]), ALU.subtract).then_inc(e_sh.sem, 1)

            def router_gates(g, h):
                dve.wait_ge(e_ex.sem, e_ex.at(g, 1))
                dve.tensor_reduce(lsum, pexp, AX.X, ALU.add).then_inc(e_sm.sem, 1)
                dve.wait_ge(e_sm.sem, e_sm.at(g, 1))
                dve.reciprocal(linv, lsum).then_inc(e_sm.sem, 1)
                dve.wait_ge(e_sm.sem, e_sm.at(g, 2))
                dve.tensor_tensor(prob, pexp, linv.unsqueeze(2).to_broadcast([P, MT, EXP]), ALU.mult).then_inc(e_pr.sem, 1)
                dve.wait_ge(e_pr.sem, e_pr.at(g, 1))
                other = prob.unsqueeze(2).to_broadcast([P, MT, EXP, EXP])
                own = prob.unsqueeze(3).to_broadcast([P, MT, EXP, EXP])
                dve.tensor_tensor(above, other, own, ALU.is_gt).then_inc(e_cm.sem, 1)
                dve.tensor_tensor(equal, other, own, ALU.is_equal).then_inc(e_cm.sem, 1)
                dve.wait_ge(e_cm.sem, e_cm.at(g, 2))
                dve.tensor_tensor(equal, equal, before[:].unsqueeze(1).to_broadcast([P, MT, EXP, EXP]), ALU.mult).then_inc(e_cm.sem, 1)
                dve.wait_ge(e_cm.sem, e_cm.at(g, 3))
                dve.tensor_tensor(above, above, equal, ALU.add).then_inc(e_cm.sem, 1)
                dve.wait_ge(e_cm.sem, e_cm.at(g, 4))
                dve.tensor_reduce(rank, above, AX.X, ALU.add).then_inc(e_rk.sem, 1)
                dve.wait_ge(e_rk.sem, e_rk.at(g, 1))
                dve.scalar_tensor_tensor(out=gates[:, h], in0=rank, scalar=2.0, in1=prob, op0=ALU.is_lt, op1=ALU.mult).then_inc(e_gt.sem, 1)

            def two_groups(m, nxt):
                for h in range(2):
                    g = m * 2 + h
                    ahead = h == 0 or nxt
                    dve.wait_ge(e_gt.sem, e_gt.at(g, 1))
                    for e in range(EXP):
                        dve.wait_ge(e_yf.sem, e_yf.at(g, e + 1))
                        if e:
                            dve.wait_ge(e_ya.sem, e_ya.at(g, e))
                        for i in range(MT):
                            ins = dve.scalar_tensor_tensor(out=e_acc[:, h, i], in0=bank[6 + e % 2][:, i * P:(i + 1) * P], scalar=gates[:, h, i, e:e + 1], in1=e_acc[:, h, i],
                                                           op0=ALU.mult, op1=ALU.add)
                        ins.then_inc(e_ya.sem, 1)
                        if ahead and e == STEP[h]:
                            project_att(g + 1, (h + 1) % 2)
                        if ahead and e == STEP[h] + 1:
                            e_normed(g + 1, (h + 1) % 2)
                        if h == 0 and nxt and e in QK_SUMS:
                            sum_qk(m + 1, QK_SUMS[e])
                            if e == max(QK_SUMS):
                                score_max(m + 1)
                        if ahead and e == STEP[h] + 3:
                            router_logits(g + 1)
                        if ahead and e == min(STEP[h] + 5, EXP - 1):
                            router_gates(g + 1, (h + 1) % 2)
                            if h == 0 and nxt:
                                score_sum(m + 1)
                        if h == 0 and nxt and e in PV_SUMS:
                            sum_pv(m + 1, PV_SUMS[e])
                            if e == max(PV_SUMS):
                                attention_out(m + 1)

            sum_qk(0, range(NB))
            score_max(0)
            score_sum(0)
            sum_pv(0, range(NB))
            attention_out(0)
            project_att(0, 0, True)
            e_normed(0, 0)
            router_logits(0)
            router_gates(0, 0)
            with dve.Fori(0, MT - 1) as m:
                two_groups(m, True)
            two_groups(MT - 1, False)
            meet(dve, "dve", 11)
            for m in range(MT):
                dve.wait_ge(z_si.sem, m + 1)
                if m >= 2:
                    dve.wait_ge(z_dm[m % 2], 16 * (m // 2))
                so = s_out.rearrange("p (s m c) -> p m s c", s=NB, m=MT)[:, m]
                xo = x1.rearrange("p (s m c) -> p m s c", s=NB, m=MT)[:, m]
                dve.tensor_tensor(fin[:, m % 2], so, qkv[:, m, :, P:2 * P], ALU.mult).then_inc(z_pr.sem, 1)
                dve.wait_ge(z_pr.sem, z_pr.at(m, 1))
                dve.tensor_tensor(fo[:, m % 2], fin[:, m % 2], xo, ALU.add).then_inc(z_fo.sem, 1)

        @block.tensor
        def _(pe):
            pe.wait_ge(s_const, 2 + 5)
            pe.wait_ge(s_rows, 16 * n_row_dmas)
            pe.transpose(bank[7][:, 0:N_ROWS], rows[:], ident[0:N_ROWS, 0:N_ROWS]).then_inc(s_cols_t, 1)
            pe.wait_ge(s_wud, 16)
            for t in range(2):
                ins = pe.transpose(bank[6][:, t * P:(t + 1) * P], wud_raw[:, t], ident[:])
            ins.then_inc(s_wud_t, 1)
            pe.wait_ge(s_wud_c, 1)
            pe.sem_inc(c_xT_t.sem, 1)
            with pe.Fori(0, NB) as b:
                pe.wait_ge(c_xn.sem, b + NB * MT + 1)
                pe.wait_ge(c_xT.sem, c_xT.at(b, 0))
                for m in range(MT):
                    ins = pe.transpose(bank[0][:, m * P:(m + 1) * P], xn[:, 0, m], ident[:])
                ins.then_inc(c_xT_t.sem, 1)
                pe.wait_ge(c_xT.sem, c_xT.at(b, 1))
                pe.wait_ge(c_u.sem, c_u.at(b, 0))
                pe.matmul(bank[1][:, :], wud[:, 0], batch(xt0, b), start=True, stop=True).then_inc(c_ups.sem, 1)
                pe.wait_ge(c_drelu.sem, c_drelu.at(b, 0))
                pe.matmul(bank[2][:, :], wud[:, 1], batch(xt0, b), start=True, stop=True).then_inc(c_dps.sem, 1)
            meet(pe, "pe", 1)
            meet(pe, "pe", 2)
            for c in (p_wt, a_proj, a_qkt, f_tf, f_nt, f_dn):
                pe.sem_inc(c.sem, c.per)
            with pe.Fori(0, LAYERS) as l:
                pe.wait_ge(s_lw, l * 144 + 144)
                wr = wbc_raw.rearrange("p h s k -> p (h s) k")
                for i in range(2 * NSH):
                    ins = pe.transpose(bank[i // 4][:, (i % 4) * P:(i % 4 + 1) * P], wr[:, i], ident[:])
                    if i % 4 == 3:
                        ins.then_inc(p_wt.sem, 1)
                pe.wait_ge(p_lc.sem, p_lc.at(l, 2))
                for j in range(2 * FT):
                    ins = pe.matmul(bank[5][:, j:j + 1], w1[:, j // FT, (j % FT) * P:(j % FT + 1) * P], lcol[:, 2 * FT + 2:2 * FT + 3], start=True, stop=True)
                ins.then_inc(p_b1p.sem, 1)
                meet(pe, "pe", l * 3 + 3)

                def turn_bank_free(it, ring):
                    pe.wait_ge(a_be.sem, a_be.at(it, ring[0]))
                    ring[0] += 1

                def project(it, m):
                    t = m % MT
                    pe.wait_ge(a_h.sem, a_h.at(it, m // MT + 1))
                    pe.wait_ge(a_qke.sem, a_qke.at(it, m))
                    lhs = hpad[:, WIN + t * P:WIN + (t + 1) * P]
                    pe.matmul(bank[0][:, :], lhs, wqkv[:, 0], start=True, stop=True)
                    pe.matmul(bank[1][:, :], lhs, wqkv[:, 1], start=True, stop=True).then_inc(a_proj.sem, 1)

                def turn_probs(it, ring, m, pair):
                    if pair % 2 == 0:
                        pe.wait_ge(a_exp.sem, a_exp.at(it, 2 * m + pair // 2 + 1))
                    turn_bank_free(it, ring)
                    for i in range(3):
                        ins = pe.transpose(bank[2][:, i * P:(i + 1) * P], probs[:, pair, i * P:(i + 1) * P], ident[:])
                    ins.then_inc(a_bf.sem, 1)
                    return ring[0]

                def weigh(it, copied, m, pair):
                    t = m % MT
                    pe.wait_ge(a_be.sem, a_be.at(it, copied))
                    if pair == 0 and t % 2 == 0:
                        pe.wait_ge(a_edge.sem, a_edge.at(it, t // 2 + 1))
                    if pair == 0:
                        pe.wait_ge(a_oe.sem, a_oe.at(it, m))
                    pt = probsT[:, pair % 2]
                    o = bank[3][:, pair * P:(pair + 1) * P]
                    pe.matmul(o, pt[:, P:2 * P], edge[:, t, pair], start=True, stop=False)
                    pe.matmul(o[:, 0:HD], pt[:, 0:P], vals[:, t, 0, pair], start=False, stop=False)
                    ins = pe.matmul(o[:, HD:P], pt[:, 2 * P:3 * P], vals[:, t + 1, 1, pair], start=False, stop=True)
                    if pair == PAIRS - 1:
                        ins.then_inc(a_of.sem, 1)

                def turn_o(it, ring, m):
                    pe.wait_ge(a_oe.sem, a_oe.at(it, m + 1 if m >= 0 else -1))
                    turn_bank_free(it, ring)
                    for r in range(MT):
                        ins = pe.transpose(bank[2][:, r * P:(r + 1) * P], o_tok[:, r * P:(r + 1) * P], ident[:])
                    ins.then_inc(a_bf.sem, 1)
                    return ring[0]

                def out_projection(r):
                    ins = pe.matmul(bank[3][:, :], wo[:, r], oT[:, r], start=(r == 0), stop=(r == MT - 1))
                    if r == MT - 1:
                        ins.then_inc(a_of.sem, 1)

                def start(it):
                    project(it, 0)

                def turn(b, it, prev, nxt):
                    ring = [-TAIL if prev else 0]

                    def values(i):
                        turn_bank_free(it, ring)
                        wv = wqkv[:, 2].rearrange("p (r e d) -> p e r d", e=2, d=HD)
                        n = P if i < MT else HD
                        ins = pe.matmul(bank[2][0:n, 0:256], hpad[:, i * P:i * P + n], wv[:, 0], start=True, stop=True)
                        if i:
                            ins = pe.matmul(bank[2][:, 256:512], hpad[:, WIN + (i - 1) * P:WIN + i * P], wv[:, 1], start=True, stop=True)
                        ins.then_inc(a_bf.sem, 1)

                    def turn_qk(m):
                        pe.wait_ge(a_rq.sem, a_rq.at(it, m + 1))
                        pe.wait_ge(a_rk.sem, a_rk.at(it, m + 1))
                        for w, t in enumerate((rot_q, rot_k)):
                            for r in range(PAIRS):
                                for i in range(2):
                                    ins = pe.matmul(bank[w][:, r * P:(r + 1) * P], t[:, i, r * P:(r + 1) * P], ident[:], is_transpose=True, start=(i == 0), stop=(i == 1))
                        ins.then_inc(a_qkt.sem, 1)

                    def scores(m, step):
                        pe.wait_ge(a_qke.sem, a_qke.at(it, m + 1))
                        pe.wait_ge(a_exp.sem, a_exp.at(it, 2 * m + step))
                        mask = maskb[:, 1 if m == 0 else 0].unsqueeze(1).to_broadcast([P, 2, KEYS])
                        for eo in range(2):
                            pe.matmul(bank[4 + eo][:, 0:2 * KEYS], identb[:], mask, start=True, stop=False)
                        for j in range(2):
                            for eo in range(2):
                                ps = slice(eo * HD, (eo + 1) * HD)
                                ins = pe.matmul(bank[4 + eo][:, j * KEYS:(j + 1) * KEYS], qT[ps, 2 * step + j], kT[ps, 2 * step + j, m * P:m * P + KEYS],
                                                start=False, stop=(j == 1))
                        ins.then_inc(a_sim.sem, 1)

                    def scan_b(s):
                        pe.wait_ge(c_bu.sem, c_bu.at(it, s))
                        pe.matmul(bank[6][:, :], wbc[:, 0, s], batch(xt0, b), start=True, stop=True).then_inc(c_bps.sem, 1)

                    def scan_c(s):
                        pe.wait_ge(c_ch.sem, c_ch.at(it, s))
                        pe.matmul(bank[7][:, :], wbc[:, 1, s], batch(xt0, b), start=True, stop=True).then_inc(c_cps.sem, 1)

                    copied = ring[0]
                    for m in range(MT):
                        behind = m or prev
                        turn_qk(m)
                        if behind:
                            weigh(it, copied, m - 1, 1)
                            copied = turn_probs(it, ring, m - 1, 2)
                        scan_b(2 * m)
                        if m + 1 < MT or nxt:
                            project(it, m + 1)
                        scores(m, 0)
                        if behind:
                            weigh(it, copied, m - 1, 2)
                            copied = turn_probs(it, ring, m - 1, 3)
                        scan_c(2 * m)
                        if behind:
                            weigh(it, copied, m - 1, 3)
                        if m == 0:
                            values(0)
                        scan_b(2 * m + 1)
                        if behind:
                            o_turned = turn_o(it, ring, m - 1)
                        scores(m, 1)
                        if m == 0:
                            for i in range(1, MT + 1):
                                values(i)
                                if prev:
                                    if i == 1:
                                        pe.wait_ge(a_be.sem, a_be.at(it, o_turned))
                                    out_projection(i - 1)
                        copied = turn_probs(it, ring, m, 0)
                        scan_c(2 * m + 1)
                        weigh(it, copied, m, 0)
                        copied = turn_probs(it, ring, m, 1)

                it0 = pe.snap(l * NB)
                start(it0)
                turn(0, it0, False, True)
                with pe.Fori(1, NB - 1) as b:
                    turn(b, pe.snap(l * NB + b), True, True)
                it_last = pe.snap(l * NB + NB - 1)
                turn(NB - 1, it_last, True, False)
                it_end = pe.snap(l * NB + NB)
                ring = [-TAIL]
                copied = -TAIL
                for pair in range(1, PAIRS):
                    weigh(it_end, copied, -1, pair)
                    if pair + 1 < PAIRS:
                        copied = turn_probs(it_end, ring, -1, pair + 1)
                o_turned = turn_o(it_end, ring, -1)
                pe.wait_ge(a_be.sem, a_be.at(it_end, o_turned))
                for r in range(MT):
                    out_projection(r)
                meet(pe, "pe", l * 3 + 4)
                pe.wait_ge(f_zero.sem, f_zero.at(l, 1))

                def turn_h(it, n):
                    pe.wait_ge(f_hc.sem, f_hc.at(it, n + 1))
                    pe.wait_ge(f_nm.sem, f_nm.at(it, n))
                    for m in range(MT):
                        ins = pe.transpose(bank[0][:, m * P:(m + 1) * P], f_h[:, m * P:(m + 1) * P], ident[:])
                    ins.then_inc(f_tf.sem, 1)

                def turn_normed(it, n):
                    pe.wait_ge(f_nm.sem, f_nm.at(it, n + 1))
                    pe.wait_ge(f_ne.sem, f_ne.at(it, n))
                    for m in range(MT):
                        ins = pe.transpose(bank[1][:, m * P:(m + 1) * P], f_hn[:, m], ident[:])
                    ins.then_inc(f_nt.sem, 1)

                def ffn(b, it, nxt):
                    pe.wait_ge(f_ne.sem, f_ne.at(it, 1))
                    for j in range(FT):
                        pe.wait_ge(f_ac.sem, f_ac.at(it, j - 1))
                        pe.matmul(bank[2 + 2 * (j % 2)][:, :], w1s[:, 0, j * P:(j + 1) * P], f_hnT, start=True, stop=True)
                        pe.matmul(bank[3 + 2 * (j % 2)][:, :], w1s[:, 1, j * P:(j + 1) * P], f_hnT, start=True, stop=True).then_inc(f_up.sem, 1)
                        if j == 0 and nxt:
                            turn_h(it, 1)
                    for j in range(FT):
                        pe.wait_ge(f_ac.sem, f_ac.at(it, j + 1))
                        if j == 0:
                            pe.wait_ge(f_ad.sem, f_ad.at(it, 0))
                        if j == FT - 1 and nxt:
                            turn_normed(it, 1)
                        ins = pe.matmul(bank[6][:, :], w2[:, j], f_act[:, j], start=(j == 0), stop=(j == FT - 1))
                    ins.then_inc(f_dn.sem, 1)

                it_first = pe.snap(l * NB)
                turn_h(it_first, 0)
                turn_normed(it_first, 0)
                with pe.Fori(0, NB - 1) as b:
                    ffn(b, pe.snap(l * NB + b), True)
                it_last = pe.snap(l * NB + NB - 1)
                ffn(NB - 1, it_last, False)
                meet(pe, "pe", l * 3 + 5)
            pe.wait_ge(s_w2nd, 16 * len(second_list))
            for t in range(3):
                pe.transpose(bank[0][:, t * P:(t + 1) * P], inp_raw[:, t], ident[:])
            pe.transpose(bank[1][:, 0:P], outp_raw, ident[:])
            pe.transpose(bank[2][:, 0:EXP], rout_raw[0:EXP], ident[0:EXP, 0:EXP]).then_inc(q_t, 1)
            for k in range(3):
                for j in range(KT):
                    n = k * KT + j
                    pe.matmul(bank[5][:, n:n + 1], w_up[:, k, j * P:(j + 1) * P], cols[:, R_B:R_B + 1], start=True, stop=True)
            for e in range(EXP):
                for f in range(2):
                    n = 3 * KT + 2 * e + f
                    pe.matmul(bank[5][:, n:n + 1], m_up[:, e, f * P:(f + 1) * P], cols[:, R_N2B:R_N2B + 1], start=True, stop=True)
            pe.wait_ge(q_wide, 1)
            pe.wait_ge(q_tc, 1)
            pe.matmul(bank[6][:, 0:3 * P], n1b_wide, inpT, start=True, stop=True)
            pe.matmul(bank[7][:, 0:EXP], n2b_wide, routT, start=True, stop=True).then_inc(q_prod, 1)
            meet(pe, "pe", 9)
            for c in (l_sgt, l_zt, l_ff, l_tf, e_t1, e_yf):
                pe.sem_inc(c.sem, c.per)
            with pe.Fori(0, NB) as b:
                pe.wait_ge(l_sg.sem, l_sg.at(b, 1))
                pe.wait_ge(l_x1.sem, l_x1.at(b - 1, 1))
                for m in range(MT):
                    ins = pe.transpose(bank[0][:, m * P:(m + 1) * P], sg[:, m * P:(m + 1) * P], ident[:])
                ins.then_inc(l_sgt.sem, 1)

            def up(b, n, k, j, src):
                pe.wait_ge(l_ue.sem, l_ue.at(b, n - 1))
                pe.matmul(bank[4 + n % 2][:, :], w_up[:, k, j * P:(j + 1) * P], src, start=True, stop=True).then_inc(l_uf.sem, 1)

            def turn_z(b, n, first):
                pe.wait_ge(l_z.sem, l_z.at(b, n + 1))
                for m in range(MT):
                    ins = pe.transpose(bank[0][:, m * P:(m + 1) * P], z_tok[:, m], ident[:])
                ins.then_inc(l_zt.sem, 1)
                pe.wait_ge(l_zc.sem, l_zc.at(b, n + 1))
                for m in range(MT):
                    pe.wait_ge(l_re.sem, l_re.at(b, first + m - 1))
                    pe.matmul(bank[2 + m % 2][:, 0:3 * P], zT[:, m * P:(m + 1) * P], inpT, start=True, stop=True).then_inc(l_rf.sem, 1)

            def turn_z2(b):
                pe.wait_ge(l_z2.sem, l_z2.at(b, 0))
                pe.wait_ge(l_so.sem, l_so.at(b, -1))
                for m in range(MT):
                    ins = pe.transpose(bank[1][:, m * P:(m + 1) * P], z2[:, m], ident[:])
                ins.then_inc(l_z2t.sem, 1)

            def last_mlp(b, n):
                pe.wait_ge(l_z2c.sem, l_z2c.at(b, 0))
                for j in range(KT):
                    up(b, n + j, 2, j, z2T)
                pe.wait_ge(l_ue.sem, l_ue.at(b, n + KT))
                for m in range(MT):
                    for j in range(KT):
                        ins = pe.matmul(bank[1][:, m * P:(m + 1) * P], hid[:, 0, j, m * P:(m + 1) * P], w_dn[:, 2, j], start=(j == 0), stop=(j == KT - 1))
                ins.then_inc(l_ff.sem, 1)

            def l1_turn(b, prev, nxt):
                first = -KT if prev else 0
                for k in range(2):
                    for j in range(KT):
                        up(b, first + k * KT + j, k, j, zT)
                    pe.wait_ge(l_we.sem, l_we.at(b, k))
                    for j in range(KT):
                        pe.wait_ge(l_ue.sem, l_ue.at(b, first + k * KT + j + 1))
                        ins = pe.matmul(bank[6][:, :], w_dn[:, k, j], hid[:, k, j], start=(j == 0), stop=(j == KT - 1))
                    ins.then_inc(l_wf.sem, 1)
                if nxt:
                    turn_z(b, 1, MT)
                if prev:
                    turn_z2(b)
                    last_mlp(b, first + 2 * KT)
                pe.wait_ge(l_we.sem, l_we.at(b, 2))
                for j in range(MT):
                    n = (2 if nxt else 1) * MT + j
                    pe.wait_ge(l_re.sem, l_re.at(b, n - 1))
                    pe.matmul(bank[2 + n % 2][:, 0:(MT - j) * P], wT[:, 1, j * P:(j + 1) * P], wT[:, 0, j * P:], start=True, stop=True).then_inc(l_rf.sem, 1)
                pe.wait_ge(l_n.sem, l_n.at(b, 1))
                pe.wait_ge(l_re.sem, l_re.at(b, (3 if nxt else 2) * MT))
                pe.wait_ge(l_tg.sem, l_tg.at(b, 0))
                for i in range(MT):
                    for j in range(i + 1):
                        ins = pe.matmul(bank[7][:, i * P:(i + 1) * P], w3[:, j, (i - j) * P:(i - j + 1) * P], n_tok[:, j], start=(j == 0), stop=(j == i))
                ins.then_inc(l_tf.sem, 1)

            turn_z(0, 0, 0)
            l1_turn(0, False, True)
            with pe.Fori(1, NB - 1) as b:
                l1_turn(b, True, True)
            l1_turn(NB - 1, True, False)
            turn_z2(NB)
            last_mlp(NB, -KT)
            meet(pe, "pe", 10)

            def turn_att(g):
                pe.wait_ge(e_ld.sem, e_ld.at(g, 1))
                pe.wait_ge(e_c2.sem, e_c2.at(g - 1, 1))
                for i in range(MT):
                    ins = pe.transpose(bank[0][:, i * P:(i + 1) * P], e_att[:, i], ident[:])
                ins.then_inc(e_t1.sem, 1)

            def project_att(g):
                pe.wait_ge(e_c1.sem, e_c1.at(g, 1))
                for i in range(MT):
                    ins = pe.matmul(bank[1][:, i * P:(i + 1) * P], e_attT[:, i * P:(i + 1) * P], outpT, start=True, stop=True)
                ins.then_inc(e_pf.sem, 1)

            def turn_e_z(g):
                pe.wait_ge(e_zd.sem, e_zd.at(g, 1))
                for i in range(MT):
                    ins = pe.transpose(bank[0][:, i * P:(i + 1) * P], e_z[:, i], ident[:])
                ins.then_inc(e_t2.sem, 1)

            def route(g, h):
                pe.wait_ge(e_c2.sem, e_c2.at(g, 1))
                for i in range(MT):
                    ins = pe.matmul(bank[2][:, i * EXP:(i + 1) * EXP], e_zT[:, h, i * P:(i + 1) * P], routT, start=True, stop=True)
                ins.then_inc(e_rf.sem, 1)

            def two_groups(m, nxt):
                for h in range(2):
                    g = m * 2 + h
                    ahead = h == 0 or nxt
                    for e in range(EXP + 1):
                        if e < EXP:
                            for f in range(2):
                                n = 2 * e + f
                                pe.wait_ge(e_ue.sem, e_ue.at(g, n - 1))
                                pe.matmul(bank[4 + n % 2][:, :], m_up[:, e, f * P:(f + 1) * P], e_zT[:, h], start=True, stop=True).then_inc(e_uf.sem, 1)
                        if e:
                            pe.wait_ge(e_ue.sem, e_ue.at(g, 2 * e))
                            pe.wait_ge(e_ya.sem, e_ya.at(g, e - 2))
                            for i in range(MT):
                                for f in range(2):
                                    ins = pe.matmul(bank[6 + (e - 1) % 2][:, i * P:(i + 1) * P], e_hid[:, (e - 1) % 2, f, i * P:(i + 1) * P], m_dn[:, e - 1, f],
                                                    start=(f == 0), stop=(f == 1))
                            ins.then_inc(e_yf.sem, 1)
                        if ahead and e == STEP[h]:
                            turn_att(g + 1)
                        if ahead and e == STEP[h] + 1:
                            project_att(g + 1)
                        if ahead and e == STEP[h] + 3:
                            turn_e_z(g + 1)
                        if ahead and e == STEP[h] + 4:
                            route(g + 1, (h + 1) % 2)

            turn_att(0)
            project_att(0)
            turn_e_z(0)
            route(0, 0)
            with pe.Fori(0, MT - 1) as m:
                two_groups(m, True)
            two_groups(MT - 1, False)
            meet(pe, "pe", 11)


def rotary_tables():
    import numpy as np
    half = np.arange(0, HD, 2, dtype=np.float64)
    freqs = np.arange(SEQ)[:, None] * (1.0 / 10000.0 ** (half / HD))[None]
    base = (half + 0.4 * HD) / (1.4 * HD)
    scale = base[None] ** ((np.arange(SEQ) - SEQ // 2) / float(WIN // 2))[:, None]
    two = lambda a, b: np.concatenate([a, b], axis=-1)
    cos, sin, scale = two(np.cos(freqs), np.cos(freqs)), two(-np.sin(freqs), np.sin(freqs)), two(scale, scale)
    return np.stack([8.0 * cos * scale, 8.0 * sin * scale, cos / scale, sin / scale]).astype(np.float32)


_INS = ["L0_attn_x", "L0_attn_W", "L0_attn_b", "L0_attn_A", "L0_attn_D", "L0_ffn_wqkv", "L0_ffn_q_scale", "L0_ffn_k_scale",
        "L0_ffn_wo", "L0_ffn_ln_g", "L0_ffn_ln_b", "L0_ffn_w1", "L0_ffn_b1", "L0_ffn_w2", "L0_ffn_b2", "L1_attn_ln_g", "L1_attn_ln_b",
        "L1_attn_h1_w1", "L1_attn_h1_b1", "L1_attn_h1_w2", "L1_attn_h1_b2", "L1_attn_h2_w1", "L1_attn_h2_b1", "L1_attn_h2_w2",
        "L1_attn_h2_b2", "L1_attn_fm_w1", "L1_attn_fm_b1", "L1_attn_fm_w2", "L1_attn_fm_b2", "L1_ffn_ln1_w", "L1_ffn_ln1_b",
        "L1_ffn_in_proj_w", "L1_ffn_in_proj_b", "L1_ffn_out_proj_w", "L1_ffn_out_proj_b", "L1_ffn_ln2_w", "L1_ffn_ln2_b",
        "L1_ffn_router_w", "L1_ffn_w1", "L1_ffn_w2"]


def kernel(**inputs):
    import numpy as np
    import concourse.bacc as bacc
    from concourse.bass_utils import run_bass_kernel_spmd as run

    nc = bacc.Bacc("TRN2", target_bir_lowering=False, num_devices=1)
    arrays, aps = {}, {}
    given = {name: np.ascontiguousarray(inputs[name]) for name in _INS} | {"rotary": rotary_tables()}
    for name, a in given.items():
        arrays[f"in_{name}"] = a
        aps[name] = nc.dram_tensor(f"in_{name}", a.shape, mybir.dt.from_np(a.dtype), kind="ExternalInput").ap()
    out = nc.dram_tensor("out_0", (NB, SEQ, P), F32, kind="ExternalOutput").ap()
    build(nc, aps, out)
    return run(nc, [arrays], core_ids=[0]).results[0]["out_0"]
```

```python
from contextlib import ExitStack

import concourse.bass as bass
from concourse import mybir

F32 = mybir.dt.float32
BF16 = mybir.dt.bfloat16
ALU = mybir.AluOpType
ACT = mybir.ActivationFunctionType
AX = mybir.AxisListType

P = 128
NB, SEQ = 8, 512
MT = SEQ // P
LAYERS = 2
NS = 16
NSH = NS // LAYERS
HEADS, HD, WIN = 8, 64, 64
PAIRS = HEADS // 2
KEYS = 2 * WIN + WIN
HID = 341
FT = 3
DI = 512
KT = DI // P
EXP, FF = 8, 256
EPS = 1e-5
MASKED = -1e30
TOK = NB * SEQ
SCRATCH = 24000

R_BU, R_BD, R_D = 0, 1, 2
R_LAYER = 3
L_COLS = 2 * FT + 3
R_G, R_B = R_LAYER + LAYERS * L_COLS, R_LAYER + LAYERS * L_COLS + 1
R_H1B1, R_H1B2 = R_B + 1, R_B + 1 + KT
R_H2B1, R_H2B2 = R_H1B2 + 1, R_H1B2 + 1 + KT
R_FMB1 = R_H2B2 + 1
R_N1W, R_N1B, R_N2W, R_N2B = (R_FMB1 + KT + i for i in range(4))
N_ROWS = R_N2B + 1


class Count:

    def __init__(self, sem, per, ahead=False, base=0):
        self.sem, self.per, self.ahead, self.base = sem, per, int(ahead), base

    def at(self, turn, n):
        return (turn + self.ahead) * self.per + n + self.base

    def again(self, turns, per, ahead=False):
        return Count(self.sem, per, ahead, self.at(turns, 0))


def build(nc, I, out):
    with ExitStack() as ctx:
        def sb(name, shape, dt=F32):
            return ctx.enter_context(nc.sbuf_tensor(name, shape, dt))

        def sem(name):
            return ctx.enter_context(nc.semaphore(name))

        def count(name, per, ahead=False):
            return Count(sem(name), per, ahead)

        big = sb("big", [P, 6 * TOK])
        xt0 = big[:, 0:TOK]
        state = big[:, TOK:2 * TOK]
        u_all = big[:, 2 * TOK:3 * TOK]
        delta = big[:, 3 * TOK:4 * TOK]
        y_all = big[:, 4 * TOK:5 * TOK]
        x_tok = y_all
        work = big[:, 5 * TOK:6 * TOK]
        ident = sb("ident", [P, P])
        identb = sb("identb", [P, P], BF16)
        maskb = sb("maskb", [P, 2, KEYS], BF16)
        rows = sb("rows", [N_ROWS, P])
        cols = sb("cols", [P, N_ROWS])
        rot_raw = sb("rot_raw", [P, 4, MT, HD])
        abc_all = sb("abc_all", [P, 3, NS])
        upper = sb("upper", [P, P])
        before = sb("before", [P, EXP, EXP])
        pow_half = sb("pow_half", [P, NB * MT])

        scratch = sb("scratch", [P, SCRATCH])

        class Cut:
            def __init__(self, at):
                self.at = at

            def __call__(self, *shape):
                n = 1
                for s in shape:
                    n *= s
                a = scratch[:, self.at:self.at + n]
                self.at += n
                assert self.at <= SCRATCH, self.at
                if len(shape) == 1:
                    return a
                names = " ".join(f"d{i}" for i in range(len(shape)))
                return a.rearrange(f"p ({names}) -> p {names}", **{f"d{i}": s for i, s in enumerate(shape)})

        bank = [ctx.enter_context(nc.psum_tensor(f"bank{i}", [P, 512], F32)) for i in range(8)]

        cut = Cut(SCRATCH - 2 * (2 + 2) * P - 10 * NB * MT - MT * P)
        wud_raw = cut(2, P)
        wud = cut(2, P)
        x_mv = cut(NB * MT, 2)
        x_stats = cut(NB * MT, 6)
        x_var = cut(NB * MT)
        x_rstd = cut(NB * MT)
        xn = cut(MT, P)
        relu_delta = y_all
        cut = Cut(0)
        wbc_raw = cut(2, NSH, P)
        wbc = cut(2, NSH, P)
        wqkv = cut(3, HEADS * HD)
        wo = cut(MT, P)
        qk_scale = cut(2, HD)
        rot = cut(4, MT, HD)
        attention_end = cut.at
        abc = cut(3, NSH)
        lcol = cut(L_COLS)
        w1 = cut(2, FT * P)
        w1s = cut(2, FT * P)
        w2 = cut(FT, P)
        b1s = cut(2 * FT)
        layer_end = cut.at
        hpad = cut(WIN + SEQ)
        squares = cut(2, HEADS * HD)
        sumsq = cut(2, 2 * HEADS)
        rnorm = cut(2, 2 * HEADS)
        sumsq_c = cut(2 * HEADS)
        k_n = cut(HEADS * HD)
        rot_q = cut(2, HEADS * HD)
        rot_k = cut(2, HEADS * HD)
        q_r = rot_q[:, 0]
        k_r = rot_k[:, 0]
        qT = cut(PAIRS, P)
        kT = cut(PAIRS, WIN + SEQ)
        vals = cut(MT + 1, 2, PAIRS, HD)
        edge = cut(MT, PAIRS, 2, HD)
        probs = cut(PAIRS, 2 * KEYS)
        probsT = cut(2, 2 * KEYS)
        wcut = [0]

        def wk(*shape):
            n = 1
            for s in shape:
                n *= s
            a = work[:, wcut[0]:wcut[0] + n]
            wcut[0] += n
            assert wcut[0] <= TOK
            if len(shape) == 1:
                return a
            names = " ".join(f"d{i}" for i in range(len(shape)))
            return a.rearrange(f"p ({names}) -> p {names}", **{f"d{i}": s for i, s in enumerate(shape)})

        mx = wk(HEADS)
        negmax = wk(HEADS)
        rowsum = wk(HEADS)
        rinv = wk(HEADS)
        o_tok = wk(HEADS * HD)
        oT = sb("oT", [P, MT, SEQ])
        abar = wk(2, SEQ)
        bu = wk(SEQ)
        hs = wk(SEQ)
        ch = wk(2, SEQ)
        cut.at = layer_end
        f_stats = cut(MT, 6)
        f_mv = cut(MT, 2)
        f_var = cut(MT)
        f_rstd = cut(MT)
        f_h = cut(SEQ)
        f_hn = cut(MT, P)
        f_hnT = cut(SEQ)
        f_gelu = cut(2, SEQ)
        f_act = cut(FT, SEQ)
        ffn_end = cut.at

        x1 = state
        xn1 = xt0
        qkv = big[:, 2 * TOK:5 * TOK].rearrange("p (m s c) -> p m s c", m=MT, s=NB)
        s_out = work
        cut = Cut(0)
        w_up = cut(3, DI)
        w_dn = cut(3, KT, P)
        m_up = cut(EXP, FF)
        m_dn = cut(EXP, 2, P)
        assert cut.at <= attention_end
        low = cut.at
        cut = Cut(ffn_end)
        inp_raw = cut(3, P)
        inpT = cut(3 * P)
        outp_raw = cut(P)
        outpT = cut(P)
        rout_raw = cut(P)
        routT = cut(EXP)
        up_bias = cut(3 * KT + 2 * EXP)
        g_row, b_row, fm_b2_row, out_b_row = (cut(P) for _ in range(4))
        in_b_row = cut(3 * P)
        rout_b_row = cut(EXP)
        n1b_wide, n2b_wide = cut(P), cut(P)
        second_end = cut.at
        sg = cut(SEQ)
        l_stats = cut(2, MT, 6)
        l_mv = cut(2, MT, 2)
        l_var = cut(2, MT)
        l_rstd = cut(2, MT)
        z_tok = cut(MT, P)
        n_tok = cut(MT, P)
        n_scaled = cut(MT, P)
        zT = cut(SEQ)
        wT = cut(2, SEQ)
        t_gelu = cut(MT, P)
        t_norm = cut(MT, P)
        t_gain = cut(MT, P)
        xn_b = cut(MT, P)
        xn_f = cut(MT, P)
        x_mid = cut(MT, P)
        z2 = cut(MT, P)
        z2T = cut(SEQ)
        cut = Cut(low)
        hid = cut(2, KT, SEQ)
        w3 = cut(MT, SEQ)
        assert cut.at <= ffn_end
        cut = Cut(low)
        prod = cut(NB * (NB + 1) // 2 * P)
        assert cut.at <= ffn_end
        cut = Cut(0)
        sc = cut(NB, NB, 16)
        pr = cut(NB, NB, 16)
        smax = cut(NB, 16)
        ssum = cut(NB, 16)
        sinv = cut(NB, 16)
        att = pr.rearrange("p s t h -> p s (t h)")
        assert cut.at <= 2 * 3 * DI
        cut = Cut(second_end)
        e_att = cut(MT, P)
        e_attT = cut(SEQ)
        e_in = cut(MT, P)
        e_acc = cut(2, MT, P)
        e_stats = cut(MT, 6)
        e_mv = cut(MT, 2)
        e_var = cut(MT)
        e_rstd = cut(MT)
        e_z = cut(MT, P)
        e_zT = cut(2, SEQ)
        lg = cut(MT, EXP)
        lmax = cut(MT)
        lsum = cut(MT)
        linv = cut(MT)
        pexp = cut(MT, EXP)
        prob = cut(MT, EXP)
        above = cut(MT, EXP, EXP)
        equal = cut(MT, EXP, EXP)
        rank = cut(MT, EXP)
        gates = cut(2, MT, EXP)
        e_hid = cut(2, 2, SEQ)
        cut = Cut(second_end)
        fin = cut(2, NB, P)
        fo = cut(2, NB, P)

        x_loaded, rows_loaded, wud_loaded, tables_loaded, rows_zeroed = (sem(n) for n in ("x_loaded", "rows_loaded", "wud_loaded", "tables_loaded", "rows_zeroed"))
        memsets_done, constants_made = sem("pool_memset"), sem("constants_made")
        cols_turned, cols_copied, wud_turned, wud_copied = sem("cols_turned"), sem("cols_copied"), sem("wud_turned"), sem("wud_copied")
        x_stats_done, x_aggr_done, x_var_done, x_rstd_done = sem("x_stats_done"), sem("x_aggr_done"), sem("x_var_done"), sem("x_rstd_done")
        met = {e: sem(f"{e}_met") for e in ("pe", "act", "dve", "pool", "sp")}

        def meet(eng, name, nth):
            eng.drain().then_inc(met[name], 1)
            for other in met:
                if other != name:
                    eng.wait_ge(met[other], nth)
            eng.sem_inc(passed, 1)

        passed = sem("waits_passed")

        def wait_alone(eng, semaphore, value):
            eng.wait_ge(semaphore, value)
            eng.sem_inc(passed, 1)

        xn_ready = count("xn_ready", 1)
        xT_turned = count("xT_turned", 1, True)
        xT_copied = count("xT_copied", 1, True)
        u_psum = count("u_psum", 1)
        u_done = count("u_done", 1, True)
        delta_psum = count("delta_psum", 1)
        delta_abs = count("delta_abs", 1, True)
        delta_relu = count("delta_relu", 1, True)
        delta_ln = count("delta_ln", 1)
        delta_done = sem("delta_done")

        layer_weights_loaded = sem("layer_weights_loaded")
        NLW = 9
        wbc_turned = count("wbc_turned", 4, True)
        layer_columns = count("layer_columns", 2)
        tokens_padded = count("tokens_padded", 1)
        rot_scaled = count("rot_scaled", 6)
        b1_product_done = count("b1_product_done", 1)

        TU, SU = MT, NSH
        shifted_ready = count("shifted_ready", 1)
        proj_filled = count("proj_filled", 2 * TU, True)
        squares_done = count("squares_done", 2 * TU, True)
        sumsq_done = count("sumsq_done", 2 * TU, True)
        sumsq_clipped = count("sumsq_clipped", 2 * TU)
        rnorm_done = count("rnorm_done", 2 * TU)
        k_normed = count("k_normed", TU)
        q_rotary_parts = count("q_rotary_parts", TU)
        q_rotated = count("q_rotated", TU)
        k_rotary_parts = count("k_rotary_parts", TU, True)
        k_rotated = count("k_rotated", TU, True)
        qkT_filled = count("qkT_filled", 2 * TU, True)
        kT_copied = count("kT_copied", TU, True)
        qT_copied = count("qT_copied", TU, True)
        edge_values_copied = count("edge_values_copied", 2)
        sim_filled = count("sim_filled", 2 * TU)
        max_done = count("max_done", 4 * TU)
        negmax_done = count("negmax_done", 4 * TU)
        exp_done = count("exp_done", 2 * TU, True)
        RING = MT + 1 + TU * PAIRS + TU
        TAIL = 3
        turn_bank_filled = count("turn_bank_filled", RING)
        turn_bank_emptied = count("turn_bank_emptied", RING, True)
        o_bank_filled = count("o_bank_filled", TU + 1)
        o_bank_emptied = count("o_bank_emptied", TU + 1, True)
        rinv_done = count("rinv_done", TU)
        scan_b_filled = count("scan_b_filled", SU)
        scan_c_filled = count("scan_c_filled", SU)
        decay_done = count("decay_done", SU)
        scan_bu_done = count("scan_bu_done", SU, True)
        scan_done = count("scan_done", SU, True)
        scan_ch_done = count("scan_ch_done", SU, True)
        y_added = count("y_added", SU, True)

        f_shifted_ready = count("f_shifted_ready", 1, True)
        f_h_padded = count("f_h_padded", 1)
        f_h_turned = count("f_h_turned", 1, True)
        aggr_done = count("aggr_done", 1, True)
        stats_done = count("stats_done", 1)
        var_done = count("var_done", 1)
        rstd_done = count("rstd_done", 1)
        f_normed = count("f_normed", 1, True)
        norm_turned = count("norm_turned", 1, True)
        norm_turned_copied = count("norm_turned_copied", 1, True)
        up_filled = count("up_filled", FT)
        gelu_done = count("gelu_done", FT, True)
        f_act_done = count("f_act_done", FT, True)
        f_down_filled = count("f_down_filled", 1, True)
        f_added = count("f_added", 1, True)

        x_view = I["L0_attn_x"].rearrange("b (m p) d -> p b m d", p=P)

        x_reloaded = sem("x_reloaded")
        second_weights_loaded = sem("second_weights_loaded")
        projections_turned, projections_copied, norm_bias_widened, bias_products_done = (
            sem(n) for n in ("projections_turned", "projections_copied", "norm_bias_widened", "bias_products"))
        sg_ready = count("sg_ready", 1)
        sg_turned = count("sg_turned", 1, True)
        x1_done = count("x1_done", 1, True)
        x1_stats_done, x1_aggr_done, x1_var_done, x1_rstd_done = (c.again(LAYERS * NB, 1) for c in (stats_done, aggr_done, var_done, rstd_done))
        z_stats_done, z_aggr_done, z_var_done, z_rstd_done = (c.again(NB, 1) for c in (x1_stats_done, x1_aggr_done, x1_var_done, x1_rstd_done))
        mid_stats_done = count("mid_stats_done", 2)
        mid_aggr_done = count("mid_aggr_done", 2)
        mid_var_done = count("mid_var_done", 2)
        mid_rstd_done = count("mid_rstd_done", 2)
        xn1_done = count("xn1_done", 1)
        z_done = count("z_done", 1)
        z_turned = norm_turned.again(LAYERS * NB, 1, True)
        zT_copied = norm_turned_copied.again(LAYERS * NB, 1)
        n_scaled_done = count("n_scaled_done", 1)
        n_done = count("n_done", 1)
        xn_b_done = count("xn_b_done", 1)
        xn_f_done = count("xn_f_done", 1)
        two_bank_filled = count("two_bank_filled", 2 * MT)
        two_bank_emptied = count("two_bank_emptied", 2 * MT, True)
        mlp_up_filled = up_filled.again(LAYERS * NB, 3 * KT)
        mlp_gelu_done = gelu_done.again(LAYERS * NB, 3 * KT, True)
        w_filled = count("w_filled", 2)
        w_copied = count("w_copied", 2, True)
        t_filled = count("t_filled", 1, True)
        t_gelu_done = count("t_gelu_done", 1, True)
        t_normed = count("t_normed", 1)
        t_gained = count("t_gained", 1)
        x_mid_done = count("x_mid_done", 1, True)
        z2_done = count("z2_done", 1)
        z2_turned = count("z2_turned", 1)
        z2T_copied = count("z2T_copied", 1, True)
        fm_filled = count("fm_filled", 1, True)
        s_out_done = count("s_out_done", 1, True)
        qk_products = count("qk_products", NB)
        pos_scores = count("pos_scores", 1)
        pos_max = count("pos_max", 1)
        pos_shifted = count("pos_shifted", 1)
        pos_exp = count("pos_exp", 1)
        pos_sum = count("pos_sum", 1)
        pos_sum_inverted = count("pos_sum_inverted", 1)
        pv_products = count("pv_products", NB)
        pos_att_summed = count("pos_att_summed", 1)
        pos_att_done = count("pos_att_done", 1, True)
        score_pads_set = sem("score_pads_set")
        e_att_staged = count("e_att_staged", 1)
        e_att_turned = count("e_att_turned", 1, True)
        e_attT_copied = count("e_attT_copied", 1)
        e_in_done = count("e_in_done", 1)
        e_proj_filled = count("e_proj_filled", 1)
        e_x_done = count("e_x_done", 1)
        e_stats_done = z_stats_done.again(NB, 1)
        e_aggr_done = z_aggr_done.again(NB, 1)
        e_var_done = z_var_done.again(NB, 1)
        e_rstd_done = z_rstd_done.again(NB, 1)
        e_z_done = z_done.again(NB, 1)
        e_z_turned = z_turned.again(NB, 1)
        e_zT_copied = zT_copied.again(NB, 1, True)
        e_router_filled = count("e_router_filled", 1)
        e_logits = count("e_logits", 2)
        e_shifted = count("e_shifted", 1)
        e_exp = count("e_exp", 1)
        e_sum = count("e_sum", 2)
        e_prob = count("e_prob", 1)
        e_compared = count("e_compared", 4)
        e_ranked = count("e_ranked", 1)
        e_gates = count("e_gates", 1)
        e_up_filled = mlp_up_filled.again(NB, 2 * EXP)
        e_gelu_done = mlp_gelu_done.again(NB, 2 * EXP, True)
        e_y_filled = count("e_y_filled", EXP, True)
        e_y_added = count("e_y_added", EXP, True)
        e_stored = count("e_stored", 1, True)
        STEP = (1, 3)
        QK_SUMS = {0: range(0, 3), 1: range(3, 5), 2: range(5, 6), 3: range(6, NB)}
        PV_SUMS = {6: range(0, 5), 7: range(5, NB)}
        z_silu_done = count("z_silu_done", 1)
        z_product_done = count("z_product_done", 1, True)
        z_final_done = count("z_final_done", 1)
        z_stored = [sem("z_stored_even"), sem("z_stored_odd")]

        row_list = [(R_BU, I["L0_attn_b"][0:2 * P]), (R_D, I["L0_attn_D"])]
        for l in range(LAYERS):
            r = R_LAYER + l * L_COLS
            row_list += [(r, I["L0_ffn_b1"][l, 0:HID]), (r + FT, I["L0_ffn_b1"][l, HID:2 * HID]), (r + 2 * FT, I["L0_ffn_b2"][l]),
                         (r + 2 * FT + 1, I["L0_ffn_ln_g"][l]), (r + 2 * FT + 2, I["L0_ffn_ln_b"][l])]
        row_list += [(r, I["L1_" + name]) for r, name in (
            (R_G, "attn_ln_g"), (R_B, "attn_ln_b"), (R_H1B1, "attn_h1_b1"), (R_H1B2, "attn_h1_b2"), (R_H2B1, "attn_h2_b1"),
            (R_H2B2, "attn_h2_b2"), (R_FMB1, "attn_fm_b1"), (R_N1W, "ffn_ln1_w"), (R_N1B, "ffn_ln1_b"), (R_N2W, "ffn_ln2_w"),
            (R_N2B, "ffn_ln2_b"))]
        n_row_dmas = sum((ap.shape[0] >= P) + (ap.shape[0] % P > 0) for _, ap in row_list)
        second_list = [(w_up[:, k], I[f"L1_attn_{n}_w1"]) for k, n in enumerate(("h1", "h2", "fm"))]
        second_list += [(w_dn[:, k], I[f"L1_attn_{n}_w2"].rearrange("(t p) n -> p t n", p=P)) for k, n in enumerate(("h1", "h2", "fm"))]
        second_list += [
            (inp_raw, I["L1_ffn_in_proj_w"].rearrange("(t p) k -> p t k", p=P)), (outp_raw, I["L1_ffn_out_proj_w"]),
            (rout_raw[0:EXP], I["L1_ffn_router_w"]), (m_up, I["L1_ffn_w1"].rearrange("e p f -> p e f")),
            (m_dn, I["L1_ffn_w2"].rearrange("e (f p) n -> p e f n", p=P)),
            (g_row, I["L1_attn_ln_g"].unsqueeze(0).to_broadcast([P, P])), (b_row, I["L1_attn_ln_b"].unsqueeze(0).to_broadcast([P, P])),
            (fm_b2_row, I["L1_attn_fm_b2"].unsqueeze(0).to_broadcast([P, P])), (out_b_row, I["L1_ffn_out_proj_b"].unsqueeze(0).to_broadcast([P, P])),
            (in_b_row, I["L1_ffn_in_proj_b"].unsqueeze(0).to_broadcast([P, 3 * P]))]

        def qkv_b(b, m):
            return qkv[:, m, bass.ds(b, 1)].rearrange("p s c -> p (s c)")

        def batch(a, b):
            return a[:, bass.ds(b * SEQ, SEQ)]

        QUARTERS = 4

        def quarter(a, i):
            return a[:, i * (TOK // QUARTERS):(i + 1) * (TOK // QUARTERS)]

        block = ctx.enter_context(nc.Block())

        @block.sync
        def _(sp):
            xt = x_tok.rearrange("p (b m d) -> p b m d", b=NB, m=MT)
            for b in range(0, NB, 2):
                for h in range(2):
                    sp.dma_start(xt[:, b + h], x_view[:, b + h]).then_inc(x_loaded, 16)
            sp.dma_start(wud_raw, I["L0_attn_W"][0:2 * P].rearrange("(t p) k -> p t k", p=P)).then_inc(wud_loaded, 16)
            sp.wait_ge(rows_zeroed, 1)

            def load_row(r, ap):
                full = ap.shape[0] // P
                if full:
                    sp.dma_start(rows[r:r + full, :], ap[0:full * P].rearrange("(t p) -> t p", p=P)).then_inc(rows_loaded, 16)
                if ap.shape[0] % P:
                    sp.dma_start(rows[r + full:r + full + 1, 0:ap.shape[0] % P], ap[full * P:ap.shape[0]].unsqueeze(0)).then_inc(rows_loaded, 16)

            for r, ap in row_list:
                load_row(r, ap)
            sp.dma_start(rot_raw[:], I["rotary"].rearrange("k (m p) d -> p k m d", p=P)).then_inc(tables_loaded, 16)
            bc0 = 2 * P + P * NS
            for i, src in enumerate((I["L0_attn_A"], I["L0_attn_b"][2 * P:bc0].rearrange("(d s) -> d s", s=NS),
                                     I["L0_attn_b"][bc0:bc0 + P * NS].rearrange("(d s) -> d s", s=NS))):
                sp.dma_start(abc_all[:, i], src).then_inc(tables_loaded, 16)

            def load_attention(l):
                wbc_v = I["L0_attn_W"][2 * P:2 * P + 2 * P * NS].rearrange("(h d s) k -> d h s k", h=2, s=NS)
                for h in range(2):
                    sp.dma_start(wbc_raw[:, h], wbc_v[:, h, l * NSH:(l + 1) * NSH]).then_inc(layer_weights_loaded, 16)
                sp.dma_start(wqkv, I["L0_ffn_wqkv"][l].rearrange("p (c n) -> p c n", c=3)).then_inc(layer_weights_loaded, 16)
                sp.dma_start(wo, I["L0_ffn_wo"][l].rearrange("(t p) n -> p t n", p=P)).then_inc(layer_weights_loaded, 16)
                for i, nm in enumerate(("q", "k")):
                    sp.dma_start(qk_scale[:, i], I[f"L0_ffn_{nm}_scale"][l].unsqueeze(0).to_broadcast([P, HD])).then_inc(layer_weights_loaded, 16)

            def load_ffn(l):
                sp.dma_start(w1[:, :, 0:HID], I["L0_ffn_w1"][l].rearrange("p (c n) -> p c n", c=2)).then_inc(layer_weights_loaded, 16)
                sp.dma_start(w2[:, 0:FT - 1], I["L0_ffn_w2"][l, 0:(FT - 1) * P].rearrange("(t p) n -> p t n", p=P)).then_inc(layer_weights_loaded, 16)
                sp.dma_start(w2[0:HID - (FT - 1) * P, FT - 1], I["L0_ffn_w2"][l, (FT - 1) * P:HID]).then_inc(layer_weights_loaded, 16)

            load_attention(0)
            sp.wait_ge(memsets_done, 6)
            load_ffn(0)
            for nth in range(1, 5):
                meet(sp, "sp", nth)
            load_attention(1)
            meet(sp, "sp", 5)
            load_ffn(1)
            meet(sp, "sp", 6)
            meet(sp, "sp", 7)
            for b in range(NB):
                sp.dma_start(xn1.rearrange("p (b m d) -> p b m d", b=NB, m=MT)[:, b], x_view[:, b]).then_inc(x_reloaded, 16)
            for dst, src in second_list:
                sp.dma_start(dst, src).then_inc(second_weights_loaded, 16)
            for nth in range(8, 12):
                meet(sp, "sp", nth)
            out_v = out.rearrange("b (m p) d -> p m b d", p=P)
            for m in range(MT):
                sp.wait_ge(z_final_done.sem, z_final_done.at(m, 1))
                sp.dma_start(out_v[:, m], fo[:, m % 2]).then_inc(z_stored[m % 2], 16)
            for s in z_stored:
                sp.wait_ge(s, 16 * MT // 2)

        @block.gpsimd
        def _(pool):
            pool.memset(ident[:], 0.0).then_inc(memsets_done, 1)
            pool.memset(identb[:], 0.0).then_inc(memsets_done, 1)
            pool.memset(maskb[:], 0.0).then_inc(memsets_done, 1)
            pool.memset(pow_half[:], -0.5).then_inc(memsets_done, 1)
            pool.memset(w1, 0.0).then_inc(memsets_done, 1)
            pool.wait_ge(memsets_done, 5)
            pool.memset(w2[HD:P, FT - 1], 0.0).then_inc(memsets_done, 1)
            pool.wait_ge(memsets_done, 6)
            for t in (ident, identb):
                pool.affine_select(out=t[:], in_=t[:], compare_op=ALU.not_equal, fill=1.0, base=0,
                                   pattern=[[-1, P]], channel_multiplier=1).then_inc(constants_made, 1)
            n = 2
            for kind in range(2):
                for base, step, mult in ((0, 1, -1), (WIN, -1, 1), (-WIN, 1, 0))[:2 + kind]:
                    pool.wait_ge(constants_made, n)
                    pool.affine_select(out=maskb[:, kind], in_=maskb[:, kind], compare_op=ALU.is_ge, fill=MASKED,
                                       base=base, pattern=[[step, KEYS]], channel_multiplier=mult).then_inc(constants_made, 1)
                    n += 1
            pool.memset(upper[:], 1.0).then_inc(memsets_done, 1)
            pool.memset(before[:], 0.0).then_inc(memsets_done, 1)
            pool.wait_ge(memsets_done, 8)
            pool.affine_select(out=upper[:], in_=upper[:], compare_op=ALU.is_ge, fill=0.0, base=0,
                               pattern=[[1, P]], channel_multiplier=-1).then_inc(constants_made, 1)
            for e in range(1, EXP):
                pool.memset(before[:, e, 0:e], 1.0).then_inc(constants_made, 1)
            wait_alone(pool, x_aggr_done, NB)
            pool.tensor_scalar(x_var, x_mv[:, :, 1], EPS, 1.0, ALU.add, ALU.mult).then_inc(x_var_done, 1)
            pool.wait_ge(x_var_done, 1)
            pool.tensor_tensor(x_rstd, x_var, pow_half[:], ALU.pow).then_inc(x_rstd_done, 1)
            with pool.Fori(0, NB) as b:
                wait_alone(pool, xT_copied.sem, xT_copied.at(b, 1))
                pool.tensor_copy(batch(state, b), batch(xt0, b))
            meet(pool, "pool", 1)
            for i in range(QUARTERS):
                wait_alone(pool, delta_done, i + 1)
                pool.tensor_scalar(quarter(y_all, i), quarter(u_all, i), cols[:, R_D:R_D + 1], 1.0, ALU.mult, ALU.mult)
            meet(pool, "pool", 2)
            for c in (k_rotary_parts, y_added, e_stored):
                pool.sem_inc(c.sem, c.per)
            with pool.Fori(0, LAYERS) as l:
                pool.memset(hpad[:, 0:WIN + 1], 0.0).then_inc(tokens_padded.sem, 1)
                pool.memset(kT[:, :, 0:WIN], 0.0)
                pool.memset(edge, 0.0)

                def rsqrt(it, m):
                    for w in range(2):
                        n = 2 * m + w
                        h8 = slice(w * HEADS, (w + 1) * HEADS)
                        if m >= 1:
                            pool.wait_ge(rnorm_done.sem, rnorm_done.at(it, n - 1))
                        wait_alone(pool, sumsq_done.sem, sumsq_done.at(it, n + 1))
                        pool.tensor_scalar(sumsq_c[:, h8], sumsq[:, m % 2, h8], 1e-24, 1.0, ALU.max, ALU.mult).then_inc(sumsq_clipped.sem, 1)
                        pool.wait_ge(sumsq_clipped.sem, sumsq_clipped.at(it, n + 1))
                        pool.wait_ge(exp_done.sem, exp_done.at(it, 2 * (m - 1)))
                        pool.tensor_tensor(rnorm[:, m % 2, h8], sumsq_c[:, h8], pow_half[:, 0:HEADS], ALU.pow).then_inc(rnorm_done.sem, 1)

                def rotate_k(it, m):
                    t = m % MT
                    pool.wait_ge(k_normed.sem, k_normed.at(it, m + 1))
                    pool.wait_ge(qkT_filled.sem, qkT_filled.at(it, 2 * m - 1))
                    kn = k_n.rearrange("p (h d) -> p h d", d=HD)
                    o = rot_k.rearrange("p a (h d) -> p a h d", d=HD)
                    H2 = HD // 2
                    pool.tensor_tensor(o[:, 0], kn, rot[:, 2, t].unsqueeze(1).to_broadcast([P, HEADS, HD]), ALU.mult)
                    pool.tensor_tensor(o[:, 1, :, 0:H2], kn[:, :, H2:HD], rot[:, 3, t, 0:H2].unsqueeze(1).to_broadcast([P, HEADS, H2]), ALU.mult)
                    pool.tensor_tensor(o[:, 1, :, H2:HD], kn[:, :, 0:H2], rot[:, 3, t, H2:HD].unsqueeze(1).to_broadcast([P, HEADS, H2]), ALU.mult).then_inc(k_rotary_parts.sem, 1)

                it0 = pool.snap(l * NB)
                rsqrt(it0, 0)
                rotate_k(it0, 0)
                meet(pool, "pool", l * 3 + 3)

                def turn(b, it, prev, nxt):
                    def add_y(s):
                        pool.wait_ge(scan_ch_done.sem, scan_ch_done.at(it, s + 1))
                        wait_alone(pool, y_added.sem, y_added.at(it, s))
                        pool.tensor_tensor(batch(y_all, b), batch(y_all, b), ch[:, s % 2], ALU.add).then_inc(y_added.sem, 1)

                    for m in range(MT):
                        if m + 1 < MT or nxt:
                            rsqrt(it, m + 1)
                            rotate_k(it, m + 1)
                        add_y(2 * m)
                        add_y(2 * m + 1)

                turn(0, it0, False, True)
                with pool.Fori(1, NB - 1) as b:
                    turn(b, pool.snap(l * NB + b), True, True)
                it_last = pool.snap(l * NB + NB - 1)
                turn(NB - 1, it_last, True, False)
                meet(pool, "pool", l * 3 + 4)
                with pool.Fori(0, NB) as b:
                    it = pool.snap(l * NB + b)
                    wait_alone(pool, aggr_done.sem, aggr_done.at(it, 1))
                    pool.tensor_scalar(f_var, f_mv[:, :, 1], EPS, 1.0, ALU.add, ALU.mult).then_inc(var_done.sem, 1)
                    pool.wait_ge(var_done.sem, var_done.at(it, 1))
                    pool.tensor_tensor(f_rstd, f_var, pow_half[:, 0:MT], ALU.pow).then_inc(rstd_done.sem, 1)
                meet(pool, "pool", l * 3 + 5)
            meet(pool, "pool", 9)

            def rstd(b, k, ag, vr, rs):
                i = 1 if ag is z_aggr_done else 0
                wait_alone(pool, ag.sem, ag.at(b, k + 1))
                pool.tensor_scalar(l_var[:, i], l_mv[:, i, :, 1], EPS, 1.0, ALU.add, ALU.mult).then_inc(vr.sem, 1)
                pool.wait_ge(vr.sem, vr.at(b, k + 1))
                pool.tensor_tensor(l_rstd[:, i], l_var[:, i], pow_half[:, 0:MT], ALU.pow).then_inc(rs.sem, 1)

            def gate_y(b, n):
                wait_alone(pool, sg_turned.sem, sg_turned.at(b, n))
                pool.tensor_tensor(sg, batch(y_all, b + n), batch(state, b + n), ALU.mult).then_inc(sg_ready.sem, 1)

            gate_y(0, 0)
            with pool.Fori(0, NB - 1) as b:
                gate_y(b, 1)
                rstd(b, 0, x1_aggr_done, x1_var_done, x1_rstd_done)
            rstd(NB - 1, 0, x1_aggr_done, x1_var_done, x1_rstd_done)

            def scale_n(b, n):
                pool.wait_ge(z_done.sem, z_done.at(b, n + 1))
                if n:
                    pool.wait_ge(n_done.sem, n_done.at(b, n))
                pool.tensor_tensor(n_scaled, z_tok, g_row.unsqueeze(1).to_broadcast([P, MT, P]), ALU.mult).then_inc(n_scaled_done.sem, 1)

            def l1_turn(b, prev, nxt):
                wait_alone(pool, n_scaled_done.sem, n_scaled_done.at(b, 1))
                wait_alone(pool, t_filled.sem, t_filled.at(b, 0))
                pool.tensor_tensor(n_tok, n_scaled, b_row.unsqueeze(1).to_broadcast([P, MT, P]), ALU.add).then_inc(n_done.sem, 1)
                if nxt:
                    rstd(b, 1, z_aggr_done, z_var_done, z_rstd_done)
                if prev:
                    rstd(b, -2, mid_aggr_done, mid_var_done, mid_rstd_done)
                    rstd(b, -1, mid_aggr_done, mid_var_done, mid_rstd_done)
                if nxt:
                    scale_n(b, 1)
                xb = xn1[:, bass.ds(b * SEQ, SEQ)].rearrange("p (m d) -> p m d", m=MT)
                wait_alone(pool, x_mid_done.sem, x_mid_done.at(b, 0))
                pool.tensor_tensor(xn_b, xb, b_row.unsqueeze(1).to_broadcast([P, MT, P]), ALU.add).then_inc(xn_b_done.sem, 1)
                wait_alone(pool, s_out_done.sem, s_out_done.at(b, 0))
                pool.tensor_tensor(xn_f, xb, fm_b2_row.unsqueeze(1).to_broadcast([P, MT, P]), ALU.add).then_inc(xn_f_done.sem, 1)

            rstd(0, 0, z_aggr_done, z_var_done, z_rstd_done)
            scale_n(0, 0)
            l1_turn(0, False, True)
            with pool.Fori(1, NB - 1) as b:
                l1_turn(b, True, True)
            l1_turn(NB - 1, True, False)
            rstd(NB, -2, mid_aggr_done, mid_var_done, mid_rstd_done)
            rstd(NB, -1, mid_aggr_done, mid_var_done, mid_rstd_done)
            meet(pool, "pool", 10)
            pool.memset(sc, MASKED).then_inc(score_pads_set, 1)

            def products_qk(m, states):
                for s in states:
                    q = qkv[:, bass.ds(m, 1), s, 0:P].to_broadcast([P, s + 1, P])
                    k = qkv[:, bass.ds(m, 1), 0:s + 1, P:2 * P].rearrange("p a s c -> p (a s) c")
                    at = s * (s + 1) // 2 * P
                    if s == 0:
                        wait_alone(pool, pos_att_done.sem, pos_att_done.at(m, 0))
                    pool.tensor_tensor(prod[:, at:at + (s + 1) * P].rearrange("p (t c) -> p t c", c=P), q, k, ALU.mult).then_inc(qk_products.sem, 1)

            def products_pv(m):
                wait_alone(pool, pos_exp.sem, pos_exp.at(m, 1))
                for s in range(NB):
                    v = qkv[:, bass.ds(m, 1), 0:s + 1, 2 * P:3 * P].rearrange("p a s (h d) -> p (a s) h d", d=8)
                    w = pr[:, s, 0:s + 1].unsqueeze(3).to_broadcast([P, s + 1, 16, 8])
                    at = s * (s + 1) // 2 * P
                    pool.tensor_tensor(prod[:, at:at + (s + 1) * P].rearrange("p (t h d) -> p t h d", h=16, d=8), w, v, ALU.mult).then_inc(pv_products.sem, 1)

            def stage(g, m, h, first=False):
                wait_alone(pool, e_att_turned.sem, e_att_turned.at(g - 1, 1))
                wait_alone(pool, pos_att_done.sem, pos_att_done.at(m, 1))
                pool.tensor_copy(e_att, qkv[:, bass.ds(m, 1), bass.ds(h * 4, 4), 0:P].rearrange("p a s c -> p (a s) c")).then_inc(e_att_staged.sem, 1)
                xs = xn1.rearrange("p (s m c) -> p m s c", s=NB, m=MT)[:, bass.ds(m, 1), bass.ds(h * 4, 4)].rearrange("p a s c -> p (a s) c")
                if not first:
                    wait_alone(pool, e_x_done.sem, e_x_done.at(g - 1, 1))
                pool.tensor_tensor(e_in, xs, out_b_row.unsqueeze(1).to_broadcast([P, MT, P]), ALU.add).then_inc(e_in_done.sem, 1)

            def e_rstd_of(g):
                wait_alone(pool, e_aggr_done.sem, e_aggr_done.at(g, 1))
                pool.tensor_scalar(e_var, e_mv[:, :, 1], EPS, 1.0, ALU.add, ALU.mult).then_inc(e_var_done.sem, 1)
                pool.wait_ge(e_var_done.sem, e_var_done.at(g, 1))
                pool.tensor_tensor(e_rstd, e_var, pow_half[:, 0:MT], ALU.pow).then_inc(e_rstd_done.sem, 1)

            def store(g, m, h):
                wait_alone(pool, e_y_added.sem, e_y_added.at(g, EXP))
                pool.tensor_copy(qkv[:, bass.ds(m, 1), bass.ds(h * 4, 4), P:2 * P].rearrange("p a s c -> p (a s) c"), e_acc[:, h]).then_inc(e_stored.sem, 1)

            def two_groups(m, nxt):
                g = m * 2
                stage(g + 1, m, 1)
                if nxt:
                    products_qk(m + 1, range(5))
                e_rstd_of(g + 1)
                if nxt:
                    products_qk(m + 1, range(5, NB))
                    products_pv(m + 1)
                store(g, m, 0)
                if nxt:
                    stage(g + 2, m + 1, 0)
                    e_rstd_of(g + 2)
                store(g + 1, m, 1)

            products_qk(0, range(NB))
            products_pv(0)
            stage(0, 0, 0, True)
            e_rstd_of(0)
            with pool.Fori(0, MT - 1) as m:
                two_groups(m, True)
            two_groups(MT - 1, False)
            meet(pool, "pool", 11)

        @block.scalar
        def _(act):
            act.wait_ge(cols_turned, 1)
            act.activation(cols[:], bank[7][:, 0:N_ROWS], ACT.Copy).then_inc(cols_copied, 1)
            act.wait_ge(wud_turned, 1)
            act.activation(wud.rearrange("p t k -> p (t k)"), bank[6][:, 0:2 * P], ACT.Copy).then_inc(wud_copied, 1)
            act.wait_ge(cols_copied, 1)
            for c in (xT_copied, delta_abs):
                act.sem_inc(c.sem, c.per)

            def copy_xT(b, n):
                wait_alone(act, xT_turned.sem, xT_turned.at(b, n + 1))
                act.activation(batch(xt0, b + n), bank[0][:, :], ACT.Copy).then_inc(xT_copied.sem, 1)

            def softplus_start(b):
                wait_alone(act, delta_psum.sem, delta_psum.at(b, 1))
                act.activation(batch(delta, b), bank[2][:, :], ACT.Abs, bias=cols[:, R_BD:R_BD + 1]).then_inc(delta_abs.sem, 1)
                wait_alone(act, delta_abs.sem, delta_abs.at(b, 1))
                act.activation(batch(delta, b), batch(delta, b), ACT.Exp, scale=-1.0)

            copy_xT(0, 0)
            with act.Fori(0, NB - 1) as b:
                copy_xT(b, 1)
                softplus_start(b)
            softplus_start(NB - 1)
            meet(act, "act", 1)
            for i in range(QUARTERS):
                act.activation(quarter(delta, i), quarter(delta, i), ACT.Ln, bias=1.0).then_inc(delta_ln.sem, 1)
            meet(act, "act", 2)
            for c in (squares_done, qT_copied, exp_done, turn_bank_emptied, norm_turned_copied, gelu_done):
                act.sem_inc(c.sem, c.per)
            with act.Fori(0, LAYERS) as l:
                def square(it, m):
                    for w in range(2):
                        n = 2 * m + w
                        act.wait_ge(proj_filled.sem, proj_filled.at(it, n + 1))
                        act.wait_ge(sumsq_done.sem, sumsq_done.at(it, n - 1))
                        act.activation(squares[:, w], bank[1 - w][:, :], ACT.Square).then_inc(squares_done.sem, 1)

                def from_turn_bank(it, ring, out_ap, in_ap, last=True):
                    act.wait_ge(turn_bank_filled.sem, turn_bank_filled.at(it, ring[0] + 1))
                    ins = act.activation(out_ap, in_ap, ACT.Copy)
                    if last:
                        ins.then_inc(turn_bank_emptied.sem, 1)
                        ring[0] += 1

                def copy_probs(it, ring, pair):
                    from_turn_bank(it, ring, probsT[:, pair % 2], bank[2][:, 0:2 * KEYS])

                def copy_oT(it, ring, m):
                    m %= MT
                    from_turn_bank(it, ring, oT[:, :, m * P:(m + 1) * P], bank[2][:, :].rearrange("p (r t) -> p r t", t=P))

                def decay(it, b, s):
                    wait_alone(act, scan_done.sem, scan_done.at(it, s - 1))
                    at = bass.ds((b + s // NSH) * SEQ, SEQ)
                    act.activation(abar[:, s % 2], delta[:, at], ACT.Exp, scale=abc[:, 0, s % NSH:s % NSH + 1]).then_inc(decay_done.sem, 1)

                it0 = act.snap(l * NB)
                square(it0, 0)
                for k in range(4):
                    act.wait_ge(wbc_turned.sem, wbc_turned.at(l, k + 1))
                    act.activation(wbc.rearrange("p h s k -> p (h s k)")[:, k * 512:(k + 1) * 512], bank[2 + k][:, :], ACT.Copy)
                meet(act, "act", l * 3 + 3)
                decay(it0, 0, 0)

                def turn(b, it, prev, nxt):
                    ring = [-TAIL if prev else 0]

                    def copy_q(m):
                        act.wait_ge(qkT_filled.sem, qkT_filled.at(it, 2 * m + 2))
                        act.activation(qT.rearrange("p r t -> p (r t)"), bank[0][:, :], ACT.Copy).then_inc(qT_copied.sem, 1)

                    def softmax(m, step, halves=(0, 1)):
                        for eo in halves:
                            act.wait_ge(negmax_done.sem, negmax_done.at(it, 4 * m + 2 * step + eo + 1))
                            for j in range(2):
                                pair = 2 * step + j
                                h, c = 2 * pair + eo, 4 * step + 2 * eo + j
                                ins = act.activation(probs[:, pair, eo * KEYS:(eo + 1) * KEYS], bank[4 + eo][:, j * KEYS:(j + 1) * KEYS], ACT.Exp,
                                                     scale=rnorm[:, m % 2, HEADS + h:HEADS + h + 1], bias=negmax[:, c:c + 1], accum_out=rowsum[:, h:h + 1])
                        if halves[-1]:
                            ins.then_inc(exp_done.sem, 1)

                    def values(i):
                        if i == 0:
                            from_turn_bank(it, ring, vals[:, 0, 0].rearrange("p r d -> p (r d)"), bank[2][:, 0:256])
                        elif i < MT:
                            from_turn_bank(it, ring, vals[:, i].rearrange("p e r d -> p (e r d)"), bank[2][:, :])
                        else:
                            from_turn_bank(it, ring, vals[0:HD, MT, 0].rearrange("p r d -> p (r d)"), bank[2][0:HD, 0:256], last=False)
                            from_turn_bank(it, ring, vals[:, MT, 1].rearrange("p r d -> p (r d)"), bank[2][:, 256:512])

                    for m in range(MT):
                        behind = m or prev
                        copy_q(m)
                        if behind:
                            copy_probs(it, ring, 2)
                        if m + 1 < MT or nxt:
                            square(it, m + 1)
                        if behind:
                            copy_probs(it, ring, 3)
                        if m == 0:
                            values(0)
                        softmax(m, 0)
                        decay(it, b, 2 * m + 1)
                        if behind:
                            copy_oT(it, ring, m - 1)
                        if m == 0:
                            for i in range(1, MT + 1):
                                values(i)
                        copy_probs(it, ring, 0)
                        if m + 1 < MT or nxt:
                            decay(it, b, 2 * m + 2)
                        softmax(m, 1, (0,))
                        copy_probs(it, ring, 1)
                        softmax(m, 1, (1,))

                turn(0, it0, False, True)
                with act.Fori(1, NB - 1) as b:
                    turn(b, act.snap(l * NB + b), True, True)
                it_last = act.snap(l * NB + NB - 1)
                turn(NB - 1, it_last, True, False)
                ring = [MT * PAIRS + 2 * MT + 1 - TAIL]
                copy_probs(it_last, ring, 2)
                copy_probs(it_last, ring, 3)
                copy_oT(it_last, ring, MT - 1)
                meet(act, "act", l * 3 + 4)

                def copy_normed(it, n):
                    act.wait_ge(norm_turned.sem, norm_turned.at(it, n + 1))
                    act.activation(f_hnT, bank[1][:, :], ACT.Copy).then_inc(norm_turned_copied.sem, 1)

                def ffn(b, it, nxt):
                    for j in range(FT):
                        act.wait_ge(up_filled.sem, up_filled.at(it, j + 1))
                        act.wait_ge(f_act_done.sem, f_act_done.at(it, j - 1))
                        act.activation(f_gelu[:, j % 2], bank[3 + 2 * (j % 2)][:, :], ACT.Gelu, bias=b1s[:, FT + j:FT + j + 1]).then_inc(gelu_done.sem, 1)
                    if nxt:
                        copy_normed(it, 1)

                it_first = act.snap(l * NB)
                act.activation(mx[:, 0:1], pow_half[:, 0:1], ACT.Gelu)
                copy_normed(it_first, 0)
                with act.Fori(0, NB - 1) as b:
                    ffn(b, act.snap(l * NB + b), True)
                it_last = act.snap(l * NB + NB - 1)
                ffn(NB - 1, it_last, False)
                meet(act, "act", l * 3 + 5)
            for i in range(QUARTERS):
                act.activation(quarter(state, i), quarter(state, i), ACT.Silu)
            act.wait_ge(projections_turned, 1)
            act.activation(inpT, bank[0][:, 0:3 * P], ACT.Copy)
            act.activation(outpT, bank[1][:, 0:P], ACT.Copy)
            act.activation(routT, bank[2][:, 0:EXP], ACT.Copy).then_inc(projections_copied, 1)
            meet(act, "act", 9)
            for c in (mlp_gelu_done, w_copied, t_gelu_done, z2T_copied):
                act.sem_inc(c.sem, c.per)

            def gelu_up(b, n, k, j):
                act.wait_ge(mlp_up_filled.sem, mlp_up_filled.at(b, n + 1))
                act.activation(hid[:, k % 2, j], bank[4 + n % 2][:, :], ACT.Gelu, bias=up_bias[:, k * KT + j:k * KT + j + 1]).then_inc(mlp_gelu_done.sem, 1)

            def copy_z(b, n):
                act.wait_ge(z_turned.sem, z_turned.at(b, n + 1))
                act.activation(zT, bank[0][:, :], ACT.Copy).then_inc(zT_copied.sem, 1)

            def gelu_t(b):
                act.wait_ge(t_filled.sem, t_filled.at(b, 0))
                act.activation(t_gelu.rearrange("p m d -> p (m d)"), bank[7][:, :], ACT.Gelu).then_inc(t_gelu_done.sem, 1)

            def last_mlp(b, n):
                act.wait_ge(z2_turned.sem, z2_turned.at(b, 0))
                act.activation(z2T, bank[1][:, :], ACT.Copy).then_inc(z2T_copied.sem, 1)
                for j in range(KT):
                    gelu_up(b, n + j, 2, j)

            def l1_turn(b, prev, nxt):
                first = -KT if prev else 0
                if prev:
                    gelu_t(b)
                for k, r in ((0, R_H1B2), (1, R_H2B2)):
                    for j in range(KT):
                        gelu_up(b, first + k * KT + j, k, j)
                    if k == 1 and nxt:
                        copy_z(b, 1)
                    act.wait_ge(w_filled.sem, w_filled.at(b, k + 1))
                    act.activation(wT[:, k], bank[6][:, :], ACT.Identity, bias=cols[:, r:r + 1]).then_inc(w_copied.sem, 1)
                if prev:
                    last_mlp(b, first + 2 * KT)

            copy_z(0, 0)
            l1_turn(0, False, True)
            with act.Fori(1, NB - 1) as b:
                l1_turn(b, True, True)
            l1_turn(NB - 1, True, False)
            gelu_t(NB)
            last_mlp(NB, -KT)
            meet(act, "act", 10)
            for c in (e_zT_copied, e_gelu_done):
                act.sem_inc(c.sem, c.per)

            def attention_exp(m):
                act.wait_ge(pos_shifted.sem, pos_shifted.at(m, 1))
                act.activation(pr, sc, ACT.Exp, scale=float(8) ** -0.5).then_inc(pos_exp.sem, 1)

            def router_exp(g):
                act.wait_ge(e_shifted.sem, e_shifted.at(g, 1))
                act.activation(pexp, lg, ACT.Exp).then_inc(e_exp.sem, 1)

            def copy_att(g):
                act.wait_ge(e_att_turned.sem, e_att_turned.at(g, 1))
                act.activation(e_attT, bank[0][:, :], ACT.Copy).then_inc(e_attT_copied.sem, 1)

            def copy_e_z(g, h):
                act.wait_ge(e_z_turned.sem, e_z_turned.at(g, 1))
                act.activation(e_zT[:, h], bank[0][:, :], ACT.Copy).then_inc(e_zT_copied.sem, 1)

            def two_groups(m, nxt):
                for h in range(2):
                    g = m * 2 + h
                    ahead = h == 0 or nxt
                    for e in range(EXP):
                        for f in range(2):
                            n = 2 * e + f
                            act.wait_ge(e_up_filled.sem, e_up_filled.at(g, n + 1))
                            if f == 0:
                                act.wait_ge(e_y_filled.sem, e_y_filled.at(g, e - 1))
                            act.activation(e_hid[:, e % 2, f], bank[2 + n % 4][:, :], ACT.Gelu, bias=up_bias[:, 3 * KT + n:3 * KT + n + 1]).then_inc(e_gelu_done.sem, 1)
                        if ahead:
                            if e == STEP[h] + 1:
                                copy_att(g + 1)
                            if e == STEP[h] + 4:
                                copy_e_z(g + 1, (h + 1) % 2)
                            if e == min(STEP[h] + 5, EXP - 1):
                                if h == 0 and nxt:
                                    attention_exp(m + 1)
                                router_exp(g + 1)

            attention_exp(0)
            copy_att(0)
            copy_e_z(0, 0)
            router_exp(0)
            with act.Fori(0, MT - 1) as m:
                two_groups(m, True)
            two_groups(MT - 1, False)
            meet(act, "act", 11)
            for m in range(MT):
                v = qkv[:, m, :, P:2 * P]
                act.activation(v, v, ACT.Silu).then_inc(z_silu_done.sem, 1)

        @block.vector
        def _(dve):
            dve.memset(rows[:], 0.0).then_inc(rows_zeroed, 1)
            dve.wait_ge(x_loaded, 16 * NB)
            for b in range(NB):
                for i in range(b * MT, (b + 1) * MT):
                    ins = dve.bn_stats(x_stats[:, i], x_tok[:, i * P:(i + 1) * P])
                ins.then_inc(x_stats_done, 1)
                dve.wait_ge(x_stats_done, b + 1)
                for i in range(b * MT, (b + 1) * MT):
                    ins = dve.bn_aggr(x_mv[:, i], x_stats[:, i])
                ins.then_inc(x_aggr_done, 1)
            dve.wait_ge(x_rstd_done, 1)
            dve.wait_ge(x_aggr_done, NB)
            for c in (u_done, delta_relu):
                dve.sem_inc(c.sem, c.per)

            def norm_x(b, n):
                dve.wait_ge(xT_turned.sem, xT_turned.at(b, n))
                for m in range(MT):
                    i = (b + n) * MT + m
                    ins = dve.tensor_scalar(xn[:, m], x_tok[:, bass.ds(i * P, P)], x_mv[:, bass.ds(i, 1), 0], x_rstd[:, bass.ds(i, 1)],
                                            ALU.subtract, ALU.mult)
                ins.then_inc(xn_ready.sem, 1)

            def u_and_delta(b):
                dve.wait_ge(u_psum.sem, u_psum.at(b, 1))
                dve.tensor_scalar(batch(u_all, b), bank[1][:, :], cols[:, R_BU:R_BU + 1], None, ALU.add).then_inc(u_done.sem, 1)
                dve.wait_ge(delta_abs.sem, delta_abs.at(b, 1))
                dve.tensor_scalar(batch(relu_delta, b), bank[2][:, :], cols[:, R_BD:R_BD + 1], 0.0, ALU.add, ALU.max).then_inc(delta_relu.sem, 1)

            norm_x(0, 0)
            norm_x(0, 1)
            wait_alone(dve, cols_copied, 1)
            with dve.Fori(0, NB - 2) as b:
                norm_x(b, 2)
                u_and_delta(b)
            u_and_delta(NB - 2)
            u_and_delta(NB - 1)
            meet(dve, "dve", 1)
            for i in range(QUARTERS):
                dve.wait_ge(delta_ln.sem, i + 1)
                dve.tensor_tensor(quarter(delta, i), quarter(delta, i), quarter(relu_delta, i), ALU.add).then_inc(delta_done, 1)
            meet(dve, "dve", 2)
            for c in (sumsq_done, kT_copied, k_rotated, o_bank_emptied, scan_bu_done, scan_done, scan_ch_done, f_shifted_ready, aggr_done, f_act_done, f_added, f_normed, pos_att_done):
                dve.sem_inc(c.sem, c.per)
            with dve.Fori(0, LAYERS) as l:
                dve.wait_ge(tables_loaded, 16 * 4)
                dve.tensor_copy(abc, abc_all[:, :, bass.ds(l * NSH, NSH)]).then_inc(layer_columns.sem, 1)
                dve.tensor_copy(lcol, cols[:, bass.ds(l * L_COLS + R_LAYER, L_COLS)]).then_inc(layer_columns.sem, 1)
                dve.wait_ge(layer_columns.sem, layer_columns.at(l, 2))
                H2 = HD // 2

                def shift(it, b, n):
                    if n:
                        dve.wait_ge(proj_filled.sem, proj_filled.at(it, 2 * MT))
                    dve.tensor_copy(hpad[0:HD, WIN:WIN + SEQ], state[0:HD, bass.ds((b + n) * SEQ, SEQ)])
                    dve.tensor_copy(hpad[HD:P, WIN + 1:WIN + SEQ], state[HD:P, bass.ds((b + n) * SEQ, SEQ - 1)]).then_inc(shifted_ready.sem, 1)

                def sum_squares(it, m):
                    for w in range(2):
                        dve.wait_ge(squares_done.sem, squares_done.at(it, 2 * m + w + 1))
                        dve.tensor_reduce(sumsq[:, m % 2, w * HEADS:(w + 1) * HEADS], squares[:, w].rearrange("p (h d) -> p h d", d=HD), AX.X, ALU.add).then_inc(sumsq_done.sem, 1)

                def norm_k(it, m):
                    par = m % 2
                    dve.wait_ge(rnorm_done.sem, rnorm_done.at(it, 2 * m + 1))
                    dve.wait_ge(k_rotary_parts.sem, k_rotary_parts.at(it, m))
                    kb = bank[1][:, :].rearrange("p (h d) -> p h d", d=HD)
                    dve.tensor_tensor(k_n.rearrange("p (h d) -> p h d", d=HD), kb, rnorm[:, par, 0:HEADS].unsqueeze(2).to_broadcast([P, HEADS, HD]),
                                      ALU.mult).then_inc(k_normed.sem, 1)

                def rotate_q(it, m):
                    t = m % MT
                    qb = bank[0][:, :].rearrange("p (h d) -> p h d", d=HD)
                    o = rot_q.rearrange("p a (h d) -> p a h d", d=HD)
                    dve.tensor_tensor(o[:, 1, :, 0:H2], qb[:, :, H2:HD], rot[:, 1, t, 0:H2].unsqueeze(1).to_broadcast([P, HEADS, H2]), ALU.mult)
                    dve.tensor_tensor(o[:, 1, :, H2:HD], qb[:, :, 0:H2], rot[:, 1, t, H2:HD].unsqueeze(1).to_broadcast([P, HEADS, H2]), ALU.mult)
                    dve.wait_ge(qkT_filled.sem, qkT_filled.at(it, 2 * m))
                    dve.tensor_tensor(o[:, 0], qb, rot[:, 0, t].unsqueeze(1).to_broadcast([P, HEADS, HD]), ALU.mult).then_inc(q_rotary_parts.sem, 1)
                    dve.wait_ge(q_rotary_parts.sem, q_rotary_parts.at(it, m + 1))
                    dve.tensor_tensor(q_r, rot_q[:, 0], rot_q[:, 1], ALU.add).then_inc(q_rotated.sem, 1)

                def add_k(it, m):
                    dve.wait_ge(k_rotary_parts.sem, k_rotary_parts.at(it, m + 1))
                    dve.tensor_tensor(k_r, rot_k[:, 0], rot_k[:, 1], ALU.add).then_inc(k_rotated.sem, 1)

                def invert_sums(it, m):
                    dve.wait_ge(exp_done.sem, exp_done.at(it, 2 * m + 2))
                    dve.reciprocal(rinv, rowsum).then_inc(rinv_done.sem, 1)

                def normalise(it, m):
                    dve.wait_ge(rinv_done.sem, rinv_done.at(it, m + 1))
                    dve.wait_ge(o_bank_filled.sem, o_bank_filled.at(it, m + 1 if m >= 0 else -1))
                    dve.tensor_tensor(o_tok.rearrange("p (h d) -> p h d", d=HD), bank[3][:, :].rearrange("p (h d) -> p h d", d=HD),
                                      rinv.unsqueeze(2).to_broadcast([P, HEADS, HD]), ALU.mult).then_inc(o_bank_emptied.sem, 1)

                def residual(it, b):
                    dve.wait_ge(o_bank_filled.sem, o_bank_filled.at(it, 0))
                    at = bass.ds((b - 1) * SEQ, SEQ)
                    dve.tensor_tensor(state[:, at], bank[3][:, :], state[:, at], ALU.add).then_inc(o_bank_emptied.sem, 1)

                it0 = dve.snap(l * NB)
                dve.wait_ge(tokens_padded.sem, tokens_padded.at(l, 1))
                shift(it0, 0, 0)
                dve.wait_ge(layer_weights_loaded, 16 * NLW * (l + 1))
                for t in range(4):
                    s = qk_scale[:, t // 2]
                    for a, c in (((0, HD),) if t % 2 == 0 else ((0, H2), (H2, HD))):
                        w = c - a
                        src = a if t % 2 == 0 else (H2 if a == 0 else 0)
                        dve.tensor_tensor(rot[:, t, :, a:c], rot_raw[:, t, :, a:c], s[:, src:src + w].unsqueeze(1).to_broadcast([P, MT, w]),
                                          ALU.mult).then_inc(rot_scaled.sem, 1)
                sum_squares(it0, 0)
                norm_k(it0, 0)
                dve.wait_ge(rot_scaled.sem, rot_scaled.at(l, 6))
                rotate_q(it0, 0)
                dve.tensor_scalar(w1s, w1, lcol[:, 2 * FT + 1:2 * FT + 2], None, ALU.mult)
                dve.wait_ge(b1_product_done.sem, b1_product_done.at(l, 1))
                dve.tensor_tensor(b1s, bank[6][:, 0:2 * FT], lcol[:, 0:2 * FT], ALU.add)
                add_k(it0, 0)
                meet(dve, "dve", l * 3 + 3)

                def turn(b, it, prev, nxt):
                    def maxima(m, step):
                        dve.wait_ge(sim_filled.sem, sim_filled.at(it, 2 * m + step + 1))
                        dve.wait_ge(rnorm_done.sem, rnorm_done.at(it, 2 * m + 2))
                        qn = rnorm[:, m % 2, HEADS + 4 * step:HEADS + 4 * step + 4].rearrange("p (j e) -> p e j", e=2)
                        for eo in range(2):
                            n = 4 * m + 2 * step + eo + 1
                            c = slice(4 * step + 2 * eo, 4 * step + 2 * eo + 2)
                            dve.tensor_reduce(mx[:, c], bank[4 + eo][:, 0:2 * KEYS].rearrange("p (j k) -> p j k", k=KEYS), AX.X, ALU.max).then_inc(max_done.sem, 1)
                            dve.wait_ge(max_done.sem, max_done.at(it, n))
                            dve.scalar_tensor_tensor(out=negmax[:, c], in0=mx[:, c], scalar=-1.0, in1=qn[:, eo], op0=ALU.mult, op1=ALU.mult).then_inc(negmax_done.sem, 1)

                    def scan_in(s):
                        dve.wait_ge(scan_b_filled.sem, scan_b_filled.at(it, s + 1))
                        dve.wait_ge(scan_done.sem, scan_done.at(it, s))
                        dve.scalar_tensor_tensor(out=bu, in0=bank[6][:, :], scalar=abc[:, 1, s:s + 1], in1=batch(u_all, b), op0=ALU.add, op1=ALU.mult).then_inc(scan_bu_done.sem, 1)

                    def scan(s):
                        dve.wait_ge(scan_bu_done.sem, scan_bu_done.at(it, s + 1))
                        dve.wait_ge(decay_done.sem, decay_done.at(it, s + 1))
                        dve.wait_ge(scan_ch_done.sem, scan_ch_done.at(it, s))
                        dve.tensor_tensor_scan(hs, abar[:, s % 2], bu, 0.0, ALU.mult, ALU.add).then_inc(scan_done.sem, 1)

                    def scan_out(s):
                        dve.wait_ge(scan_done.sem, scan_done.at(it, s + 1))
                        dve.wait_ge(scan_c_filled.sem, scan_c_filled.at(it, s + 1))
                        dve.wait_ge(y_added.sem, y_added.at(it, s - 1))
                        dve.scalar_tensor_tensor(out=ch[:, s % 2], in0=bank[7][:, :], scalar=abc[:, 2, s:s + 1], in1=hs, op0=ALU.add, op1=ALU.mult).then_inc(scan_ch_done.sem, 1)

                    def edges(part):
                        lo, hi = (0, 2) if part == 0 else (2, MT)
                        dve.wait_ge(turn_bank_emptied.sem, turn_bank_emptied.at(it, 3 if part == 0 else MT + 1))
                        dve.tensor_copy(edge[0:HD, lo:hi, :, 0], vals[0:HD, lo + 1:hi + 1, 0])
                        lo = max(lo, 1)
                        dve.tensor_copy(edge[HD:P, lo:hi, :, 1], vals[HD:P, lo:hi, 1]).then_inc(edge_values_copied.sem, 1)

                    def copy_k(m):
                        dve.wait_ge(qkT_filled.sem, qkT_filled.at(it, 2 * m + 1))
                        dve.tensor_copy(kT[:, :, WIN + m * P:WIN + (m + 1) * P], bank[1][:, :].rearrange("p (r t) -> p r t", t=P)).then_inc(kT_copied.sem, 1)

                    for m in range(MT):
                        behind = m or prev
                        copy_k(m)
                        if behind:
                            invert_sums(it, m - 1)
                        scan_in(2 * m)
                        scan(2 * m)
                        if m + 1 < MT or nxt:
                            sum_squares(it, m + 1)
                        maxima(m, 0)
                        if m + 1 < MT or nxt:
                            norm_k(it, m + 1)
                        if behind:
                            normalise(it, m - 1)
                        scan_out(2 * m)
                        if m == MT - 2 and nxt:
                            shift(it, b, 1)
                        scan_in(2 * m + 1)
                        if m + 1 < MT or nxt:
                            rotate_q(it, m + 1)
                            add_k(it, m + 1)
                        maxima(m, 1)
                        scan(2 * m + 1)
                        if m == 0:
                            edges(0)
                            edges(1)
                            if prev:
                                residual(it, b)
                        scan_out(2 * m + 1)

                turn(0, it0, False, True)
                with dve.Fori(1, NB - 1) as b:
                    turn(b, dve.snap(l * NB + b), True, True)
                it_last = dve.snap(l * NB + NB - 1)
                turn(NB - 1, it_last, True, False)
                invert_sums(it_last, MT - 1)
                normalise(it_last, MT - 1)
                it_end = dve.snap(l * NB + NB)
                residual(it_end, NB)
                meet(dve, "dve", l * 3 + 4)
                dve.memset(f_h[HD:P, 0:1], 0.0).then_inc(f_h_padded.sem, 1)

                def shift_h(it, b, n):
                    dve.wait_ge(f_h_turned.sem, f_h_turned.at(it, n))
                    dve.tensor_copy(f_h[0:HD], state[0:HD, bass.ds((b + n) * SEQ, SEQ)])
                    dve.tensor_copy(f_h[HD:P, 1:SEQ], state[HD:P, bass.ds((b + n) * SEQ, SEQ - 1)]).then_inc(f_shifted_ready.sem, 1)

                def statistics(it, n):
                    dve.wait_ge(f_h_turned.sem, f_h_turned.at(it, n + 1))
                    for m in range(MT):
                        ins = dve.bn_stats(f_stats[:, m], bank[0][:, m * P:(m + 1) * P])
                    ins.then_inc(stats_done.sem, 1)

                def aggregate(it, n):
                    wait_alone(dve, stats_done.sem, stats_done.at(it, n + 1))
                    for m in range(MT):
                        ins = dve.bn_aggr(f_mv[:, m], f_stats[:, m])
                    ins.then_inc(aggr_done.sem, 1)

                def normed(it, n):
                    dve.wait_ge(aggr_done.sem, aggr_done.at(it, n + 1))
                    dve.wait_ge(rstd_done.sem, rstd_done.at(it, n + 1))
                    dve.wait_ge(norm_turned.sem, norm_turned.at(it, n))
                    for m in range(MT):
                        ins = dve.tensor_scalar(f_hn[:, m], bank[0][:, m * P:(m + 1) * P], f_mv[:, m, 0:1], f_rstd[:, m:m + 1], ALU.subtract, ALU.mult)
                    ins.then_inc(f_normed.sem, 1)

                def ffn(b, it, nxt):
                    if nxt:
                        shift_h(it, b, 1)
                        statistics(it, 1)
                    for j in range(FT):
                        dve.wait_ge(gelu_done.sem, gelu_done.at(it, j + 1))
                        if j == 0:
                            dve.wait_ge(f_down_filled.sem, f_down_filled.at(it, 0))
                        dve.scalar_tensor_tensor(out=f_act[:, j], in0=bank[2 + 2 * (j % 2)][:, :], scalar=b1s[:, j:j + 1], in1=f_gelu[:, j % 2],
                                                 op0=ALU.add, op1=ALU.mult).then_inc(f_act_done.sem, 1)
                        if j == 0 and nxt:
                            aggregate(it, 1)
                        if j == 1 and nxt:
                            normed(it, 1)
                    dve.wait_ge(f_down_filled.sem, f_down_filled.at(it, 1))
                    dve.scalar_tensor_tensor(out=batch(state, b), in0=bank[6][:, :], scalar=lcol[:, 2 * FT:2 * FT + 1], in1=batch(state, b),
                                             op0=ALU.add, op1=ALU.add).then_inc(f_added.sem, 1)

                it_first = dve.snap(l * NB)
                shift_h(it_first, 0, 0)
                statistics(it_first, 0)
                aggregate(it_first, 0)
                normed(it_first, 0)
                with dve.Fori(0, NB - 1) as b:
                    ffn(b, dve.snap(l * NB + b), True)
                it_last = dve.snap(l * NB + NB - 1)
                ffn(NB - 1, it_last, False)
                meet(dve, "dve", l * 3 + 5)
            dve.tensor_copy(n1b_wide, cols[:, R_N1B:R_N1B + 1].to_broadcast([P, P]))
            dve.tensor_copy(n2b_wide, cols[:, R_N2B:R_N2B + 1].to_broadcast([P, P])).then_inc(norm_bias_widened, 1)
            dve.wait_ge(bias_products_done, 1)
            dve.wait_ge(second_weights_loaded, 16 * len(second_list))
            for k, r in enumerate((R_H1B1, R_H2B1, R_FMB1)):
                dve.tensor_tensor(up_bias[:, k * KT:(k + 1) * KT], bank[5][:, k * KT:(k + 1) * KT], cols[:, r:r + KT], ALU.add)
            dve.tensor_copy(up_bias[:, 3 * KT:], bank[5][:, 3 * KT:3 * KT + 2 * EXP])
            dve.tensor_tensor(in_b_row, bank[6][:, 0:3 * P], in_b_row, ALU.add)
            dve.tensor_copy(rout_b_row, bank[7][:, 0:EXP])
            dve.tensor_scalar(w_up, w_up, cols[:, R_G:R_G + 1], None, ALU.mult)
            dve.tensor_scalar(inpT, inpT, cols[:, R_N1W:R_N1W + 1], None, ALU.mult)
            dve.tensor_scalar(routT, routT, cols[:, R_N2W:R_N2W + 1], None, ALU.mult)
            dve.tensor_scalar(m_up, m_up, cols[:, R_N2W:R_N2W + 1], None, ALU.mult)
            meet(dve, "dve", 9)
            dve.wait_ge(x_reloaded, 16 * NB)
            for c in (x1_done, two_bank_emptied, s_out_done, x_mid_done, z_product_done, e_y_added):
                dve.sem_inc(c.sem, c.per)

            def tile_of(a, b):
                return lambda m: a[:, bass.ds(b * SEQ + m * P, P)]

            def statistics(b, k, i, bn, ag, src):
                for m in range(MT):
                    ins = dve.bn_stats(l_stats[:, i, m], src(m))
                ins.then_inc(bn.sem, 1)
                wait_alone(dve, bn.sem, bn.at(b, k + 1))
                for m in range(MT):
                    ins = dve.bn_aggr(l_mv[:, i, m], l_stats[:, i, m])
                ins.then_inc(ag.sem, 1)

            def normed(b, k, i, ag, rs, src, dst, done):
                dve.wait_ge(ag.sem, ag.at(b, k + 1))
                dve.wait_ge(rs.sem, rs.at(b, k + 1))
                for m in range(MT):
                    ins = dve.tensor_scalar(dst(m), src(m), l_mv[:, i, m, 0:1], l_rstd[:, i, m:m + 1], ALU.subtract, ALU.mult)
                ins.then_inc(done.sem, 1)

            def block_out(b):
                dve.wait_ge(sg_turned.sem, sg_turned.at(b, 1))
                dve.tensor_tensor(batch(x1, b), bank[0][:, :], batch(xn1, b), ALU.add).then_inc(x1_done.sem, 1)

            def x1_statistics(b):
                wait_alone(dve, x1_done.sem, x1_done.at(b, 1))
                statistics(b, 0, 0, x1_stats_done, x1_aggr_done, tile_of(x1, b))

            def x1_normed(b):
                normed(b, 0, 0, x1_aggr_done, x1_rstd_done, tile_of(x1, b), tile_of(xn1, b), xn1_done)

            block_out(0)
            x1_statistics(0)
            with dve.Fori(1, NB - 1) as b:
                block_out(b)
                x1_normed(b - 1)
                x1_statistics(b)
            block_out(NB - 1)
            x1_normed(NB - 2)
            x1_statistics(NB - 1)
            x1_normed(NB - 1)
            dve.wait_ge(xn1_done.sem, NB)

            def z_statistics(b, n):
                statistics(b, n, 1, z_stats_done, z_aggr_done, tile_of(xn1, b + n))

            def z_normed(b, n):
                if n:
                    dve.wait_ge(n_scaled_done.sem, n_scaled_done.at(b, 1))
                normed(b, n, 1, z_aggr_done, z_rstd_done, tile_of(xn1, b + n), lambda m: z_tok[:, m], z_done)

            def project_qkv(b, n, first):
                for m in range(MT):
                    dve.wait_ge(two_bank_filled.sem, two_bank_filled.at(b, first + m + 1))
                    dve.tensor_tensor(qkv_b(b + n, m), bank[2 + m % 2][:, 0:3 * P], in_b_row, ALU.add).then_inc(two_bank_emptied.sem, 1)

            def norm_t(b):
                wait_alone(dve, t_gelu_done.sem, t_gelu_done.at(b, 0))
                statistics(b, -2, 0, mid_stats_done, mid_aggr_done, lambda m: t_gelu[:, m])

            def norm_x_mid(b):
                normed(b, -2, 0, mid_aggr_done, mid_rstd_done, lambda m: t_gelu[:, m], lambda m: t_norm[:, m], t_normed)
                dve.wait_ge(t_normed.sem, t_normed.at(b, 0))
                dve.tensor_tensor(t_gain, t_norm, g_row.unsqueeze(1).to_broadcast([P, MT, P]), ALU.mult).then_inc(t_gained.sem, 1)
                dve.wait_ge(t_gained.sem, t_gained.at(b, 0))
                dve.wait_ge(xn_b_done.sem, xn_b_done.at(b, 0))
                dve.tensor_tensor(x_mid, t_gain, xn_b, ALU.add).then_inc(x_mid_done.sem, 1)
                wait_alone(dve, x_mid_done.sem, x_mid_done.at(b, 0))
                statistics(b, -1, 0, mid_stats_done, mid_aggr_done, lambda m: x_mid[:, m])
                normed(b, -1, 0, mid_aggr_done, mid_rstd_done, lambda m: x_mid[:, m], lambda m: z2[:, m], z2_done)

            def finish(b):
                dve.wait_ge(fm_filled.sem, fm_filled.at(b, 0))
                dve.wait_ge(xn_f_done.sem, xn_f_done.at(b, 0))
                dve.tensor_tensor(s_out[:, bass.ds((b - 1) * SEQ, SEQ)], bank[1][:, :], xn_f.rearrange("p m d -> p (m d)"), ALU.add).then_inc(s_out_done.sem, 1)

            def l1_turn(b, prev, nxt):
                if nxt:
                    z_statistics(b, 1)
                if prev:
                    norm_t(b)
                if nxt:
                    z_normed(b, 1)
                if prev:
                    norm_x_mid(b)
                if nxt:
                    project_qkv(b, 1, MT)
                for j in range(MT):
                    n = (2 if nxt else 1) * MT + j
                    dve.wait_ge(two_bank_filled.sem, two_bank_filled.at(b, n + 1))
                    ins = dve.tensor_tensor(w3[:, j, 0:P], bank[2 + n % 2][:, 0:P], upper[:], ALU.mult)
                    if j < MT - 1:
                        ins = dve.tensor_copy(w3[:, j, P:(MT - j) * P], bank[2 + n % 2][:, P:(MT - j) * P])
                    ins.then_inc(two_bank_emptied.sem, 1)
                    if j == 1 and prev:
                        finish(b)

            z_statistics(0, 0)
            z_normed(0, 0)
            project_qkv(0, 0, 0)
            l1_turn(0, False, True)
            with dve.Fori(1, NB - 1) as b:
                l1_turn(b, True, True)
            l1_turn(NB - 1, True, False)
            norm_t(NB)
            norm_x_mid(NB)
            finish(NB)
            meet(dve, "dve", 10)
            dve.wait_ge(score_pads_set, 1)

            def sum_qk(m, batches):
                for s in batches:
                    at = s * (s + 1) // 2 * P
                    dve.wait_ge(qk_products.sem, qk_products.at(m, s + 1))
                    ins = dve.tensor_reduce(sc[:, s, 0:s + 1].rearrange("p t h -> p (t h)"), prod[:, at:at + (s + 1) * P].rearrange("p (g d) -> p g d", d=8), AX.X, ALU.add)
                    if s == NB - 1:
                        ins.then_inc(pos_scores.sem, 1)

            def score_max(m):
                dve.wait_ge(pos_scores.sem, pos_scores.at(m, 1))
                dve.tensor_reduce(smax, sc.rearrange("p s t h -> p s h t"), AX.X, ALU.max).then_inc(pos_max.sem, 1)
                dve.wait_ge(pos_max.sem, pos_max.at(m, 1))
                dve.tensor_tensor(sc, sc, smax.unsqueeze(2).to_broadcast([P, NB, NB, 16]), ALU.subtract).then_inc(pos_shifted.sem, 1)

            def score_sum(m):
                dve.wait_ge(pos_exp.sem, pos_exp.at(m, 1))
                dve.tensor_reduce(ssum, pr.rearrange("p s t h -> p s h t"), AX.X, ALU.add).then_inc(pos_sum.sem, 1)
                dve.wait_ge(pos_sum.sem, pos_sum.at(m, 1))
                dve.reciprocal(sinv, ssum).then_inc(pos_sum_inverted.sem, 1)

            def sum_pv(m, batches):
                for s in batches:
                    at = s * (s + 1) // 2 * P
                    dve.wait_ge(pv_products.sem, pv_products.at(m, s + 1))
                    ins = dve.tensor_reduce(att[:, s], prod[:, at:at + (s + 1) * P].rearrange("p (t c) -> p c t", c=P), AX.X, ALU.add)
                    if s == NB - 1:
                        ins.then_inc(pos_att_summed.sem, 1)

            def attention_out(m):
                dve.wait_ge(pos_att_summed.sem, pos_att_summed.at(m, 1))
                dve.wait_ge(pos_sum_inverted.sem, pos_sum_inverted.at(m, 1))
                dve.tensor_tensor(qkv[:, bass.ds(m, 1), :, 0:P].rearrange("p a s (h d) -> p (a s) h d", d=8), att.rearrange("p s (h d) -> p s h d", d=8),
                                  sinv.unsqueeze(3).to_broadcast([P, NB, 16, 8]), ALU.mult).then_inc(pos_att_done.sem, 1)

            def project_att(g, h, first=False):
                dve.wait_ge(e_proj_filled.sem, e_proj_filled.at(g, 1))
                dve.wait_ge(e_in_done.sem, e_in_done.at(g, 1))
                if not first:
                    dve.wait_ge(e_stored.sem, e_stored.at(g - 2, 1))
                acc = e_acc[:, h]
                dve.tensor_tensor(acc.rearrange("p m d -> p (m d)"), bank[0][:, :], e_in.rearrange("p m d -> p (m d)"), ALU.add).then_inc(e_x_done.sem, 1)
                wait_alone(dve, e_x_done.sem, e_x_done.at(g, 1))
                for i in range(MT):
                    ins = dve.bn_stats(e_stats[:, i], acc[:, i])
                ins.then_inc(e_stats_done.sem, 1)
                wait_alone(dve, e_stats_done.sem, e_stats_done.at(g, 1))
                for i in range(MT):
                    ins = dve.bn_aggr(e_mv[:, i], e_stats[:, i])
                ins.then_inc(e_aggr_done.sem, 1)

            def e_normed(g, h):
                dve.wait_ge(e_aggr_done.sem, e_aggr_done.at(g, 1))
                dve.wait_ge(e_rstd_done.sem, e_rstd_done.at(g, 1))
                for i in range(MT):
                    ins = dve.tensor_scalar(e_z[:, i], e_acc[:, h, i], e_mv[:, i, 0:1], e_rstd[:, i:i + 1], ALU.subtract, ALU.mult)
                ins.then_inc(e_z_done.sem, 1)

            def router_logits(g):
                dve.wait_ge(e_router_filled.sem, e_router_filled.at(g, 1))
                dve.tensor_tensor(lg, bank[1][:, 0:MT * EXP].rearrange("p (i e) -> p i e", e=EXP), rout_b_row.unsqueeze(1).to_broadcast([P, MT, EXP]), ALU.add).then_inc(e_logits.sem, 1)
                dve.wait_ge(e_logits.sem, e_logits.at(g, 1))
                dve.tensor_reduce(lmax, lg, AX.X, ALU.max).then_inc(e_logits.sem, 1)
                dve.wait_ge(e_logits.sem, e_logits.at(g, 2))
                dve.tensor_tensor(lg, lg, lmax.unsqueeze(2).to_broadcast([P, MT, EXP]), ALU.subtract).then_inc(e_shifted.sem, 1)

            def router_gates(g, h):
                dve.wait_ge(e_exp.sem, e_exp.at(g, 1))
                dve.tensor_reduce(lsum, pexp, AX.X, ALU.add).then_inc(e_sum.sem, 1)
                dve.wait_ge(e_sum.sem, e_sum.at(g, 1))
                dve.reciprocal(linv, lsum).then_inc(e_sum.sem, 1)
                dve.wait_ge(e_sum.sem, e_sum.at(g, 2))
                dve.tensor_tensor(prob, pexp, linv.unsqueeze(2).to_broadcast([P, MT, EXP]), ALU.mult).then_inc(e_prob.sem, 1)
                dve.wait_ge(e_prob.sem, e_prob.at(g, 1))
                other = prob.unsqueeze(2).to_broadcast([P, MT, EXP, EXP])
                own = prob.unsqueeze(3).to_broadcast([P, MT, EXP, EXP])
                dve.tensor_tensor(above, other, own, ALU.is_gt).then_inc(e_compared.sem, 1)
                dve.tensor_tensor(equal, other, own, ALU.is_equal).then_inc(e_compared.sem, 1)
                dve.wait_ge(e_compared.sem, e_compared.at(g, 2))
                dve.tensor_tensor(equal, equal, before[:].unsqueeze(1).to_broadcast([P, MT, EXP, EXP]), ALU.mult).then_inc(e_compared.sem, 1)
                dve.wait_ge(e_compared.sem, e_compared.at(g, 3))
                dve.tensor_tensor(above, above, equal, ALU.add).then_inc(e_compared.sem, 1)
                dve.wait_ge(e_compared.sem, e_compared.at(g, 4))
                dve.tensor_reduce(rank, above, AX.X, ALU.add).then_inc(e_ranked.sem, 1)
                dve.wait_ge(e_ranked.sem, e_ranked.at(g, 1))
                dve.scalar_tensor_tensor(out=gates[:, h], in0=rank, scalar=2.0, in1=prob, op0=ALU.is_lt, op1=ALU.mult).then_inc(e_gates.sem, 1)

            def two_groups(m, nxt):
                for h in range(2):
                    g = m * 2 + h
                    ahead = h == 0 or nxt
                    dve.wait_ge(e_gates.sem, e_gates.at(g, 1))
                    for e in range(EXP):
                        dve.wait_ge(e_y_filled.sem, e_y_filled.at(g, e + 1))
                        if e:
                            dve.wait_ge(e_y_added.sem, e_y_added.at(g, e))
                        for i in range(MT):
                            ins = dve.scalar_tensor_tensor(out=e_acc[:, h, i], in0=bank[6 + e % 2][:, i * P:(i + 1) * P], scalar=gates[:, h, i, e:e + 1], in1=e_acc[:, h, i],
                                                           op0=ALU.mult, op1=ALU.add)
                        ins.then_inc(e_y_added.sem, 1)
                        if ahead and e == STEP[h]:
                            project_att(g + 1, (h + 1) % 2)
                        if ahead and e == STEP[h] + 1:
                            e_normed(g + 1, (h + 1) % 2)
                        if h == 0 and nxt and e in QK_SUMS:
                            sum_qk(m + 1, QK_SUMS[e])
                            if e == max(QK_SUMS):
                                score_max(m + 1)
                        if ahead and e == STEP[h] + 3:
                            router_logits(g + 1)
                        if ahead and e == min(STEP[h] + 5, EXP - 1):
                            router_gates(g + 1, (h + 1) % 2)
                            if h == 0 and nxt:
                                score_sum(m + 1)
                        if h == 0 and nxt and e in PV_SUMS:
                            sum_pv(m + 1, PV_SUMS[e])
                            if e == max(PV_SUMS):
                                attention_out(m + 1)

            sum_qk(0, range(NB))
            score_max(0)
            score_sum(0)
            sum_pv(0, range(NB))
            attention_out(0)
            project_att(0, 0, True)
            e_normed(0, 0)
            router_logits(0)
            router_gates(0, 0)
            with dve.Fori(0, MT - 1) as m:
                two_groups(m, True)
            two_groups(MT - 1, False)
            meet(dve, "dve", 11)
            for m in range(MT):
                dve.wait_ge(z_silu_done.sem, m + 1)
                if m >= 2:
                    dve.wait_ge(z_stored[m % 2], 16 * (m // 2))
                so = s_out.rearrange("p (s m c) -> p m s c", s=NB, m=MT)[:, m]
                xo = x1.rearrange("p (s m c) -> p m s c", s=NB, m=MT)[:, m]
                dve.tensor_tensor(fin[:, m % 2], so, qkv[:, m, :, P:2 * P], ALU.mult).then_inc(z_product_done.sem, 1)
                dve.wait_ge(z_product_done.sem, z_product_done.at(m, 1))
                dve.tensor_tensor(fo[:, m % 2], fin[:, m % 2], xo, ALU.add).then_inc(z_final_done.sem, 1)

        @block.tensor
        def _(pe):
            pe.wait_ge(constants_made, 2 + 5)
            pe.wait_ge(rows_loaded, 16 * n_row_dmas)
            pe.transpose(bank[7][:, 0:N_ROWS], rows[:], ident[0:N_ROWS, 0:N_ROWS]).then_inc(cols_turned, 1)
            pe.wait_ge(wud_loaded, 16)
            for t in range(2):
                ins = pe.transpose(bank[6][:, t * P:(t + 1) * P], wud_raw[:, t], ident[:])
            ins.then_inc(wud_turned, 1)
            pe.wait_ge(wud_copied, 1)
            pe.sem_inc(xT_turned.sem, xT_turned.per)

            def turn_x(b, n):
                pe.wait_ge(xn_ready.sem, xn_ready.at(b, n + 1))
                pe.wait_ge(xT_copied.sem, xT_copied.at(b, n))
                for m in range(MT):
                    ins = pe.transpose(bank[0][:, m * P:(m + 1) * P], xn[:, m], ident[:])
                ins.then_inc(xT_turned.sem, 1)

            def project_u_delta(b):
                pe.wait_ge(u_done.sem, u_done.at(b, 0))
                pe.matmul(bank[1][:, :], wud[:, 0], batch(xt0, b), start=True, stop=True).then_inc(u_psum.sem, 1)
                pe.wait_ge(delta_relu.sem, delta_relu.at(b, 0))
                pe.matmul(bank[2][:, :], wud[:, 1], batch(xt0, b), start=True, stop=True).then_inc(delta_psum.sem, 1)

            turn_x(0, 0)
            with pe.Fori(0, NB - 1) as b:
                turn_x(b, 1)
                project_u_delta(b)
            pe.wait_ge(xT_copied.sem, xT_copied.at(NB, 0))
            project_u_delta(NB - 1)
            meet(pe, "pe", 1)
            meet(pe, "pe", 2)
            for c in (wbc_turned, proj_filled, qkT_filled, f_h_turned, norm_turned, f_down_filled):
                pe.sem_inc(c.sem, c.per)
            with pe.Fori(0, LAYERS) as l:
                def turn_bank_free(it, ring):
                    pe.wait_ge(turn_bank_emptied.sem, turn_bank_emptied.at(it, ring[0]))
                    ring[0] += 1

                def project(it, m):
                    t = m % MT
                    pe.wait_ge(shifted_ready.sem, shifted_ready.at(it, m // MT + 1))
                    lhs = hpad[:, WIN + t * P:WIN + (t + 1) * P]
                    pe.wait_ge(kT_copied.sem, kT_copied.at(it, m))
                    pe.matmul(bank[1][:, :], lhs, wqkv[:, 1], start=True, stop=True).then_inc(proj_filled.sem, 1)
                    pe.wait_ge(qT_copied.sem, qT_copied.at(it, m))
                    pe.matmul(bank[0][:, :], lhs, wqkv[:, 0], start=True, stop=True).then_inc(proj_filled.sem, 1)

                def turn_probs(it, ring, m, pair):
                    if pair % 2 == 0:
                        pe.wait_ge(exp_done.sem, exp_done.at(it, 2 * m + pair // 2 + 1))
                    turn_bank_free(it, ring)
                    for i in range(3):
                        ins = pe.transpose(bank[2][:, i * P:(i + 1) * P], probs[:, pair, i * P:(i + 1) * P], ident[:])
                    ins.then_inc(turn_bank_filled.sem, 1)
                    return ring[0]

                def weigh(it, copied, m, pair):
                    t = m % MT
                    pe.wait_ge(turn_bank_emptied.sem, turn_bank_emptied.at(it, copied))
                    if pair == 0 and t % 2 == 0:
                        pe.wait_ge(edge_values_copied.sem, edge_values_copied.at(it, t // 2 + 1))
                    if pair == 0:
                        pe.wait_ge(o_bank_emptied.sem, o_bank_emptied.at(it, m))
                    pt = probsT[:, pair % 2]
                    o = bank[3][:, pair * P:(pair + 1) * P]
                    pe.matmul(o, pt[:, P:2 * P], edge[:, t, pair], start=True, stop=False)
                    pe.matmul(o[:, 0:HD], pt[:, 0:P], vals[:, t, 0, pair], start=False, stop=False)
                    ins = pe.matmul(o[:, HD:P], pt[:, 2 * P:3 * P], vals[:, t + 1, 1, pair], start=False, stop=True)
                    if pair == PAIRS - 1:
                        ins.then_inc(o_bank_filled.sem, 1)

                def turn_o(it, ring, m):
                    pe.wait_ge(o_bank_emptied.sem, o_bank_emptied.at(it, m + 1 if m >= 0 else -1))
                    turn_bank_free(it, ring)
                    for r in range(MT):
                        ins = pe.transpose(bank[2][:, r * P:(r + 1) * P], o_tok[:, r * P:(r + 1) * P], ident[:])
                    ins.then_inc(turn_bank_filled.sem, 1)
                    return ring[0]

                def out_projection(r):
                    ins = pe.matmul(bank[3][:, :], wo[:, r], oT[:, r], start=(r == 0), stop=(r == MT - 1))
                    if r == MT - 1:
                        ins.then_inc(o_bank_filled.sem, 1)

                def scan_b(it, b, s):
                    pe.wait_ge(scan_bu_done.sem, scan_bu_done.at(it, s))
                    at = bass.ds((b + s // NSH) * SEQ, SEQ)
                    pe.matmul(bank[6][:, :], wbc[:, 0, s % NSH], xt0[:, at], start=True, stop=True).then_inc(scan_b_filled.sem, 1)

                it0 = pe.snap(l * NB)
                pe.wait_ge(layer_weights_loaded, 16 * NLW * (l + 1))
                project(it0, 0)
                wr = wbc_raw.rearrange("p h s k -> p (h s) k")
                for i in range(2 * NSH):
                    ins = pe.transpose(bank[2 + i // 4][:, (i % 4) * P:(i % 4 + 1) * P], wr[:, i], ident[:])
                    if i % 4 == 3:
                        ins.then_inc(wbc_turned.sem, 1)
                pe.wait_ge(layer_columns.sem, layer_columns.at(l, 2))
                for j in range(2 * FT):
                    ins = pe.matmul(bank[6][:, j:j + 1], w1[:, j // FT, (j % FT) * P:(j % FT + 1) * P], lcol[:, 2 * FT + 2:2 * FT + 3], start=True, stop=True)
                ins.then_inc(b1_product_done.sem, 1)
                meet(pe, "pe", l * 3 + 3)
                scan_b(it0, 0, 0)

                def turn(b, it, prev, nxt):
                    ring = [-TAIL if prev else 0]

                    def values(i):
                        turn_bank_free(it, ring)
                        wv = wqkv[:, 2].rearrange("p (r e d) -> p e r d", e=2, d=HD)
                        n = P if i < MT else HD
                        ins = pe.matmul(bank[2][0:n, 0:256], hpad[:, i * P:i * P + n], wv[:, 0], start=True, stop=True)
                        if i:
                            ins = pe.matmul(bank[2][:, 256:512], hpad[:, WIN + (i - 1) * P:WIN + i * P], wv[:, 1], start=True, stop=True)
                        ins.then_inc(turn_bank_filled.sem, 1)

                    def turn_qk(m):
                        for w, t, done in ((1, k_r, k_rotated), (0, q_r, q_rotated)):
                            pe.wait_ge(done.sem, done.at(it, m + 1))
                            for r in range(PAIRS):
                                ins = pe.transpose(bank[w][:, r * P:(r + 1) * P], t[:, r * P:(r + 1) * P], ident[:])
                            ins.then_inc(qkT_filled.sem, 1)

                    def scores(m, step):
                        pe.wait_ge(kT_copied.sem, kT_copied.at(it, m + 1))
                        pe.wait_ge(qT_copied.sem, qT_copied.at(it, m + 1))
                        pe.wait_ge(exp_done.sem, exp_done.at(it, 2 * m + step))
                        mask = maskb[:, 1 if m == 0 else 0].unsqueeze(1).to_broadcast([P, 2, KEYS])
                        for eo in range(2):
                            pe.matmul(bank[4 + eo][:, 0:2 * KEYS], identb[:], mask, start=True, stop=False)
                        for j in range(2):
                            for eo in range(2):
                                ps = slice(eo * HD, (eo + 1) * HD)
                                ins = pe.matmul(bank[4 + eo][:, j * KEYS:(j + 1) * KEYS], qT[ps, 2 * step + j], kT[ps, 2 * step + j, m * P:m * P + KEYS],
                                                start=False, stop=(j == 1))
                        ins.then_inc(sim_filled.sem, 1)

                    def scan_c(s):
                        pe.wait_ge(scan_ch_done.sem, scan_ch_done.at(it, s))
                        pe.matmul(bank[7][:, :], wbc[:, 1, s], batch(xt0, b), start=True, stop=True).then_inc(scan_c_filled.sem, 1)

                    copied = ring[0]
                    for m in range(MT):
                        behind = m or prev
                        turn_qk(m)
                        if behind:
                            weigh(it, copied, m - 1, 1)
                            copied = turn_probs(it, ring, m - 1, 2)
                        if m + 1 < MT or nxt:
                            project(it, m + 1)
                        scores(m, 0)
                        if behind:
                            weigh(it, copied, m - 1, 2)
                            copied = turn_probs(it, ring, m - 1, 3)
                        scan_c(2 * m)
                        if behind:
                            weigh(it, copied, m - 1, 3)
                        if m == 0:
                            values(0)
                        scan_b(it, b, 2 * m + 1)
                        if behind:
                            o_turned = turn_o(it, ring, m - 1)
                        scan_c(2 * m + 1)
                        scores(m, 1)
                        if m == 0:
                            for i in range(1, MT + 1):
                                values(i)
                                if prev:
                                    if i == 1:
                                        pe.wait_ge(turn_bank_emptied.sem, turn_bank_emptied.at(it, o_turned))
                                    out_projection(i - 1)
                        copied = turn_probs(it, ring, m, 0)
                        if m + 1 < MT or nxt:
                            scan_b(it, b, 2 * m + 2)
                        weigh(it, copied, m, 0)
                        copied = turn_probs(it, ring, m, 1)

                turn(0, it0, False, True)
                with pe.Fori(1, NB - 1) as b:
                    turn(b, pe.snap(l * NB + b), True, True)
                it_last = pe.snap(l * NB + NB - 1)
                turn(NB - 1, it_last, True, False)
                it_end = pe.snap(l * NB + NB)
                ring = [-TAIL]
                copied = -TAIL
                for pair in range(1, PAIRS):
                    weigh(it_end, copied, -1, pair)
                    if pair + 1 < PAIRS:
                        copied = turn_probs(it_end, ring, -1, pair + 1)
                o_turned = turn_o(it_end, ring, -1)
                pe.wait_ge(turn_bank_emptied.sem, turn_bank_emptied.at(it_end, o_turned))
                for r in range(MT):
                    out_projection(r)
                meet(pe, "pe", l * 3 + 4)
                pe.wait_ge(f_h_padded.sem, f_h_padded.at(l, 1))

                def turn_h(it, n):
                    pe.wait_ge(f_shifted_ready.sem, f_shifted_ready.at(it, n + 1))
                    pe.wait_ge(f_normed.sem, f_normed.at(it, n))
                    for m in range(MT):
                        ins = pe.transpose(bank[0][:, m * P:(m + 1) * P], f_h[:, m * P:(m + 1) * P], ident[:])
                    ins.then_inc(f_h_turned.sem, 1)

                def turn_normed(it, n):
                    pe.wait_ge(f_normed.sem, f_normed.at(it, n + 1))
                    pe.wait_ge(norm_turned_copied.sem, norm_turned_copied.at(it, n))
                    for m in range(MT):
                        ins = pe.transpose(bank[1][:, m * P:(m + 1) * P], f_hn[:, m], ident[:])
                    ins.then_inc(norm_turned.sem, 1)

                def ffn(b, it, nxt):
                    pe.wait_ge(norm_turned_copied.sem, norm_turned_copied.at(it, 1))
                    for j in range(FT):
                        pe.wait_ge(f_act_done.sem, f_act_done.at(it, j - 1))
                        pe.matmul(bank[2 + 2 * (j % 2)][:, :], w1s[:, 0, j * P:(j + 1) * P], f_hnT, start=True, stop=True)
                        pe.matmul(bank[3 + 2 * (j % 2)][:, :], w1s[:, 1, j * P:(j + 1) * P], f_hnT, start=True, stop=True).then_inc(up_filled.sem, 1)
                        if j == 0 and nxt:
                            turn_h(it, 1)
                    for j in range(FT):
                        pe.wait_ge(f_act_done.sem, f_act_done.at(it, j + 1))
                        if j == 0:
                            pe.wait_ge(f_added.sem, f_added.at(it, 0))
                        if j == FT - 1 and nxt:
                            turn_normed(it, 1)
                        ins = pe.matmul(bank[6][:, :], w2[:, j], f_act[:, j], start=(j == 0), stop=(j == FT - 1))
                    ins.then_inc(f_down_filled.sem, 1)

                it_first = pe.snap(l * NB)
                turn_h(it_first, 0)
                turn_normed(it_first, 0)
                with pe.Fori(0, NB - 1) as b:
                    ffn(b, pe.snap(l * NB + b), True)
                it_last = pe.snap(l * NB + NB - 1)
                ffn(NB - 1, it_last, False)
                meet(pe, "pe", l * 3 + 5)
            pe.wait_ge(second_weights_loaded, 16 * len(second_list))
            for t in range(3):
                pe.transpose(bank[0][:, t * P:(t + 1) * P], inp_raw[:, t], ident[:])
            pe.transpose(bank[1][:, 0:P], outp_raw, ident[:])
            pe.transpose(bank[2][:, 0:EXP], rout_raw[0:EXP], ident[0:EXP, 0:EXP]).then_inc(projections_turned, 1)
            for k in range(3):
                for j in range(KT):
                    n = k * KT + j
                    pe.matmul(bank[5][:, n:n + 1], w_up[:, k, j * P:(j + 1) * P], cols[:, R_B:R_B + 1], start=True, stop=True)
            for e in range(EXP):
                for f in range(2):
                    n = 3 * KT + 2 * e + f
                    pe.matmul(bank[5][:, n:n + 1], m_up[:, e, f * P:(f + 1) * P], cols[:, R_N2B:R_N2B + 1], start=True, stop=True)
            pe.wait_ge(norm_bias_widened, 1)
            pe.wait_ge(projections_copied, 1)
            pe.matmul(bank[6][:, 0:3 * P], n1b_wide, inpT, start=True, stop=True)
            pe.matmul(bank[7][:, 0:EXP], n2b_wide, routT, start=True, stop=True).then_inc(bias_products_done, 1)
            meet(pe, "pe", 9)
            for c in (sg_turned, z_turned, fm_filled, t_filled, e_att_turned, e_y_filled):
                pe.sem_inc(c.sem, c.per)
            with pe.Fori(0, NB) as b:
                pe.wait_ge(sg_ready.sem, sg_ready.at(b, 1))
                pe.wait_ge(x1_done.sem, x1_done.at(b - 1, 1))
                for m in range(MT):
                    ins = pe.transpose(bank[0][:, m * P:(m + 1) * P], sg[:, m * P:(m + 1) * P], ident[:])
                ins.then_inc(sg_turned.sem, 1)

            def up(b, n, k, j, src):
                pe.wait_ge(mlp_gelu_done.sem, mlp_gelu_done.at(b, n - 1))
                pe.matmul(bank[4 + n % 2][:, :], w_up[:, k, j * P:(j + 1) * P], src, start=True, stop=True).then_inc(mlp_up_filled.sem, 1)

            def turn_z(b, n):
                pe.wait_ge(z_done.sem, z_done.at(b, n + 1))
                for m in range(MT):
                    ins = pe.transpose(bank[0][:, m * P:(m + 1) * P], z_tok[:, m], ident[:])
                ins.then_inc(z_turned.sem, 1)

            def project_z(b, n, first):
                pe.wait_ge(zT_copied.sem, zT_copied.at(b, n + 1))
                for m in range(MT):
                    pe.wait_ge(two_bank_emptied.sem, two_bank_emptied.at(b, first + m - 1))
                    pe.matmul(bank[2 + m % 2][:, 0:3 * P], zT[:, m * P:(m + 1) * P], inpT, start=True, stop=True).then_inc(two_bank_filled.sem, 1)

            def turn_z2(b):
                pe.wait_ge(z2_done.sem, z2_done.at(b, 0))
                pe.wait_ge(s_out_done.sem, s_out_done.at(b, -1))
                for m in range(MT):
                    ins = pe.transpose(bank[1][:, m * P:(m + 1) * P], z2[:, m], ident[:])
                ins.then_inc(z2_turned.sem, 1)

            def last_up(b, n):
                pe.wait_ge(z2T_copied.sem, z2T_copied.at(b, 0))
                for j in range(KT):
                    up(b, n + j, 2, j, z2T)

            def last_down(b, n):
                pe.wait_ge(mlp_gelu_done.sem, mlp_gelu_done.at(b, n + KT))
                for m in range(MT):
                    for j in range(KT):
                        ins = pe.matmul(bank[1][:, m * P:(m + 1) * P], hid[:, 0, j, m * P:(m + 1) * P], w_dn[:, 2, j], start=(j == 0), stop=(j == KT - 1))
                ins.then_inc(fm_filled.sem, 1)

            def l1_turn(b, prev, nxt):
                first = -KT if prev else 0
                for k in range(2):
                    for j in range(KT):
                        up(b, first + k * KT + j, k, j, zT)
                    if k == 1 and nxt:
                        turn_z(b, 1)
                    pe.wait_ge(w_copied.sem, w_copied.at(b, k))
                    for j in range(KT):
                        pe.wait_ge(mlp_gelu_done.sem, mlp_gelu_done.at(b, first + k * KT + j + 1))
                        ins = pe.matmul(bank[6][:, :], w_dn[:, k, j], hid[:, k, j], start=(j == 0), stop=(j == KT - 1))
                    ins.then_inc(w_filled.sem, 1)
                if prev:
                    turn_z2(b)
                if nxt:
                    project_z(b, 1, MT)
                if prev:
                    last_up(b, first + 2 * KT)
                pe.wait_ge(w_copied.sem, w_copied.at(b, 2))
                for j in range(MT):
                    n = (2 if nxt else 1) * MT + j
                    pe.wait_ge(two_bank_emptied.sem, two_bank_emptied.at(b, n - 1))
                    pe.matmul(bank[2 + n % 2][:, 0:(MT - j) * P], wT[:, 1, j * P:(j + 1) * P], wT[:, 0, j * P:], start=True, stop=True).then_inc(two_bank_filled.sem, 1)
                    if j == 1 and prev:
                        last_down(b, first + 2 * KT)
                pe.wait_ge(n_done.sem, n_done.at(b, 1))
                pe.wait_ge(t_gelu_done.sem, t_gelu_done.at(b, 0))
                for i in range(MT):
                    pe.wait_ge(two_bank_emptied.sem, two_bank_emptied.at(b, (2 if nxt else 1) * MT + i + 1))
                    for j in range(i + 1):
                        ins = pe.matmul(bank[7][:, i * P:(i + 1) * P], w3[:, j, (i - j) * P:(i - j + 1) * P], n_tok[:, j], start=(j == 0), stop=(j == i))
                ins.then_inc(t_filled.sem, 1)

            turn_z(0, 0)
            project_z(0, 0, 0)
            l1_turn(0, False, True)
            with pe.Fori(1, NB - 1) as b:
                l1_turn(b, True, True)
            l1_turn(NB - 1, True, False)
            turn_z2(NB)
            last_up(NB, -KT)
            last_down(NB, -KT)
            meet(pe, "pe", 10)

            def turn_att(g):
                pe.wait_ge(e_att_staged.sem, e_att_staged.at(g, 1))
                pe.wait_ge(e_zT_copied.sem, e_zT_copied.at(g - 1, 1))
                for i in range(MT):
                    ins = pe.transpose(bank[0][:, i * P:(i + 1) * P], e_att[:, i], ident[:])
                ins.then_inc(e_att_turned.sem, 1)

            def project_att(g):
                pe.wait_ge(e_attT_copied.sem, e_attT_copied.at(g, 1))
                for i in range(MT):
                    ins = pe.matmul(bank[0][:, i * P:(i + 1) * P], e_attT[:, i * P:(i + 1) * P], outpT, start=True, stop=True)
                ins.then_inc(e_proj_filled.sem, 1)

            def turn_e_z(g):
                pe.wait_ge(e_z_done.sem, e_z_done.at(g, 1))
                for i in range(MT):
                    ins = pe.transpose(bank[0][:, i * P:(i + 1) * P], e_z[:, i], ident[:])
                ins.then_inc(e_z_turned.sem, 1)

            def route(g, h):
                pe.wait_ge(e_zT_copied.sem, e_zT_copied.at(g, 1))
                for i in range(MT):
                    ins = pe.matmul(bank[1][:, i * EXP:(i + 1) * EXP], e_zT[:, h, i * P:(i + 1) * P], routT, start=True, stop=True)
                ins.then_inc(e_router_filled.sem, 1)

            def two_groups(m, nxt):
                for h in range(2):
                    g = m * 2 + h
                    ahead = h == 0 or nxt
                    for e in range(EXP + 2):
                        if e < EXP:
                            for f in range(2):
                                n = 2 * e + f
                                pe.wait_ge(e_gelu_done.sem, e_gelu_done.at(g, n - 3))
                                pe.matmul(bank[2 + n % 4][:, :], m_up[:, e, f * P:(f + 1) * P], e_zT[:, h], start=True, stop=True).then_inc(e_up_filled.sem, 1)
                        if e >= 2:
                            x = e - 2
                            pe.wait_ge(e_gelu_done.sem, e_gelu_done.at(g, 2 * x + 2))
                            pe.wait_ge(e_y_added.sem, e_y_added.at(g, x - 1))
                            for i in range(MT):
                                for f in range(2):
                                    ins = pe.matmul(bank[6 + x % 2][:, i * P:(i + 1) * P], e_hid[:, x % 2, f, i * P:(i + 1) * P], m_dn[:, x, f],
                                                    start=(f == 0), stop=(f == 1))
                            ins.then_inc(e_y_filled.sem, 1)
                        if ahead and e == STEP[h] + 1:
                            turn_att(g + 1)
                        if ahead and e == STEP[h] + 2:
                            project_att(g + 1)
                        if ahead and e == STEP[h] + 4:
                            turn_e_z(g + 1)
                        if ahead and e == STEP[h] + 5:
                            route(g + 1, (h + 1) % 2)

            turn_att(0)
            project_att(0)
            turn_e_z(0)
            route(0, 0)
            with pe.Fori(0, MT - 1) as m:
                two_groups(m, True)
            two_groups(MT - 1, False)
            meet(pe, "pe", 11)


def rotary_tables():
    import numpy as np
    half = np.arange(0, HD, 2, dtype=np.float64)
    freqs = np.arange(SEQ)[:, None] * (1.0 / 10000.0 ** (half / HD))[None]
    base = (half + 0.4 * HD) / (1.4 * HD)
    scale = base[None] ** ((np.arange(SEQ) - SEQ // 2) / float(WIN // 2))[:, None]
    two = lambda a, b: np.concatenate([a, b], axis=-1)
    cos, sin, scale = two(np.cos(freqs), np.cos(freqs)), two(-np.sin(freqs), np.sin(freqs)), two(scale, scale)
    return np.stack([8.0 * cos * scale, 8.0 * sin * scale, cos / scale, sin / scale]).astype(np.float32)


_INS = ["L0_attn_x", "L0_attn_W", "L0_attn_b", "L0_attn_A", "L0_attn_D", "L0_ffn_wqkv", "L0_ffn_q_scale", "L0_ffn_k_scale",
        "L0_ffn_wo", "L0_ffn_ln_g", "L0_ffn_ln_b", "L0_ffn_w1", "L0_ffn_b1", "L0_ffn_w2", "L0_ffn_b2", "L1_attn_ln_g", "L1_attn_ln_b",
        "L1_attn_h1_w1", "L1_attn_h1_b1", "L1_attn_h1_w2", "L1_attn_h1_b2", "L1_attn_h2_w1", "L1_attn_h2_b1", "L1_attn_h2_w2",
        "L1_attn_h2_b2", "L1_attn_fm_w1", "L1_attn_fm_b1", "L1_attn_fm_w2", "L1_attn_fm_b2", "L1_ffn_ln1_w", "L1_ffn_ln1_b",
        "L1_ffn_in_proj_w", "L1_ffn_in_proj_b", "L1_ffn_out_proj_w", "L1_ffn_out_proj_b", "L1_ffn_ln2_w", "L1_ffn_ln2_b",
        "L1_ffn_router_w", "L1_ffn_w1", "L1_ffn_w2"]


def kernel(**inputs):
    import numpy as np
    import concourse.bacc as bacc
    from concourse.bass_utils import run_bass_kernel_spmd as run

    nc = bacc.Bacc("TRN2", target_bir_lowering=False, num_devices=1)
    arrays, aps = {}, {}
    given = {name: np.ascontiguousarray(inputs[name]) for name in _INS} | {"rotary": rotary_tables()}
    for name, a in given.items():
        arrays[f"in_{name}"] = a
        aps[name] = nc.dram_tensor(f"in_{name}", a.shape, mybir.dt.from_np(a.dtype), kind="ExternalInput").ap()
    out = nc.dram_tensor("out_0", (NB, SEQ, P), F32, kind="ExternalOutput").ap()
    build(nc, aps, out)
    return run(nc, [arrays], core_ids=[0]).results[0]["out_0"]
```
